# Optimizing a Trainium2 kernel written in Bass

```python
import numpy as np
import jax
import jax.numpy as jnp

def _softmax(x, axis=-1):
    return jax.nn.softmax(x, axis=axis)

def _gelu(x):
    return jax.nn.gelu(x, approximate=True)

def _silu(x):
    return jax.nn.silu(x)

def _sigmoid(x):
    return jax.nn.sigmoid(x)

def _layernorm(x, axis=-1, eps=1e-05):
    m = jnp.mean(x, axis=axis, keepdims=True)
    v = jnp.var(x, axis=axis, keepdims=True)
    return (x - m) / jnp.sqrt(v + eps)

def _scatter_add(tgt, idx, src, axis=0):
    return tgt.at[idx].add(src)

def _segment_sum(src, seg, n):
    return jax.ops.segment_sum(src, seg, n)
kernel_name = 'mk_xattn_ffn_d2_seqx_r4_88db03'

def setup_inputs(seed: int=0):
    np.random.seed(seed)
    _w = jnp.asarray

    def _rec_inputs():
        import jax
        import jax.numpy as jnp
        _rk = jax.random.key(seed)
        x = -0.0005207 + 1.001 * jax.random.normal(jax.random.fold_in(_rk, 1), (8, 512, 256), jnp.float32)
        _lenS = 512 - jax.random.randint(jax.random.fold_in(_rk, 7), (8,), 0, max(1, 512 // 4) + 1, jnp.int32)
        _lenS2 = 512 - jax.random.randint(jax.random.fold_in(_rk, 8), (8,), 0, max(1, 512 // 4) + 1, jnp.int32)
        _ctx_1024P = jax.random.normal(jax.random.fold_in(_rk, 11), (8, 16, 256), jnp.float32)
        _ctx_1024c = jax.random.dirichlet(jax.random.fold_in(_rk, 511), 0.3 * jnp.ones((16,), jnp.float32), (8, 512))
        _ctx_1024t = jnp.einsum('bsk,bkd->bsd', _ctx_1024c, _ctx_1024P)
        _ctx_1024t = _ctx_1024t * jax.lax.rsqrt(jnp.mean(jnp.square(_ctx_1024t)) + 1e-12) * 0.953939
        ctx_1024 = 2.81802e-05 + 1.00001 * (_ctx_1024t + 0.3 * jax.random.normal(jax.random.fold_in(_rk, 611), (8, 512, 256), jnp.float32))
        _validS = jnp.arange(512)[None, :] < _lenS[:, None]
        _validS2 = jnp.arange(512)[None, :] < _lenS2[:, None]
        _causal = jnp.tril(jnp.ones((512, 512), dtype=bool))
        mask_BxS2_bf1 = jnp.ones((8, 512), dtype=bool)
        return (x, ctx_1024, mask_BxS2_bf1)
    x, ctx_1024, mask_BxS2_bf1 = _rec_inputs()

    def _L0_xattn_setup():
        import jax, jax.numpy as jnp
        import numpy as np
        E = 256
        H = 16
        D = E // H
        key = jax.random.key(seed)
        ks = jax.random.split(key, 12)
        B, Tq, Tk = (2, 256, 2048)
        s = 0.02
        return {'hidden_states': jax.random.normal(ks[0], (B, Tq, E), jnp.float32), 'key_value_states': jax.random.normal(ks[1], (B, Tk, E), jnp.float32), 'Wq': jax.random.normal(ks[2], (E, E), jnp.float32) * s, 'bq': jnp.zeros((E,), jnp.float32), 'Wk': jax.random.normal(ks[3], (E, E), jnp.float32) * s, 'bk': jnp.zeros((E,), jnp.float32), 'Wv': jax.random.normal(ks[4], (E, E), jnp.float32) * s, 'bv': jnp.zeros((E,), jnp.float32), 'Wo': jax.random.normal(ks[5], (E, E), jnp.float32) * s, 'bo': jnp.zeros((E,), jnp.float32), 'stride': 16}
    _L0_xattn_all = _L0_xattn_setup()
    _L0_xattn_in = {k: v for k, v in _L0_xattn_all.items() if k in ('Wq', 'bq', 'Wk', 'bk', 'Wv', 'bv', 'Wo', 'bo')}
    del _L0_xattn_all

    def _L0_ffn_setup():
        import jax, jax.numpy as jnp
        import numpy as np
        HIDDEN = 256
        INTER = 128
        N_EXPERTS = 16
        N_GROUP = 4
        TOPK_GROUP = 2
        TOP_K = 4
        SCALING = 2.5

        def _gate(x_flat, gate_w, e_bias):
            logits = x_flat @ gate_w.T
            scores = jax.nn.sigmoid(logits)
            scores_for_choice = scores + e_bias[None, :]
            T = x_flat.shape[0]
            per_group = N_EXPERTS // N_GROUP
            grouped = scores_for_choice.reshape(T, N_GROUP, per_group)
            top2, _ = jax.lax.top_k(grouped, 2)
            group_scores = top2.sum(-1)
            _, group_idx = jax.lax.top_k(group_scores, TOPK_GROUP)
            group_mask = jax.nn.one_hot(group_idx, N_GROUP, dtype=jnp.float32).sum(1) > 0
            score_mask = jnp.repeat(group_mask, per_group, axis=-1)
            tmp_scores = jnp.where(score_mask, scores_for_choice, 0.0)
            _, topk_idx = jax.lax.top_k(tmp_scores, TOP_K)
            topk_weight = jnp.take_along_axis(scores, topk_idx, axis=1)
            topk_weight = topk_weight / (topk_weight.sum(-1, keepdims=True) + 1e-20)
            topk_weight = topk_weight * SCALING
            return (topk_idx, topk_weight)
        key = jax.random.key(seed)
        ks = jax.random.split(key, 8)
        B, S = (2, 512)
        hidden_states = jax.random.normal(ks[0], (B, S, HIDDEN), dtype=jnp.float32)
        gate_w = jax.random.normal(ks[1], (N_EXPERTS, HIDDEN), dtype=jnp.float32) * 0.02
        e_bias = jnp.zeros((N_EXPERTS,), dtype=jnp.float32)
        gate_proj = jax.random.normal(ks[2], (N_EXPERTS, INTER, HIDDEN), dtype=jnp.float32) * 0.02
        up_proj = jax.random.normal(ks[3], (N_EXPERTS, INTER, HIDDEN), dtype=jnp.float32) * 0.02
        down_proj = jax.random.normal(ks[4], (N_EXPERTS, HIDDEN, INTER), dtype=jnp.float32) * 0.02
        shared_gate_w = jax.random.normal(ks[5], (INTER, HIDDEN), dtype=jnp.float32) * 0.02
        shared_up_w = jax.random.normal(ks[6], (INTER, HIDDEN), dtype=jnp.float32) * 0.02
        shared_down_w = jax.random.normal(ks[7], (HIDDEN, INTER), dtype=jnp.float32) * 0.02
        return {'hidden_states': hidden_states, 'gate_w': gate_w, 'e_bias': e_bias, 'gate_proj': gate_proj, 'up_proj': up_proj, 'down_proj': down_proj, 'shared_gate_w': shared_gate_w, 'shared_up_w': shared_up_w, 'shared_down_w': shared_down_w}
    _L0_ffn_all = _L0_ffn_setup()
    _L0_ffn_in = {k: v for k, v in _L0_ffn_all.items() if k in ('gate_w', 'e_bias', 'gate_proj', 'up_proj', 'down_proj', 'shared_gate_w', 'shared_up_w', 'shared_down_w')}
    del _L0_ffn_all

    def _L1_xattn_setup():
        import jax, jax.numpy as jnp
        import numpy as np
        DIM = 256
        HEADS = 16
        DIM_HEAD = 64
        INNER = HEADS * DIM_HEAD
        B, F, Q = (16, 1024, 64)
        EPS = 1e-05
        SCALE = DIM_HEAD ** (-0.5)

        def _layernorm(x, gamma, beta):
            mu = jnp.mean(x, axis=-1, keepdims=True)
            var = jnp.var(x, axis=-1, keepdims=True)
            return (x - mu) * jax.lax.rsqrt(var + EPS) * gamma + beta
        key = jax.random.key(seed)
        ks = jax.random.split(key, 8)
        features = jax.random.normal(ks[0], (B, F, DIM), dtype=jnp.float32)
        masks = jnp.ones((B, F), dtype=bool)
        latents = jax.random.normal(ks[1], (B, Q, DIM), dtype=jnp.float32)
        Wq = jax.random.normal(ks[2], (DIM, INNER), dtype=jnp.float32) / np.sqrt(DIM)
        Wk = jax.random.normal(ks[3], (DIM, INNER), dtype=jnp.float32) / np.sqrt(DIM)
        Wv = jax.random.normal(ks[4], (DIM, INNER), dtype=jnp.float32) / np.sqrt(DIM)
        Wo = jax.random.normal(ks[5], (INNER, DIM), dtype=jnp.float32) / np.sqrt(INNER)
        gm = jnp.ones((DIM,), jnp.float32)
        bm = jnp.zeros((DIM,), jnp.float32)
        gl = jnp.ones((DIM,), jnp.float32)
        bl = jnp.zeros((DIM,), jnp.float32)
        return {'features': features, 'masks': masks, 'latents': latents, 'gm': gm, 'bm': bm, 'gl': gl, 'bl': bl, 'Wq': Wq, 'Wk': Wk, 'Wv': Wv, 'Wo': Wo}
    _L1_xattn_all = _L1_xattn_setup()
    _L1_xattn_in = {k: v for k, v in _L1_xattn_all.items() if k in ('gm', 'bm', 'gl', 'bl', 'Wq', 'Wk', 'Wv', 'Wo')}
    del _L1_xattn_all

    def _L1_ffn_setup():
        import jax, jax.numpy as jnp
        import numpy as np
        B, S, D = (1, 512, 256)
        E, K, F = (8, 2, 352)
        NS = 2
        SCALE = 2.5

        def _swiglu_mlp(x, wg, wu, wd):
            return jax.nn.silu(x @ wg) * (x @ wu) @ wd
        key = jax.random.key(seed)
        ks = jax.random.split(key, 8)
        s = 0.02
        return {'hidden_states': jax.random.normal(ks[0], (B, S, D), jnp.float32), 'gate_w': jax.random.normal(ks[1], (E, D), jnp.float32) * s, 'w_gate': jax.random.normal(ks[2], (E, D, F), jnp.float32) * s, 'w_up': jax.random.normal(ks[3], (E, D, F), jnp.float32) * s, 'w_down': jax.random.normal(ks[4], (E, F, D), jnp.float32) * s, 'sw_gate': jax.random.normal(ks[5], (D, F * NS), jnp.float32) * s, 'sw_up': jax.random.normal(ks[6], (D, F * NS), jnp.float32) * s, 'sw_down': jax.random.normal(ks[7], (F * NS, D), jnp.float32) * s}
    _L1_ffn_all = _L1_ffn_setup()
    _L1_ffn_in = {k: v for k, v in _L1_ffn_all.items() if k in ('gate_w', 'w_gate', 'w_up', 'w_down', 'sw_gate', 'sw_up', 'sw_down')}
    del _L1_ffn_all
    return {'x': x, 'ctx_1024': ctx_1024, 'mask_BxS2_bf1': mask_BxS2_bf1, 'L0_xattn_Wq': _L0_xattn_in['Wq'], 'L0_xattn_bq': _L0_xattn_in['bq'], 'L0_xattn_Wk': _L0_xattn_in['Wk'], 'L0_xattn_bk': _L0_xattn_in['bk'], 'L0_xattn_Wv': _L0_xattn_in['Wv'], 'L0_xattn_bv': _L0_xattn_in['bv'], 'L0_xattn_Wo': _L0_xattn_in['Wo'], 'L0_xattn_bo': _L0_xattn_in['bo'], 'L0_ffn_gate_w': _L0_ffn_in['gate_w'], 'L0_ffn_e_bias': _L0_ffn_in['e_bias'], 'L0_ffn_gate_proj': _L0_ffn_in['gate_proj'], 'L0_ffn_up_proj': _L0_ffn_in['up_proj'], 'L0_ffn_down_proj': _L0_ffn_in['down_proj'], 'L0_ffn_shared_gate_w': _L0_ffn_in['shared_gate_w'], 'L0_ffn_shared_up_w': _L0_ffn_in['shared_up_w'], 'L0_ffn_shared_down_w': _L0_ffn_in['shared_down_w'], 'L1_xattn_gm': _L1_xattn_in['gm'], 'L1_xattn_bm': _L1_xattn_in['bm'], 'L1_xattn_gl': _L1_xattn_in['gl'], 'L1_xattn_bl': _L1_xattn_in['bl'], 'L1_xattn_Wq': _L1_xattn_in['Wq'], 'L1_xattn_Wk': _L1_xattn_in['Wk'], 'L1_xattn_Wv': _L1_xattn_in['Wv'], 'L1_xattn_Wo': _L1_xattn_in['Wo'], 'L1_ffn_gate_w': _L1_ffn_in['gate_w'], 'L1_ffn_w_gate': _L1_ffn_in['w_gate'], 'L1_ffn_w_up': _L1_ffn_in['w_up'], 'L1_ffn_w_down': _L1_ffn_in['w_down'], 'L1_ffn_sw_gate': _L1_ffn_in['sw_gate'], 'L1_ffn_sw_up': _L1_ffn_in['sw_up'], 'L1_ffn_sw_down': _L1_ffn_in['sw_down']}

def reference(x, ctx_1024, mask_BxS2_bf1, L0_xattn_Wq, L0_xattn_bq, L0_xattn_Wk, L0_xattn_bk, L0_xattn_Wv, L0_xattn_bv, L0_xattn_Wo, L0_xattn_bo, L0_ffn_gate_w, L0_ffn_e_bias, L0_ffn_gate_proj, L0_ffn_up_proj, L0_ffn_down_proj, L0_ffn_shared_gate_w, L0_ffn_shared_up_w, L0_ffn_shared_down_w, L1_xattn_gm, L1_xattn_bm, L1_xattn_gl, L1_xattn_bl, L1_xattn_Wq, L1_xattn_Wk, L1_xattn_Wv, L1_xattn_Wo, L1_ffn_gate_w, L1_ffn_w_gate, L1_ffn_w_up, L1_ffn_w_down, L1_ffn_sw_gate, L1_ffn_sw_up, L1_ffn_sw_down):
    import jax
    import jax.numpy as jnp

    def _L0_xattn_ref(hidden_states, key_value_states, Wq, bq, Wk, bk, Wv, bv, Wo, bo, stride):
        import jax, jax.numpy as jnp
        import numpy as np
        E = 256
        H = 16
        D = E // H
        B, Tq, _ = hidden_states.shape
        Tk = key_value_states.shape[1]
        scaling = D ** (-0.5)
        Q = (hidden_states @ Wq.T + bq).reshape(B, Tq, H, D).transpose(0, 2, 1, 3)
        K = (key_value_states @ Wk.T + bk).reshape(B, Tk, H, D).transpose(0, 2, 1, 3)
        V = (key_value_states @ Wv.T + bv).reshape(B, Tk, H, D).transpose(0, 2, 1, 3)
        m = Tk // stride
        idx = jnp.arange(H)[:, None] + stride * jnp.arange(m)[None, :]
        gather = idx[None, :, :, None]
        Kg = jnp.take_along_axis(K, gather, axis=2)
        Vg = jnp.take_along_axis(V, gather, axis=2)
        scores = jnp.einsum('bhqd,bhkd->bhqk', Q, Kg) * scaling
        attn = jax.nn.softmax(scores, axis=-1)
        out = jnp.einsum('bhqk,bhkd->bhqd', attn, Vg)
        out = out.transpose(0, 2, 1, 3).reshape(B, Tq, E)
        return out @ Wo.T + bo

    def _L0_ffn_ref(hidden_states, gate_w, e_bias, gate_proj, up_proj, down_proj, shared_gate_w, shared_up_w, shared_down_w):
        import jax, jax.numpy as jnp
        import numpy as np
        HIDDEN = 256
        INTER = 128
        N_EXPERTS = 16
        N_GROUP = 4
        TOPK_GROUP = 2
        TOP_K = 4
        SCALING = 2.5

        def _gate(x_flat, gate_w, e_bias):
            logits = x_flat @ gate_w.T
            scores = jax.nn.sigmoid(logits)
            scores_for_choice = scores + e_bias[None, :]
            T = x_flat.shape[0]
            per_group = N_EXPERTS // N_GROUP
            grouped = scores_for_choice.reshape(T, N_GROUP, per_group)
            top2, _ = jax.lax.top_k(grouped, 2)
            group_scores = top2.sum(-1)
            _, group_idx = jax.lax.top_k(group_scores, TOPK_GROUP)
            group_mask = jax.nn.one_hot(group_idx, N_GROUP, dtype=jnp.float32).sum(1) > 0
            score_mask = jnp.repeat(group_mask, per_group, axis=-1)
            tmp_scores = jnp.where(score_mask, scores_for_choice, 0.0)
            _, topk_idx = jax.lax.top_k(tmp_scores, TOP_K)
            topk_weight = jnp.take_along_axis(scores, topk_idx, axis=1)
            topk_weight = topk_weight / (topk_weight.sum(-1, keepdims=True) + 1e-20)
            topk_weight = topk_weight * SCALING
            return (topk_idx, topk_weight)
        B, S, H = hidden_states.shape
        x = hidden_states.reshape(-1, H)
        T = x.shape[0]
        topk_idx, topk_weight = _gate(x, gate_w, e_bias)
        g = jnp.einsum('th,eih->eti', x, gate_proj)
        u = jnp.einsum('th,eih->eti', x, up_proj)
        inter = jax.nn.silu(g) * u
        expert_out = jnp.einsum('eti,ehi->eth', inter, down_proj)
        sel = expert_out[topk_idx, jnp.arange(T)[:, None]]
        y = jnp.einsum('tkh,tk->th', sel, topk_weight)
        y = y.reshape(B, S, H)
        sg = hidden_states @ shared_gate_w.T
        su = hidden_states @ shared_up_w.T
        shared_out = jax.nn.silu(sg) * su @ shared_down_w.T
        return y + shared_out

    def _L1_xattn_ref(features, masks, latents, gm, bm, gl, bl, Wq, Wk, Wv, Wo):
        import jax, jax.numpy as jnp
        import numpy as np
        DIM = 256
        HEADS = 16
        DIM_HEAD = 64
        INNER = HEADS * DIM_HEAD
        B, F, Q = (16, 1024, 64)
        EPS = 1e-05
        SCALE = DIM_HEAD ** (-0.5)

        def _layernorm(x, gamma, beta):
            mu = jnp.mean(x, axis=-1, keepdims=True)
            var = jnp.var(x, axis=-1, keepdims=True)
            return (x - mu) * jax.lax.rsqrt(var + EPS) * gamma + beta
        b, f, d = features.shape
        q_len = latents.shape[1]
        x = _layernorm(features, gm, bm)
        lat = _layernorm(latents, gl, bl)
        q = (lat @ Wq).reshape(b, q_len, HEADS, DIM_HEAD).transpose(0, 2, 1, 3)
        kv_input = jnp.concatenate([x, lat], axis=1)
        kv_mask = jnp.concatenate([masks, jnp.ones((b, q_len), dtype=bool)], axis=1)
        kv_mask = kv_mask[:, None, None, :]
        k = (kv_input @ Wk).reshape(b, f + q_len, HEADS, DIM_HEAD).transpose(0, 2, 1, 3)
        v = (kv_input @ Wv).reshape(b, f + q_len, HEADS, DIM_HEAD).transpose(0, 2, 1, 3)
        q = q * SCALE
        sim = jnp.einsum('bhqd,bhfd->bhqf', q, k)
        sim = sim - jax.lax.stop_gradient(jnp.max(sim, axis=-1, keepdims=True))
        sim = jnp.where(kv_mask, sim, -jnp.inf)
        alphas = jax.nn.softmax(sim, axis=-1)
        out = jnp.einsum('bhqf,bhfd->bhqd', alphas, v)
        out = out.transpose(0, 2, 1, 3).reshape(b, q_len, INNER)
        return out @ Wo

    def _L1_ffn_ref(hidden_states, gate_w, w_gate, w_up, w_down, sw_gate, sw_up, sw_down):
        import jax, jax.numpy as jnp
        import numpy as np
        B, S, D = (1, 512, 256)
        E, K, F = (8, 2, 352)
        NS = 2
        SCALE = 2.5

        def _swiglu_mlp(x, wg, wu, wd):
            return jax.nn.silu(x @ wg) * (x @ wu) @ wd
        identity = hidden_states
        x = hidden_states.reshape(-1, hidden_states.shape[-1])
        T = x.shape[0]
        logits = x.astype(jnp.float32) @ gate_w.astype(jnp.float32).T
        scores = jax.nn.softmax(logits, axis=-1)
        topk_w, topk_i = jax.lax.top_k(scores, K)
        topk_w = topk_w / (topk_w.sum(-1, keepdims=True) + 1e-20) * SCALE
        combine = jnp.zeros((T, E), jnp.float32).at[jnp.arange(T)[:, None], topk_i].set(topk_w)
        g = jax.nn.silu(jnp.einsum('td,edf->etf', x, w_gate)) * jnp.einsum('td,edf->etf', x, w_up)
        expert_out = jnp.einsum('etf,efd->etd', g, w_down)
        y = jnp.einsum('te,etd->td', combine, expert_out).astype(x.dtype)
        y = y.reshape(identity.shape)
        return y + _swiglu_mlp(identity, sw_gate, sw_up, sw_down)
    x = x + _L0_xattn_ref(_layernorm(x, axis=-1), ctx_1024, L0_xattn_Wq, L0_xattn_bq, L0_xattn_Wk, L0_xattn_bk, L0_xattn_Wv, L0_xattn_bv, L0_xattn_Wo, L0_xattn_bo, 16)
    x = x + _L0_ffn_ref(_layernorm(x, axis=-1), L0_ffn_gate_w, L0_ffn_e_bias, L0_ffn_gate_proj, L0_ffn_up_proj, L0_ffn_down_proj, L0_ffn_shared_gate_w, L0_ffn_shared_up_w, L0_ffn_shared_down_w)
    x = x + _L1_xattn_ref(ctx_1024, mask_BxS2_bf1, _layernorm(x, axis=-1), L1_xattn_gm, L1_xattn_bm, L1_xattn_gl, L1_xattn_bl, L1_xattn_Wq, L1_xattn_Wk, L1_xattn_Wv, L1_xattn_Wo)
    x = x + _L1_ffn_ref(_layernorm(x, axis=-1), L1_ffn_gate_w, L1_ffn_w_gate, L1_ffn_w_up, L1_ffn_w_down, L1_ffn_sw_gate, L1_ffn_sw_up, L1_ffn_sw_down)
    return x

_drawn_inputs = setup_inputs


def setup_inputs(seed=0):
    import zlib

    import numpy as np

    out = dict(_drawn_inputs(seed))
    spreads = {'L0_xattn_bq': (0.0, 0.8),
     'L0_xattn_bk': (0.0, 2.0),
     'L0_xattn_bv': (0.0, 0.1),
     'L0_xattn_bo': (0.0, 0.1),
     'L0_ffn_e_bias': (0.0, 0.485),
     'L1_xattn_gm': (1.0, 0.2),
     'L1_xattn_bm': (0.0, 0.34),
     'L1_xattn_gl': (1.0, 0.6),
     'L1_xattn_bl': (0.0, 0.329)}
    factors = {'L0_xattn_Wq': 8.0,
     'L0_xattn_Wk': 8.0,
     'L0_ffn_gate_w': 7.85,
     'L0_ffn_gate_proj': 3.842,
     'L0_ffn_up_proj': 3.783,
     'L0_ffn_down_proj': 3.79,
     'L0_ffn_shared_gate_w': 4.857,
     'L0_ffn_shared_up_w': 4.789,
     'L0_ffn_shared_down_w': 4.801,
     'L1_ffn_gate_w': 4.167,
     'L1_ffn_w_gate': 3.649,
     'L1_ffn_w_up': 3.611,
     'L1_ffn_w_down': 3.617,
     'L1_ffn_sw_gate': 4.597,
     'L1_ffn_sw_up': 4.543,
     'L1_ffn_sw_down': 4.561}
    for name, (base, spread) in spreads.items():
        noise = np.random.default_rng([zlib.crc32(name.encode()), seed]).standard_normal(out[name].shape)
        drawn = base * np.exp(spread * noise) if base else spread * noise
        out[name] = jnp.asarray(drawn.astype(out[name].dtype))
    for name, factor in factors.items():
        out[name] = (out[name] * factor).astype(out[name].dtype)
    return out
```

```python
from contextlib import ExitStack

import concourse.bass as bass
from concourse import mybir

P = 128
B, S, D = 8, 512, 256
TPB = S // P
NT = B * TPB
DC = D // P
EPS = 1e-5

H0 = 16
HD0 = D // H0
STRIDE = 16
KPH = S // STRIDE
SCALE0 = HD0 ** -0.5

E0, G0, I0 = 16, 4, 128
PG0 = E0 // G0
TOPG0, TOPK0 = 2, 4
N0 = E0 + 1

H1, HD1 = 16, 64
INNER = H1 * HD1
KEYS = 2 * S
NKT = KEYS // P
SCALE1 = HD1 ** -0.5
NPAIR = H1 // 2
NQUAD = H1 // 4
MASKED = 1.0e30

E1, F1, NS1 = 8, 352, 2
TOPK1 = 2
N1 = E1 + NS1
FCH1 = [(0, 128), (128, 128), (256, 96)]
ROUTE_SCALE = 2.5

F32 = mybir.dt.float32
F32R = mybir.dt.float32r
U8 = mybir.dt.uint8
ALU = mybir.AluOpType
ACT = mybir.ActivationFunctionType
AX = mybir.AxisListType

HI, LO = 0, 1
PASSES = [(LO, HI), (HI, LO), (HI, HI)]


class Counted:

    def __init__(self, sem, base=0):
        self.sem, self.base, self.n = sem, base, 0

    def done(self, instruction, by=1):
        instruction.then_inc(self.sem, by)
        self.n += by
        return self.base + self.n

    def now(self):
        return self.base + self.n


def scope(nc, ctx):
    def sb(name, shape, dt=F32):
        return ctx.enter_context(nc.sbuf_tensor(name, shape, dt))

    def ps(name, shape, dt=F32):
        return ctx.enter_context(nc.psum_tensor(name, shape, dt))

    def sem(name):
        return ctx.enter_context(nc.semaphore(name))

    return sb, ps, sem


def ln_sems(sem, tag):
    return {n: sem(f"{tag}_{n}") for n in ("stats", "cleared", "moments", "var", "sd", "rstd", "xhat")}


LN_STATS, LN_ONE = TPB, 1


def ln_vector(dve, s, n, src, st, mv, ve, rs, dst):
    for t in range(TPB):
        dve.bn_stats(st[:, t, :], src(t)).then_inc(s["stats"], 1)
    dve.wait_ge(s["stats"], n * TPB + TPB)
    dve.memset(ve[:, :], 0.0).then_inc(s["cleared"], 1)
    for t in range(TPB):
        dve.bn_aggr(mv[:, t, :], st[:, t, :]).then_inc(s["moments"], 1)
    dve.wait_ge(s["moments"], n * TPB + TPB)
    dve.wait_ge(s["cleared"], n + 1)
    dve.tensor_scalar(ve[:, :], mv[:, :, 1], EPS, None, ALU.add).then_inc(s["var"], 1)
    dve.wait_ge(s["sd"], n + 1)
    dve.reciprocal(rs[:, :], ve[:, :]).then_inc(s["rstd"], 1)
    dve.wait_ge(s["rstd"], n + 1)
    for t in range(TPB):
        dve.tensor_scalar(dst(t), src(t), mv[:, t, 0:1], rs[:, t:t + 1], ALU.subtract,
                          ALU.mult).then_inc(s["xhat"], 1)


def ln_scalar(act, s, n, ve):
    act.wait_ge(s["var"], n + 1)
    act.activation(ve[:, :], ve[:, :], ACT.Sqrt).then_inc(s["sd"], 1)


def layer0_attention(nc, io, res, ident):
    with ExitStack() as ctx:
        sb, ps, sem = scope(nc, ctx)
        xT = sb("a_xT", [P, DC, B * S])
        cT = sb("a_cT", [P, DC, B * S])

        with ExitStack() as inner:
            sb1, ps1, sem1 = scope(nc, inner)
            cin = sb1("a_cin", [P, 2, TPB, D])
            xh = sb1("a_xh", [P, 2, TPB, D])
            ahead = sb1("a_ahead", [P, 4])
            st = sb1("a_st", [P, TPB, 6])
            mv = sb1("a_mv", [P, TPB, 2])
            ve = sb1("a_ve", [P, TPB])
            rs = sb1("a_rs", [P, TPB])
            px = [ps1(f"a_px{k}", [P, DC, S]) for k in range(2)]
            pc = [ps1(f"a_pc{k}", [P, DC, S]) for k in range(2)]
            x_in = [sem1(f"a_x_in{k}") for k in range(2)]
            c_in = [sem1(f"a_c_in{k}") for k in range(2)]
            ls = ln_sems(sem1, "a")
            x_turned, c_turned, x_out, c_out = (sem1(f"a_{n}") for n in ("x_turned", "c_turned", "x_out", "c_out"))

            with nc.Block() as block:
                @block.sync
                def _(sp):
                    with sp.Fori(0, B // 2) as i:
                        for k in range(2):
                            b = 2 * i + k
                            sp.wait_ge(x_out, b + 1)
                            sp.dma_start(res[:, bass.ds(b * TPB, TPB), :],
                                         io["x"][bass.ds(b, 1)].rearrange("b (t p) d -> p (b t) d", p=P)
                                         ).then_inc(x_in[k], 16)

                @block.gpsimd
                def _(pool):
                    with pool.Fori(0, B // 2) as i:
                        for k in range(2):
                            b = 2 * i + k
                            pool.wait_ge(c_out, b + 1)
                            for t in range(TPB):
                                hpt = P // KPH
                                pool.dma_start(cin[:, k, t, :],
                                               io["ctx"][bass.ds(b, 1)].rearrange(
                                                   "b (j h) d -> (b h) j d", h=STRIDE)[t * hpt:(t + 1) * hpt]
                                               ).then_inc(c_in[k], 16)

                @block.vector
                def _(dve):
                    for k in range(2):
                        dve.memset(ahead[:, k:k + 1], 0.0).then_inc(x_out, 1)
                    with dve.Fori(0, B // 2) as i:
                        for k in range(2):
                            b = 2 * i + k
                            dve.wait_ge(x_in[k], 16 * i + 16)
                            ln_vector(dve, ls, b, lambda t: res[:, bass.ds(b * TPB + t, 1), :].rearrange(
                                "p a d -> p (a d)"), st, mv, ve, rs, lambda t: xh[:, k, t, :])
                            dve.wait_ge(x_turned, b + 1)
                            dve.tensor_copy(xT[:, :, bass.ds(b * S, S)], px[k][:, :, :]).then_inc(x_out, 1)

                @block.scalar
                def _(act):
                    for k in range(2):
                        act.copy(ahead[:, 2 + k:3 + k], ident[:, 0:1]).then_inc(c_out, 1)
                    with act.Fori(0, B // 2) as i:
                        for k in range(2):
                            b = 2 * i + k
                            ln_scalar(act, ls, b, ve)
                            act.wait_ge(c_turned, b + 1)
                            act.copy(cT[:, :, bass.ds(b * S, S)], pc[k][:, :, :]).then_inc(c_out, 1)

                @block.tensor
                def _(pe):
                    with pe.Fori(0, B // 2) as i:
                        for k in range(2):
                            b = 2 * i + k
                            pe.wait_ge(c_in[k], 16 * TPB * (i + 1))
                            pe.wait_ge(c_out, b + 1)
                            for t in range(TPB):
                                for c in range(DC):
                                    last = pe.transpose(pc[k][:, c, t * P:(t + 1) * P],
                                                        cin[:, k, t, c * P:(c + 1) * P], ident[:, :])
                            last.then_inc(c_turned, 1)
                            pe.wait_ge(ls["xhat"], TPB * (b + 1))
                            pe.wait_ge(x_out, b + 1)
                            for t in range(TPB):
                                for c in range(DC):
                                    last = pe.transpose(px[k][:, c, t * P:(t + 1) * P],
                                                        xh[:, k, t, c * P:(c + 1) * P], ident[:, :])
                            last.then_inc(x_turned, 1)

        with ExitStack() as inner:
            sb2, ps2, sem2 = scope(nc, inner)
            w = {n: sb2(f"a_w{n}", [P, DC, D]) for n in "qkvo"}
            bias = {n: sb2(f"a_b{n}", [P, DC]) for n in "qkv"}
            bo = sb2("a_bo", [P, D])
            own = sb2("a_own", [P, S // 2])
            KT = sb2("a_KT", [P, DC, S // 2])
            VT = sb2("a_VT", [P, DC, S // 2])
            QT = sb2("a_QT", [P, DC, S])
            Vk = sb2("a_Vk", [P, 4, P])
            sc = sb2("a_sc", [P, 2, S])
            pr = sb2("a_pr", [P, 2, S])
            PT = sb2("a_PT", [P, 4, S])
            OT = sb2("a_OT", [P, DC, S])
            mx = sb2("a_mx", [P, 2, H0])
            sm = sb2("a_sm", [P, 2, H0])
            rc = sb2("a_rc", [P, 2, H0])
            yb = sb2("a_yb", [P, 2 * D])
            ahead = sb2("a_ahead2", [P, 8])
            pKV = ps2("a_pKV", [P, 2, S])
            pQ = ps2("a_pQ", [P, DC, S])
            pS = ps2("a_pS", [P, 2, S])
            pT = ps2("a_pT", [P, 2, S])
            names = ("w_in own_ready kv_done kv_used q_done q_ready v_ready vk_turned vk_ready s_done max_ready "
                     "shifted exp_ready sum_ready rcp_ready probs_ready p_turned p_used pv_done o_ready y_done "
                     "y_biased y_added").split()
            (w_in, own_ready, kv_done, k_ready, q_done, q_ready, v_ready, vk_turned, vk_ready, s_done, max_ready,
             shifted, exp_ready, sum_ready, rcp_ready, probs_ready, p_turned, p_ready, pv_done, o_ready, y_done,
             y_biased, y_added) = (sem2("a_" + n) for n in names)

            with nc.Block() as block:
                @block.sync
                def _(sp):
                    for n in "qkvo":
                        sp.dma_start(w[n][:, :, :], io[f"w{n}0"]).then_inc(w_in, 16)
                    for n in "qkv":
                        sp.dma_start(bias[n][:, :], io[f"b{n}0"]).then_inc(w_in, 16)
                    sp.dma_start(bo[:, :], io["bo0"].partition_broadcast(P)).then_inc(w_in, 16)

                @block.gpsimd
                def _(pool):
                    for k, (free, n) in enumerate(((v_ready, 2), (o_ready, 2), (y_added, 2), (p_ready, 1),
                                                   (shifted, 1), (s_done, 1), (vk_turned, 1), (pv_done, 1))):
                        pool.memset(ahead[:, k:k + 1], 0.0).then_inc(free, n)
                    pool.memset(own[:, :], 1.0).then_inc(own_ready, 1)
                    pool.wait_ge(own_ready, 1)
                    v = own[:, :].rearrange("p (h j) -> p h j", j=KPH)
                    pool.affine_select(out=v, in_=v, compare_op=ALU.is_ge, fill=0.0, base=0,
                                       pattern=[[-HD0, H0 // 2], [0, KPH]], channel_multiplier=1).then_inc(own_ready, 1)
                    pool.wait_ge(own_ready, 2)
                    pool.affine_select(out=v, in_=v, compare_op=ALU.is_ge, fill=0.0, base=HD0 - 1,
                                       pattern=[[HD0, H0 // 2], [0, KPH]], channel_multiplier=-1).then_inc(own_ready, 1)

                @block.tensor
                def _(pe):
                    pe.wait_ge(w_in, 128)
                    with pe.Fori(0, B) as b:
                        pe.wait_ge(v_ready, b * 2 + 2)
                        for m, n in enumerate("kv"):
                            for c in range(DC):
                                for k in range(DC):
                                    last = pe.matmul(pKV[:, m, c * 256:(c + 1) * 256],
                                                     w[n][:, k, c * P:(c + 1) * P],
                                                     cT[:, k, bass.ds(b * S + c * 256, 256)],
                                                     start=(k == 0), stop=(k == DC - 1))
                            last.then_inc(kv_done, 1)
                        pe.wait_ge(o_ready, b * 2 + 2)
                        for c in range(DC):
                            for k in range(DC):
                                last = pe.matmul(pQ[:, c, :], w["q"][:, k, c * P:(c + 1) * P],
                                                 xT[:, k, bass.ds(b * S, S)], start=(k == 0), stop=(k == DC - 1))
                            last.then_inc(q_done, 1)
                        pe.wait_ge(v_ready, b * 2 + 4)
                        pe.wait_ge(p_ready, b * TPB + 1)
                        for kc in range(4):
                            last = pe.transpose(pT[:, 0, kc * P:(kc + 1) * P],
                                                VT[:, kc // 2, (kc % 2) * P:(kc % 2 + 1) * P], ident[:, :])
                        last.then_inc(vk_turned, 1)

                        def scores(qt):
                            if qt == 0:
                                pe.wait_ge(k_ready, b * 2 + 2)
                                pe.wait_ge(q_ready, b * 2 + 2)
                                pe.wait_ge(y_added, b * 2 + 2)
                            else:
                                pe.wait_ge(shifted, b * TPB + qt)
                            for c in range(DC):
                                last = pe.matmul(pS[:, qt % 2, c * 256:(c + 1) * 256],
                                                 QT[:, c, qt * P:(qt + 1) * P], KT[:, c, :], start=True, stop=True)
                            last.then_inc(s_done, 1)

                        scores(0)
                        scores(1)
                        for qt in range(TPB):
                            pe.wait_ge(probs_ready, b * TPB + qt + 1)
                            if qt == 0:
                                pe.wait_ge(vk_ready, b + 1)
                            else:
                                pe.wait_ge(p_ready, b * TPB + qt)
                            for kc in range(4):
                                last = pe.transpose(pT[:, (qt + 1) % 2, kc * P:(kc + 1) * P],
                                                    pr[:, qt % 2, kc * P:(kc + 1) * P], ident[:, :])
                            last.then_inc(p_turned, 1)
                            if qt + 2 < TPB:
                                scores(qt + 2)
                        pe.wait_ge(p_ready, b * TPB + TPB + 1)
                        for c in range(DC):
                            for j in range(2):
                                last = pe.matmul(pQ[:, c, :], Vk[:, 2 * c + j, :], PT[:, 2 * c + j, :],
                                                 start=(j == 0), stop=(j == 1))
                            last.then_inc(pv_done, 1)
                        pe.wait_ge(o_ready, b * 2 + 4)
                        pe.wait_ge(shifted, b * TPB + TPB + 1)
                        for t in range(TPB):
                            for c in range(DC):
                                last = pe.matmul(pS[:, t // 2, (t % 2) * D:(t % 2 + 1) * D],
                                                 OT[:, c, t * P:(t + 1) * P], w["o"][:, c, :],
                                                 start=(c == 0), stop=(c == DC - 1))
                            if t % 2:
                                last.then_inc(y_done, 1)

                @block.vector
                def _(dve):
                    dve.wait_ge(w_in, 128)
                    dve.wait_ge(own_ready, 3)
                    with dve.Fori(0, B) as b:
                        for m, (n, out, ready) in enumerate((("k", KT, k_ready), ("v", VT, v_ready))):
                            dve.wait_ge(kv_done, 2 * b + m + 1)
                            if m == 0:
                                dve.wait_ge(s_done, b * TPB + 1)
                            else:
                                dve.wait_ge(vk_turned, b + 1)
                            for c in range(DC):
                                dve.scalar_tensor_tensor(out[:, c, :], pKV[:, m, c * 256:(c + 1) * 256],
                                                         bias[n][:, c:c + 1], own[:, :], ALU.add,
                                                         ALU.mult).then_inc(ready, 1)
                        for c in range(DC):
                            dve.wait_ge(q_done, 2 * b + c + 1)
                            dve.tensor_scalar(QT[:, c, :], pQ[:, c, :], bias["q"][:, c:c + 1], SCALE0, ALU.add,
                                              ALU.mult).then_inc(q_ready, 1)
                        for qt in range(TPB):
                            n = b * TPB + qt + 1
                            k = qt % 2

                            def heads(a):
                                return a.rearrange("p (h j) -> p h j", j=KPH)

                            def each(a):
                                return a.rearrange("p (h o) -> p h o", o=1).to_broadcast([P, H0, KPH])

                            dve.wait_ge(s_done, n + 1)
                            dve.tensor_reduce(mx[:, k, :], heads(pS[:, k, :]), AX.X, ALU.max).then_inc(max_ready, 1)
                            dve.wait_ge(max_ready, n)
                            if qt >= 2:
                                dve.wait_ge(exp_ready, n - 2)
                            dve.tensor_tensor(heads(sc[:, k, :]), heads(pS[:, k, :]), each(mx[:, k, :]),
                                              ALU.subtract).then_inc(shifted, 1)
                            dve.wait_ge(exp_ready, n)
                            dve.tensor_reduce(sm[:, k, :], heads(sc[:, k, :]), AX.X, ALU.add).then_inc(sum_ready, 1)
                            dve.wait_ge(sum_ready, n)
                            dve.reciprocal(rc[:, k, :], sm[:, k, :]).then_inc(rcp_ready, 1)
                            dve.wait_ge(rcp_ready, n)
                            if qt >= 2:
                                dve.wait_ge(p_turned, n - 2)
                            dve.tensor_tensor(heads(pr[:, k, :]), heads(sc[:, k, :]), each(rc[:, k, :]),
                                              ALU.mult).then_inc(probs_ready, 1)
                        for c in range(DC):
                            dve.wait_ge(pv_done, 2 * b + c + 2)
                            dve.tensor_copy(OT[:, c, :], pQ[:, c, :]).then_inc(o_ready, 1)
                        for m in range(2):
                            dve.wait_ge(y_done, 2 * b + m + 1)
                            dve.tensor_tensor(yb[:, :].rearrange("p (t d) -> p t d", d=D),
                                              pS[:, m, :].rearrange("p (t d) -> p t d", d=D),
                                              bo[:, :].rearrange("p (o d) -> p o d", o=1).to_broadcast([P, 2, D]),
                                              ALU.add).then_inc(y_biased, 1)
                            dve.wait_ge(y_biased, 2 * b + m + 1)
                            r = res[:, bass.ds(b * TPB + 2 * m, 2), :]
                            dve.tensor_tensor(r, r, yb[:, :].rearrange("p (t d) -> p t d", d=D),
                                              ALU.add).then_inc(y_added, 1)
                            dve.wait_ge(y_added, 2 * b + m + 3)

                @block.scalar
                def _(act):
                    with act.Fori(0, B) as b:
                        act.wait_ge(vk_turned, b + 2)
                        act.wait_ge(pv_done, 2 * b + 1)
                        act.copy(Vk[:, :, :].rearrange("p a d -> p (a d)"), pT[:, 0, :]).then_inc(vk_ready, 1)
                        for qt in range(TPB):
                            n = b * TPB + qt + 1
                            k = qt % 2
                            act.wait_ge(shifted, n + 1)
                            act.activation(sc[:, k, :], sc[:, k, :], ACT.Exp).then_inc(exp_ready, 1)
                            act.wait_ge(p_turned, n)
                            act.copy(PT[:, :, qt * P:(qt + 1) * P],
                                     pT[:, (qt + 1) % 2, :].rearrange("p (a q) -> p a q", q=P)).then_inc(p_ready, 1)


def moe_routes(nc, io, res, ident, XH, Wt, tag, E, route):
    with ExitStack() as ctx:
        sb, ps, sem = scope(nc, ctx)
        xh = sb(f"{tag}_xh", [P, 2, TPB, D])
        xs = sb(f"{tag}_xs", [P, 2, DC, S])
        gate = sb(f"{tag}_gate", [P, DC, E])
        st = sb(f"{tag}_st", [P, TPB, 6])
        mv = sb(f"{tag}_mv", [P, TPB, 2])
        ve = sb(f"{tag}_ve", [P, TPB])
        rs = sb(f"{tag}_rs", [P, TPB])
        ahead = sb(f"{tag}_ahead", [P, 4])
        px = [ps(f"{tag}_px{k}", [P, DC, S]) for k in range(2)]
        pl = ps(f"{tag}_pl", [P, NT, E])
        ls = ln_sems(sem, tag)
        gate_in, turned, x_copied, hi_done, lo_done, logits_done = (
            sem(f"{tag}_{n}") for n in ("gate_in", "turned", "x_copied", "hi_done", "lo_done", "logits_done"))
        r = route(nc, io, sb, sem, pl, Wt, logits_done, tag)

        with nc.Block() as block:
            @block.sync
            def _(sp):
                sp.dma_start(gate[:, :, :], io[f"{tag}_gate"]).then_inc(gate_in, 16)
                r["sync"](sp)

            @block.vector
            def _(dve):
                with dve.Fori(0, B // 2) as i:
                    for k in range(2):
                        b = 2 * i + k
                        ln_vector(dve, ls, b, lambda t: res[:, bass.ds(b * TPB + t, 1), :].rearrange(
                            "p a d -> p (a d)"), st, mv, ve, rs, lambda t: xh[:, k, t, :])
                        dve.wait_ge(x_copied, b + 3)
                        dve.tensor_copy(XH[:, HI, :, bass.ds(b * S, S)], xs[:, k, :, :]).then_inc(hi_done, 1)
                r["vector"](dve)

            @block.gpsimd
            def _(pool):
                for k in range(2):
                    pool.memset(ahead[:, k:k + 1], 0.0).then_inc(lo_done, 1)
                with pool.Fori(0, B // 2) as i:
                    for k in range(2):
                        b = 2 * i + k
                        pool.wait_ge(hi_done, b + 1)
                        for c in range(DC):
                            ins = pool.tensor_tensor(XH[:, LO, c, bass.ds(b * S, S)], xs[:, k, c, :],
                                                     XH[:, HI, c, bass.ds(b * S, S)].bitcast(F32), ALU.subtract)
                        ins.then_inc(lo_done, 1)
                r["gpsimd"](pool)

            @block.scalar
            def _(act):
                for k in range(2):
                    act.copy(ahead[:, 2 + k:3 + k], ident[:, 0:1]).then_inc(x_copied, 1)
                with act.Fori(0, B // 2) as i:
                    for k in range(2):
                        b = 2 * i + k
                        ln_scalar(act, ls, b, ve)
                        act.wait_ge(turned, b + 1)
                        act.wait_ge(lo_done, b + 1)
                        act.wait_ge(logits_done, b + 1)
                        act.copy(xs[:, k, :, :], px[k][:, :, :]).then_inc(x_copied, 1)
                r["scalar"](act)

            @block.tensor
            def _(pe):
                pe.wait_ge(gate_in, 16)
                for k in range(2):
                    pe.matmul(px[k][0:E, 0, 0:E], gate[:, 0, :], gate[:, 0, :], start=True,
                              stop=True).then_inc(logits_done, 1)
                pe.wait_ge(logits_done, 2)
                with pe.Fori(0, B // 2) as i:
                    for k in range(2):
                        b = 2 * i + k
                        pe.wait_ge(ls["xhat"], TPB * (b + 1))
                        pe.wait_ge(x_copied, b + 1)
                        for t in range(TPB):
                            for c in range(DC):
                                last = pe.transpose(px[k][:, c, t * P:(t + 1) * P],
                                                    xh[:, k, t, c * P:(c + 1) * P], ident[:, :])
                        last.then_inc(turned, 1)
                        pe.wait_ge(x_copied, b + 3)
                        for t in range(TPB):
                            for c in range(DC):
                                last = pe.matmul(pl[:, bass.ds(b * TPB + t, 1), :], xs[:, k, c, t * P:(t + 1) * P],
                                                 gate[:, c, :], start=(c == 0), stop=(c == DC - 1))
                        last.then_inc(logits_done, 1)


def over(a, n, axis):
    if axis == "last":
        return a.rearrange("p (m o) -> p m o", o=1).to_broadcast([P, a.shape[1], n])
    return a.rearrange("p (o m) -> p o m", o=1).to_broadcast([P, n, a.shape[1]])


def chosen(dve, c, v, G, E, top, before, wins, ties, rank, sel):
    a = v.rearrange("p (m o) -> p m o", o=1).to_broadcast([P, G * E, E])
    o = [x[:, 0:G * E * E].rearrange("p (m e) -> p m e", e=E) for x in (wins, ties)]
    for g0 in range(0, G, NT):
        pass
    w4 = [x[:, 0:G * E * E].rearrange("p (g e f) -> p g e f", e=E, f=E) for x in (wins, ties)]
    b4 = v.rearrange("p (g o f) -> p g o f", o=1, f=E).to_broadcast([P, G, E, E])
    a4 = v.rearrange("p (g e o) -> p g e o", e=E, o=1).to_broadcast([P, G, E, E])
    c.done(dve.tensor_tensor(w4[0], b4, a4, ALU.is_gt))
    n = c.done(dve.tensor_tensor(w4[1], b4, a4, ALU.is_equal))
    dve.wait_ge(c.sem, n)
    bf = before[:, 0:E, 0:E].rearrange("p (o e) f -> p o e f", o=1).to_broadcast([P, G, E, E])
    n = c.done(dve.tensor_tensor(w4[1], w4[1], bf, ALU.mult))
    dve.wait_ge(c.sem, n)
    n = c.done(dve.tensor_tensor(wins[:, 0:G * E * E], wins[:, 0:G * E * E], ties[:, 0:G * E * E], ALU.add))
    dve.wait_ge(c.sem, n)
    n = c.done(dve.tensor_reduce(rank, o[0], AX.X, ALU.add))
    dve.wait_ge(c.sem, n)
    n = c.done(dve.tensor_scalar(sel, rank, float(top), None, ALU.is_lt))
    dve.wait_ge(c.sem, n)


def weigh(dve, c, scores, sel, E, tot, Wt, shared):
    n = c.done(dve.tensor_tensor(sel, scores, sel, ALU.mult))
    dve.wait_ge(c.sem, n)
    n = c.done(dve.tensor_reduce(tot, sel.rearrange("p (t e) -> p t e", e=E), AX.X, ALU.add))
    dve.wait_ge(c.sem, n)
    n = c.done(dve.tensor_scalar(tot, tot, 1e-20, None, ALU.add))
    dve.wait_ge(c.sem, n)
    n = c.done(dve.reciprocal(tot, tot))
    dve.wait_ge(c.sem, n)
    n = c.done(dve.tensor_scalar(tot, tot, ROUTE_SCALE, None, ALU.mult))
    dve.wait_ge(c.sem, n)
    c.done(dve.memset(Wt[:, :, E:E + shared], 1.0))
    n = c.done(dve.tensor_tensor(Wt[:, :, 0:E], sel.rearrange("p (t e) -> p t e", e=E), over(tot, E, "last"),
                                 ALU.mult))
    dve.wait_ge(c.sem, n)


def make_before(pool, before, E, s):
    pool.memset(before[:, :, :], 1.0).then_inc(s, 1)
    pool.wait_ge(s, 1)
    pool.affine_select(out=before[:, :, :], in_=before[:, :, :], compare_op=ALU.is_ge, fill=0.0, base=-1,
                       pattern=[[1, E], [-1, E]], channel_multiplier=0).then_inc(s, 1)


def route0(nc, io, sb, sem, pl, Wt, logits_done, tag):
    sg, ch, sel, rank = (sb(f"{tag}_{n}", [P, NT * E0]) for n in ("sg", "ch", "sel", "rank"))
    pairs = sb(f"{tag}_pairs", [P, NT * G0, 6])
    gs, gsel, grank = (sb(f"{tag}_{n}", [P, NT * G0]) for n in ("gs", "gsel", "grank"))
    wins, ties = (sb(f"{tag}_{n}", [P, NT * E0 * E0]) for n in ("wins", "ties"))
    tot = sb(f"{tag}_tot", [P, NT])
    ebias = sb(f"{tag}_ebias", [P, E0])
    before = sb(f"{tag}_before", [P, E0, E0])
    bias_in, before_done, scored, steps = (sem(f"{tag}_{n}") for n in ("bias_in", "before_done", "scored", "steps"))

    def sync(sp):
        sp.dma_start(ebias[:, :], io["ebias"].partition_broadcast(P)).then_inc(bias_in, 16)

    def gpsimd(pool):
        make_before(pool, before, E0, before_done)

    def scalar(act):
        act.wait_ge(logits_done, B + 2)
        act.activation(sg[:, :], pl[:, :, :].rearrange("p t e -> p (t e)"), ACT.Sigmoid).then_inc(scored, 1)

    def vector(dve):
        c = Counted(steps)
        dve.wait_ge(scored, 1)
        dve.wait_ge(bias_in, 16)
        n = c.done(dve.tensor_tensor(ch[:, :].rearrange("p (t e) -> p t e", e=E0),
                                     sg[:, :].rearrange("p (t e) -> p t e", e=E0), over(ebias[:, :], NT, "ahead"),
                                     ALU.add))
        dve.wait_ge(c.sem, n)
        g = ch[:, :].rearrange("p (g e) -> p g e", e=PG0)
        c.done(dve.tensor_tensor(pairs[:, :, 0:3], g[:, :, 0:3], g[:, :, 1:4], ALU.add))
        c.done(dve.tensor_tensor(pairs[:, :, 3:5], g[:, :, 0:2], g[:, :, 2:4], ALU.add))
        n = c.done(dve.tensor_tensor(pairs[:, :, 5:6], g[:, :, 0:1], g[:, :, 3:4], ALU.add))
        dve.wait_ge(c.sem, n)
        n = c.done(dve.tensor_reduce(gs[:, :], pairs[:, :, :], AX.X, ALU.max))
        dve.wait_ge(c.sem, n)
        dve.wait_ge(before_done, 2)
        chosen(dve, c, gs[:, :], NT, G0, TOPG0, before, wins, ties, grank[:, :], gsel[:, :])
        n = c.done(dve.tensor_tensor(g, g, over(gsel[:, :], PG0, "last"), ALU.mult))
        dve.wait_ge(c.sem, n)
        chosen(dve, c, ch[:, :], NT, E0, TOPK0, before, wins, ties, rank[:, :], sel[:, :])
        weigh(dve, c, sg[:, :], sel[:, :], E0, tot[:, :], Wt, 1)

    return {"sync": sync, "gpsimd": gpsimd, "scalar": scalar, "vector": vector}


def moe_experts(nc, io, res, ident, XH, Wt, tag, NX, F):
    fch = [(f, min(P, F - f)) for f in range(0, F, P)]
    NF = len(fch)
    UPE = B * NF
    GU = 2 * DC * F
    whole = F // P
    nsplit = 2 if F % P else 1
    AHEAD = 2
    with ExitStack() as ctx:
        sb, ps, sem = scope(nc, ctx)
        raw_gu = sb(f"{tag}_raw_gu", [P, GU])
        raw_d = sb(f"{tag}_raw_d", [P, NF, D])
        Wgu = [sb(f"{tag}_Wgu{k}", [P, 2, GU], F32R) for k in range(2)]
        Wd = [sb(f"{tag}_Wd{k}", [P, 2, NF, D], F32R) for k in range(2)]
        sl = sb(f"{tag}_sl", [P, 2, S])
        hf = sb(f"{tag}_hf", [P, 2, S])
        hs = sb(f"{tag}_hs", [P, 2, 2, S], F32R)
        ahead = sb(f"{tag}_ahead", [P, 16])
        pG = [ps(f"{tag}_pG{k}", [P, S]) for k in range(2)]
        pU = [ps(f"{tag}_pU{k}", [P, S]) for k in range(2)]
        pY = [ps(f"{tag}_pY{k}", [P, TPB, D]) for k in range(2)]
        (raw_in, w_hi, w_lo, gu_done, silu_done, mult_done, hi_done, lo_done, d_done, added) = (
            sem(f"{tag}_{n}") for n in ("raw_in", "w_hi", "w_lo", "gu_done", "silu_done", "mult_done", "hi_done",
                                        "lo_done", "d_done", "added"))
        NW = 1 + nsplit
        LOADS = 2 + (nsplit - 1)

        def gu_view(w, g, k):
            return w[(g * DC + k) * F:(g * DC + k + 1) * F]

        def pieces(e2):
            k = e2 % 2
            yield Wgu[k][:, :, :], raw_gu[:, :], P
            if whole:
                yield (Wd[k][:, :, 0:whole, :].rearrange("p a f d -> p a (f d)"),
                       raw_d[:, 0:whole, :].rearrange("p f d -> p (f d)"), P)
            if F % P:
                yield Wd[k][0:F % P, :, whole, :], raw_d[0:F % P, whole, :], F % P

        def segments():
            tail = NX % 2 or 2
            return (NX - tail) // 2, tail

        loops, tail = segments()

        def for_units(eng, emit):
            with eng.Fori(0, loops) as i:
                for j in range(2):
                    for u in range(UPE):
                        emit(2 * i + j, j, u, False)
            for j in range(tail):
                for u in range(UPE):
                    emit(NX - tail + j, j, u, j == tail - 1 and u == UPE - 1)

        with nc.Block() as block:
            @block.sync
            def _(sp):
                def load(e, first=False):
                    if not first:
                        sp.wait_ge(w_lo, NW * e)
                    sp.dma_start(raw_gu[:, :], io[f"{tag}_gu"][bass.ds(e, 1)].rearrange("a p n -> (a p) n")
                                 ).then_inc(raw_in, 16)
                    if whole:
                        sp.dma_start(raw_d[:, 0:whole, :], io[f"{tag}_d"][bass.ds(e, 1), 0:whole * P].rearrange(
                            "a (f p) d -> p (a f) d", p=P)).then_inc(raw_in, 16)
                    if F % P:
                        sp.dma_start(raw_d[0:F % P, whole:whole + 1, :], io[f"{tag}_d"][
                            bass.ds(e, 1), whole * P:F].rearrange("a p d -> p a d")).then_inc(raw_in, 16)

                load(0, True)
                with sp.Fori(1, NX) as e:
                    load(e)

            def next_pair(e, j, u):
                return (e + 1, (j + 1) % 2, 0) if u == UPE - 1 else (e, j, u + 1)

            @block.tensor
            def _(pe):
                def gate_up(e, j, u):
                    n, f = divmod(u, NF)
                    f0, fw = fch[f]
                    U = e * UPE + u
                    if u == 0:
                        pe.wait_ge(w_lo, NW * (e + 1))
                    pe.wait_ge(mult_done, U + 1)
                    for g, out in enumerate((pG, pU)):
                        first = True
                        for k in range(DC):
                            for wp, xp in PASSES:
                                lhsT = Wgu[j][:, wp, (g * DC + k) * F + f0:(g * DC + k) * F + f0 + fw]
                                last = pe.matmul(out[u % 2][0:fw, :], lhsT, XH[:, xp, k, n * S:(n + 1) * S],
                                                 start=first, stop=(k == DC - 1 and (wp, xp) == PASSES[-1]))
                                first = False
                    last.then_inc(gu_done, 1)

                def down(e, j, u):
                    n, f = divmod(u, NF)
                    f0, fw = fch[f]
                    U = e * UPE + u
                    pe.wait_ge(lo_done, U + 1 + AHEAD)
                    if f == 0:
                        pe.wait_ge(added, TPB * (e * B + n) + TPB)
                    for t in range(TPB):
                        for m, (hp, wp) in enumerate(PASSES):
                            last = pe.matmul(pY[n % 2][:, t, :], hs[0:fw, u % 2, hp, t * P:(t + 1) * P],
                                             Wd[j][0:fw, wp, f, :],
                                             start=(f == 0 and m == 0 and t % 2 == 0),
                                             stop=(f == NF - 1 and m == len(PASSES) - 1),
                                             skip_group_check=True)
                    last.then_inc(d_done, 1)

                for k in range(2):
                    pe.matmul(pY[k][:, 0, 0:P], ident[:, :], ident[:, :], start=True, stop=True).then_inc(d_done, 1)
                pe.wait_ge(d_done, 2)
                gate_up(0, 0, 0)

                def emit(e, j, u, last):
                    if not last:
                        gate_up(*next_pair(e, j, u))
                    down(e, j, u)
                for_units(pe, emit)

            @block.scalar
            def _(act):
                def split(e, j):
                    act.wait_ge(raw_in, 16 * LOADS * (e + 1))
                    act.wait_ge(d_done, e * UPE - UPE + AHEAD if not isinstance(e, int) or e > 1 else AHEAD)
                    for out, raw, rows in pieces(j):
                        act.copy(out[:, HI, :], raw).then_inc(w_hi, 1)

                split(0, 0)

                def emit(e, j, u, last):
                    n, f = divmod(u, NF)
                    fw = fch[f][1]
                    U = e * UPE + u
                    act.wait_ge(gu_done, U + 1)
                    act.wait_ge(mult_done, U + 1)
                    act.activation(sl[0:fw, u % 2, :], pG[u % 2][0:fw, :], ACT.Silu).then_inc(silu_done, 1)
                    act.wait_ge(mult_done, U + 1 + AHEAD)
                    act.wait_ge(d_done, U + 1)
                    act.copy(hs[0:fw, u % 2, HI, :], hf[0:fw, u % 2, :]).then_inc(hi_done, 1)
                    if u == 1 and not (isinstance(e, int) and e == NX - 1):
                        split(e + 1, (j + 1) % 2)
                for_units(act, emit)

            @block.gpsimd
            def _(pool):
                for k in range(AHEAD):
                    pool.memset(ahead[:, k:k + 1], 0.0).then_inc(lo_done, 1)

                def split(e, j):
                    for m, (out, raw, rows) in enumerate(pieces(j)):
                        pool.wait_ge(w_hi, NW * e + m + 1)
                        pool.tensor_tensor(out[:, LO, :], raw, out[:, HI, :].bitcast(F32), ALU.subtract
                                           ).then_inc(w_lo, 1)

                split(0, 0)

                def emit(e, j, u, last):
                    n, f = divmod(u, NF)
                    fw = fch[f][1]
                    U = e * UPE + u
                    pool.wait_ge(hi_done, U + 1)
                    pool.tensor_tensor(hs[0:fw, u % 2, LO, :], hf[0:fw, u % 2, :],
                                       hs[0:fw, u % 2, HI, :].bitcast(F32), ALU.subtract).then_inc(lo_done, 1)
                    if u == 1 and not (isinstance(e, int) and e == NX - 1):
                        split(e + 1, (j + 1) % 2)
                for_units(pool, emit)

            @block.vector
            def _(dve):
                for k in range(AHEAD):
                    dve.memset(ahead[:, 2 + k:3 + k], 0.0).then_inc(mult_done, 1)
                for k in range(2 * TPB):
                    dve.memset(ahead[:, 4 + k:5 + k], 0.0).then_inc(added, 1)

                def mult(e, j, u):
                    n, f = divmod(u, NF)
                    fw = fch[f][1]
                    U = e * UPE + u
                    dve.wait_ge(silu_done, U + 1)
                    dve.wait_ge(lo_done, U + 1)
                    dve.tensor_tensor(hf[0:fw, u % 2, :], sl[0:fw, u % 2, :], pU[u % 2][0:fw, :], ALU.mult
                                      ).then_inc(mult_done, 1)

                def add(e, n):
                    dve.wait_ge(d_done, e * UPE + NF * (n + 1) + AHEAD)
                    dve.wait_ge(added, TPB * (e * B + n) + 2 * TPB)
                    for t in range(TPB):
                        tile = n * TPB + t
                        dve.scalar_tensor_tensor(res[:, tile, :], pY[n % 2][:, t, :], Wt[:, tile, bass.ds(e, 1)],
                                                 res[:, tile, :], ALU.mult, ALU.add).then_inc(added, 1)

                mult(0, 0, 0)

                def emit(e, j, u, last):
                    if not last:
                        mult(*next_pair(e, j, u))
                    if u % NF == NF - 1:
                        add(e, u // NF)
                for_units(dve, emit)


def layer0_ffn(nc, io, res, ident):
    with ExitStack() as ctx:
        sb, ps, sem = scope(nc, ctx)
        Wt = sb("m0_Wt", [P, NT, N0])
        XH = sb("m0_XH", [P, 2, DC, B * S], F32R)
        moe_routes(nc, io, res, ident, XH, Wt, "m0", E0, route0)
        moe_experts(nc, io, res, ident, XH, Wt, "e0", N0, I0)


def route1(nc, io, sb, sem, pl, Wt, logits_done, tag):
    lg, sel, rank = (sb(f"{tag}_{n}", [P, NT * E1]) for n in ("lg", "sel", "rank"))
    wins, ties = (sb(f"{tag}_{n}", [P, NT * E1 * E1]) for n in ("wins", "ties"))
    tot = sb(f"{tag}_tot", [P, NT])
    before = sb(f"{tag}_before", [P, E1, E1])
    before_done, shifted, exp_done, steps = (sem(f"{tag}_{n}") for n in ("before_done", "shifted", "exp_done", "steps"))

    def sync(sp):
        pass

    def gpsimd(pool):
        make_before(pool, before, E1, before_done)

    def scalar(act):
        act.wait_ge(shifted, 1)
        act.activation(lg[:, :], lg[:, :], ACT.Exp).then_inc(exp_done, 1)

    def vector(dve):
        c = Counted(steps)
        by_token = lg[:, :].rearrange("p (t e) -> p t e", e=E1)
        dve.wait_ge(logits_done, B + 2)
        n = c.done(dve.tensor_reduce(tot[:, :], pl[:, :, :], AX.X, ALU.max))
        dve.wait_ge(c.sem, n)
        dve.tensor_tensor(by_token, pl[:, :, :], over(tot[:, :], E1, "last"), ALU.subtract).then_inc(shifted, 1)
        dve.wait_ge(exp_done, 1)
        n = c.done(dve.tensor_reduce(tot[:, :], by_token, AX.X, ALU.add))
        dve.wait_ge(c.sem, n)
        n = c.done(dve.reciprocal(tot[:, :], tot[:, :]))
        dve.wait_ge(c.sem, n)
        n = c.done(dve.tensor_tensor(by_token, by_token, over(tot[:, :], E1, "last"), ALU.mult))
        dve.wait_ge(c.sem, n)
        dve.wait_ge(before_done, 2)
        chosen(dve, c, lg[:, :], NT, E1, TOPK1, before, wins, ties, rank[:, :], sel[:, :])
        weigh(dve, c, lg[:, :], sel[:, :], E1, tot[:, :], Wt, NS1)

    return {"sync": sync, "gpsimd": gpsimd, "scalar": scalar, "vector": vector}


def layer1_ffn(nc, io, res, ident):
    with ExitStack() as ctx:
        sb, ps, sem = scope(nc, ctx)
        Wt = sb("m1_Wt", [P, NT, N1])
        XH = sb("m1_XH", [P, 2, DC, B * S], F32R)
        moe_routes(nc, io, res, ident, XH, Wt, "m1", E1, route1)
        moe_experts(nc, io, res, ident, XH, Wt, "e1", N1, F1)


def layer1_keys_in(nc, io, res, ident, kv, wsp, mb):
    with ExitStack() as ctx:
        sb, ps, sem = scope(nc, ctx)
        cin = sb("c_cin", [P, 2, TPB, D])
        xh = [sb(f"c_xh{m}", [P, 2, TPB, D]) for m in range(2)]
        stv = [sb(f"c_st{m}", [P, TPB, 6]) for m in range(2)]
        mvv = [sb(f"c_mv{m}", [P, TPB, 2]) for m in range(2)]
        vev = [sb(f"c_ve{m}", [P, TPB]) for m in range(2)]
        rsv = [sb(f"c_rs{m}", [P, TPB]) for m in range(2)]
        la = sb("c_la", [P, TPB, D])
        gb = sb("c_gb", [P, 2, 2, DC])
        yf = sb("c_yf", [P, 2, DC, S])
        ys = sb("c_ys", [P, 2, 2, DC, S], F32R)
        wr = sb("c_wr", [P, 3, DC, INNER])
        wq = sb("c_wq", [P, 2, 3, DC, 256], F32R)
        m8 = sb("c_m8", [B, S], U8)
        mrow = sb("c_mrow", [B, KEYS], F32R)
        ahead = sb("c_ahead", [P, 8])
        px = [ps(f"c_px{m}", [P, DC, S]) for m in range(2)]
        (cin0, cin1, w_in, m_in, m_ready, turned, y_done, y_hi, y_lo, kv_out0, kv_out1, wq_hi, wq_lo, wq_out,
         m_out) = (sem("c_" + n) for n in (
             "cin0 cin1 w_in m_in m_ready turned y_done y_hi y_lo kv_out0 kv_out1 wq_hi wq_lo wq_out m_out"
         ).split())
        cin_s, kv_out = [cin0, cin1], [kv_out0, kv_out1]
        lsc, lsl = ln_sems(sem, "cc"), ln_sems(sem, "cl")

        with nc.Block() as block:
            @block.sync
            def _(sp):
                for m in range(2):
                    sp.dma_start(gb[:, m, :, :], io["gb1"][:, m]).then_inc(kv_out[m], 16)
                sp.dma_start(m8[:, :], io["mask"]).then_inc(m_in, 16)
                with sp.Fori(0, B // 2) as i:
                    for k in range(2):
                        b = 2 * i + k
                        sp.wait_ge(turned, 2 * b + 1)
                        for t in range(TPB):
                            hpt = P // KPH
                            sp.dma_start(cin[:, k, t, :],
                                         io["ctx"][bass.ds(b, 1)].rearrange("b (j h) d -> (b h) j d", h=STRIDE)[
                                             t * hpt:(t + 1) * hpt]).then_inc(cin_s[k], 16)
                        for m in range(2):
                            sp.wait_ge(y_lo, 2 * b + m + 1 + 2)
                            sp.dma_start(kv[bass.ds(b, 1), :, :, :, m * S:(m + 1) * S].rearrange(
                                "b p a c n -> p (b a) c n"), ys[:, m, :, :, :].bitcast(F32)).then_inc(kv_out[m], 16)
                for m in range(2):
                    sp.wait_ge(kv_out[m], 16 * B + 16)

            @block.gpsimd
            def _(pool):
                pool.memset(ahead[:, 4:5], 0.0).then_inc(turned, 4)
                pool.wait_ge(m_in, 16)
                pool.memset(mrow[:, S:KEYS].bitcast(F32), 0.0).then_inc(m_ready, 1)
                pool.tensor_scalar(mrow[:, 0:S].rearrange("b (h j) -> b j h", j=KPH),
                                   m8[:, :].rearrange("b (j h) -> b j h", h=STRIDE), -1.0, MASKED, ALU.add, ALU.mult
                                   ).then_inc(m_ready, 1)
                pool.wait_ge(m_ready, 2)
                pool.dma_start(mb, mrow[:, :].bitcast(F32)).then_inc(m_out, 16)
                pool.wait_ge(w_in, 48)
                for q in range(NQUAD):
                    pool.wait_ge(wq_hi, q + 1)
                    pool.tensor_tensor(wq[:, LO, :, :, :].rearrange("p w c n -> p (w c) n"),
                                       wr[:, :, :, q * 256:(q + 1) * 256].rearrange("p w c n -> p (w c) n"),
                                       wq[:, HI, :, :, :].rearrange("p w c n -> p (w c) n").bitcast(F32),
                                       ALU.subtract).then_inc(wq_lo, 1)
                    pool.wait_ge(wq_lo, q + 1)
                    pool.dma_start(wsp[q].rearrange("p a w c n -> p (a w c n)"),
                                   wq[:, :, :, :, :].rearrange("p a w c n -> p (a w c n)").bitcast(F32)).then_inc(wq_out, 16)
                pool.wait_ge(m_out, 16)
                pool.wait_ge(wq_out, 16 * NQUAD)

            @block.scalar
            def _(act):
                for m, n in enumerate("kvq"):
                    act.dma_start(wr[:, m, :, :], io[f"w{n}1"]).then_inc(w_in, 16)
                with act.Fori(0, B) as b:
                    ln_scalar(act, lsc, b, vev[0])
                    ln_scalar(act, lsl, 2 * b, vev[1])
                    ln_scalar(act, lsl, 2 * b + 1, vev[1])
                    for m in range(2):
                        act.wait_ge(y_done, DC * (2 * b + m + 1) + 2 * DC)
                        act.wait_ge(kv_out[m], 16 * b + 16)
                        act.copy(ys[:, m, HI, :, :], yf[:, m, :, :]).then_inc(y_hi, 1)
                act.wait_ge(w_in, 48)
                for q in range(NQUAD):
                    if q:
                        act.wait_ge(wq_out, 16 * q)
                    act.copy(wq[:, HI, :, :, :].rearrange("p w c n -> p (w c) n"),
                             wr[:, :, :, q * 256:(q + 1) * 256].rearrange("p w c n -> p (w c) n")).then_inc(wq_hi, 1)

            @block.vector
            def _(dve):
                for m in range(2):
                    dve.wait_ge(kv_out[m], 16)
                    dve.memset(ahead[:, m:m + 1], 0.0).then_inc(y_lo, 1)
                    dve.memset(ahead[:, 2 + m:3 + m], 0.0).then_inc(y_done, DC)
                with dve.Fori(0, B // 2) as i:
                    for k in range(2):
                        b = 2 * i + k
                        tile = lambda t: res[:, bass.ds(b * TPB + t, 1), :].rearrange("p a d -> p (a d)")
                        dve.wait_ge(cin_s[k], 16 * TPB * (i + 1))
                        ln_vector(dve, lsc, b, lambda t: cin[:, k, t, :], stv[0], mvv[0], vev[0], rsv[0],
                                  lambda t: xh[0][:, k, t, :])
                        ln_vector(dve, lsl, 2 * b, tile, stv[1], mvv[1], vev[1], rsv[1], lambda t: la[:, t, :])
                        dve.wait_ge(lsl["xhat"], TPB * (2 * b + 1))
                        ln_vector(dve, lsl, 2 * b + 1, lambda t: la[:, t, :], stv[1], mvv[1], vev[1], rsv[1],
                                  lambda t: xh[1][:, k, t, :])
                        for m in range(2):
                            dve.wait_ge(turned, 2 * b + m + 1 + 4)
                            dve.wait_ge(y_lo, 2 * b + m + 1)
                            for c in range(DC):
                                dve.tensor_scalar(yf[:, m, c, :], px[m][:, c, :], gb[:, m, 0, c:c + 1],
                                                  gb[:, m, 1, c:c + 1], ALU.mult, ALU.add).then_inc(y_done, 1)
                            dve.wait_ge(y_hi, 2 * b + m + 1)
                            dve.tensor_tensor(ys[:, m, LO, :, :], yf[:, m, :, :], ys[:, m, HI, :, :].bitcast(F32),
                                              ALU.subtract).then_inc(y_lo, 1)

            @block.tensor
            def _(pe):
                with pe.Fori(0, B // 2) as i:
                    for k in range(2):
                        b = 2 * i + k
                        for m, done in enumerate((TPB * (b + 1), TPB * (2 * b + 2))):
                            pe.wait_ge((lsc, lsl)[m]["xhat"], done)
                            pe.wait_ge(y_done, DC * (2 * b + m + 1))
                            for t in range(TPB):
                                for c in range(DC):
                                    last = pe.transpose(px[m][:, c, t * P:(t + 1) * P],
                                                        xh[m][:, k, t, c * P:(c + 1) * P], ident[:, :])
                            last.then_inc(turned, 1)


class Step:

    def __init__(self, g, parity, half, b=None, batch_half=None, off=None):
        self.g, self.parity, self.by2, self.b, self.batch_half, self.off = g, parity, half, b, batch_half, off


NSTEP = B * NPAIR


def misc_uses(g0, parity):
    if g0 == 0:
        return ["K0", "K1", "Q"]
    if g0 == NSTEP - 1 or g0 == NSTEP:
        return ["den", "R", "Y0", "Y1"]
    if parity:
        return ["K0", "K1", "den", "Q", "R", "V0", "Y0", "Y1", "V1", "V2", "V3"]
    return ["K0", "K1", "den", "Q", "R", "Y0", "Y1"]


PROLOGUE = ["K0", "K1", "Q", "V0", "V1", "V2", "V3"]


def use_before(st):
    if isinstance(st.g, int):
        if st.g == -1:
            return 0
        if st.g == 0:
            return len(PROLOGUE)
        if st.g == NSTEP:
            return 9 * (NSTEP - 1) + 1 + 4
    return 9 * st.g + (1 if st.parity else 3)


def uses_of(st):
    if isinstance(st.g, int):
        if st.g == -1:
            return PROLOGUE
        if st.g in (0, NSTEP - 1, NSTEP):
            return misc_uses(st.g, st.parity)
    return misc_uses(None, st.parity)


def use(st, name):
    return use_before(st) + uses_of(st).index(name) + 1


def order(st):
    if isinstance(st.g, int) and st.g == -1:
        return [(u, 0) for u in PROLOGUE] + [("S", c) for c in range(8)] + [("M", 0)]
    has = uses_of(st)
    nxt, fin = "K0" in has, "den" in has
    out = []

    def put(*names):
        out.extend((n, 0) for n in names if n in has)

    if fin:
        out += [("PVlast", 0), ("O", 0)]
    if isinstance(st.g, int) and st.g == NSTEP:
        put("den", "R", "Y0", "Y1")
        return out
    put("K0")
    after_scores = {1: ["K1"], 2: ["Q"], 3: ["V0"], 4: ["Y0"], 5: ["Y1"], 6: ["V2"]}
    after_outputs = {1: ["den"], 2: ["R"], 5: ["V1"], 7: ["V3"]}
    for s in range(NKT):
        if nxt and s >= 4:
            out.append(("S", 2 * (s - 4)))
        out.append(("ST", s))
        put(*after_scores.get(s, []))
        if nxt and s >= 4:
            out.append(("S", 2 * (s - 4) + 1))
        if s:
            out.append(("PV", s - 1))
        put(*after_outputs.get(s, []))
    if nxt:
        out.append(("M", 0))
    return out


def for_steps(eng, emit, unroll_halves=False):
    emit(Step(-1, 1, None))
    emit(Step(0, 0, 0, 0, 0, 0))

    def four(b, h):
        for off in range(1, 5):
            emit(Step(8 * b + 4 * h + off, off % 2, 4 * b + 2 * h + off // 2, b, h, off))

    with eng.Fori(0, B - 1) as b:
        if unroll_halves:
            four(b, 0)
            four(b, 1)
        else:
            with eng.Fori(0, 2) as h:
                four(b, h)
    four(B - 1, 0)
    for off in range(1, 4):
        emit(Step(NSTEP - 4 + off, off % 2, NSTEP // 2 - 2 + off // 2, B - 1, 1, off))
    emit(Step(NSTEP, 0, NSTEP // 2, B - 1, 1, 4))


def layer1_pairs(nc, io, res, ident, kv_d, wsp, mb):
    with ExitStack() as ctx:
        sb, ps, sem = scope(nc, ctx)
        kv = sb("d_kv", [P, 2, DC, KEYS], F32R)
        W = [sb(f"d_W{k}", [P, 2, 3, DC, 256], F32R) for k in range(2)]
        K1, K2 = ([[sb(f"d_{n}{j}{h}", [P, KEYS], F32R) for h in range(2)] for j in range(2)] for n in ("K1", "K2"))
        Q0, Q1, Q2 = ([[sb(f"d_{n}{j}{h}", [P, S], F32R) for h in range(2)] for j in range(2)]
                      for n in ("Q0", "Q1", "Q2"))
        V = [sb(f"d_V{k}", [P, NKT, 256]) for k in range(2)]
        pr = sb("d_pr", [P, 4, 2, S])
        acc = sb("d_acc", [P, 2, 2, S])
        osb = sb("d_osb", [P, 2, S])
        rb = sb("d_rb", [P, S])
        OT = sb("d_OT", [P, 2, S])
        Wo = sb("d_Wo", [P, NPAIR, D])
        nm = sb("d_nm", [P, 2, 8])
        rc = sb("d_rc", [P, 2, 8])
        ones = sb("d_ones", [P, 2])
        onerow = sb("d_onerow", [1, KEYS], F32R)
        ahead = sb("d_ahead", [P, 8])
        pT = [ps(f"d_pT{k}", [P, 2, S]) for k in range(2)]
        pS = ps("d_pS", [P, 2, S])
        pO = ps("d_pO", [P, S])
        pm = ps("d_pm", [P, S])
        (set_up, set_rows, wo_in, kv_in, misc_done, misc_read, k_hi, q_hi, s_done, max_done, m_done, m_copied,
         st_done, exp_done, pv_done, acc_done, o_copied, ot_done, den_read) = (sem("d_" + n) for n in (
             "set_up set_rows wo_in kv_in misc_done misc_read k_hi q_hi s_done max_done m_done m_copied st_done "
             "exp_done pv_done acc_done o_copied ot_done den_read").split())
        w_in = [sem(f"d_w_in{k}") for k in range(2)]
        copies = [sem(f"d_copies{k}") for k in range(2)]

        own = (slice(0, HD1), slice(HD1, P))
        other = (slice(HD1, P), slice(0, HD1))
        row0 = (HD1, 0)
        NCOPY = 16 * 8
        PT = 4
        tiles = {h: h for h in range(2)}

        def pair(st):
            if isinstance(st.g, int) and st.g == -1:
                return 0, 0, 0
            return (st.parity + 1) % 2, st.g + 1, st.by2 + (1 if st.parity else 0)

        with nc.Block() as block:
            @block.sync
            def _(sp):
                sp.dma_start(kv[:, :, :, :].bitcast(F32), kv_d[0]).then_inc(kv_in, 16)
                for k in range(2):
                    sp.dma_start(W[k][:, :, :, :, :].bitcast(F32), wsp[k]).then_inc(w_in[k], 16)
                sp.dma_start(Wo[:, :, :], io["wo1"]).then_inc(wo_in, 16)
                sp.wait_ge(set_up, 14)
                for j in range(2):
                    for h in range(2):
                        sp.dma_start(K2[j][h][row0[h]:row0[h] + 1, :].bitcast(F32), onerow[:, :].bitcast(F32)).then_inc(set_rows, 16)
                        for q in (Q0, Q2):
                            sp.dma_start(q[j][h][row0[h] + 1:row0[h] + 2, :].bitcast(F32), onerow[:, 0:S].bitcast(F32)).then_inc(set_rows, 16)
                sp.wait_ge(set_rows, 12 * 16)

                def emit(st):
                    j, gp, by2 = pair(st)
                    first = isinstance(st.g, int) and st.g == -1
                    for what, _ in order(st):
                        if what == "K1":
                            if first or st.off == 0:
                                bb = 0
                            elif st.batch_half == 1 and st.off == 3:
                                bb = st.b + 1
                            elif st.batch_half == 1 and st.off == 4:
                                bb = st.b + 1
                            else:
                                bb = st.b
                            sp.wait_ge(k_hi, 4 * gp + 4)
                            for h in range(2):
                                sp.dma_start(K2[j][h][own[h], :].bitcast(F32), K1[j][h][own[h], :].bitcast(F32)).then_inc(copies[j], 16)
                                sp.dma_start(K2[j][h][row0[h] + 1:row0[h] + 2, :].bitcast(F32),
                                             mb[bass.ds(bb, 1), :]).then_inc(copies[j], 16)
                        if what == "Q":
                            sp.wait_ge(q_hi, 2 * gp + 2)
                            for h in range(2):
                                for q, rows in ((Q1, other), (Q0, own)):
                                    sp.dma_start(q[j][h][rows[h], :].bitcast(F32), Q1[j][h][own[h], :].bitcast(F32)).then_inc(copies[j], 16)
                            if not first and not st.parity and st.off:
                                k = 1 if st.off == 2 else 0
                                nq = (2 * st.batch_half + (3 if st.off == 2 else 4)) % NQUAD
                                sp.wait_ge(misc_done, use(st, "Q"))
                                if not (isinstance(st.g, int) and st.g >= NSTEP - 4 + 2):
                                    sp.dma_start(W[k][:, :, :, :, :].bitcast(F32), wsp[nq]).then_inc(w_in[k], 16)
                                if st.batch_half == 1 and st.off == 2 and not isinstance(st.b, int):
                                    sp.dma_start(kv[:, :, :, :].bitcast(F32), kv_d[bass.ds(st.b + 1, 1)].rearrange(
                                        "b p a c n -> (b p) a c n")).then_inc(kv_in, 16)
                            if not first and st.off == 0:
                                sp.wait_ge(misc_done, use(st, "Q"))
                                sp.dma_start(W[0][:, :, :, :, :].bitcast(F32), wsp[2]).then_inc(w_in[0], 16)
                for_steps(sp, emit, unroll_halves=True)

            @block.tensor
            def _(pe):
                pe.wait_ge(set_rows, 12 * 16)
                pe.wait_ge(set_up, 14)
                pe.wait_ge(wo_in, 16)

                def emit(st):
                    first = isinstance(st.g, int) and st.g == -1
                    j, gp, by2 = pair(st)
                    nq = 0 if first else (gp_quad := None)
                    names = uses_of(st)
                    T = None if first else NKT * st.g
                    q = st.parity

                    def bank(name):
                        n = use(st, name)
                        if not (isinstance(n, int) and n == 1):
                            pe.wait_ge(misc_read, n - 1)

                    if first or st.off == 0:
                        wk = 0
                    else:
                        wk = {1: 1, 2: 1, 3: 0, 4: 0}[st.off]

                    def project(w, i):
                        for c in range(DC):
                            for n, (wp, xp) in enumerate(PASSES):
                                last = pe.matmul(pm[:, :], W[wk][:, wp, w, c, j * P:(j + 1) * P],
                                                 kv[:, xp, c, i * S:(i + 1) * S], start=(c == 0 and n == 0),
                                                 stop=(c == DC - 1 and n == len(PASSES) - 1))
                        last.then_inc(misc_done, 1)

                    def outputs(par, s, tt, vb):
                        pe.wait_ge(exp_done, tt + 1 + 2)
                        for h in range(2):
                            last = pe.matmul(pO[own[h], :], V[vb][:, s, par * P + h * HD1:par * P + (h + 1) * HD1],
                                             pr[:, s % PT, h, :], start=(s == 0), stop=(s == NKT - 1),
                                             skip_group_check=True)
                        last.then_inc(pv_done, 1)

                    if not first:
                        vb_now = {0: 0, 1: 0, 2: 1, 3: 1, 4: 0}[st.off]
                        vb_last = {0: 0, 1: 0, 2: 0, 3: 1, 4: 1}[st.off]
                    for what, n in order(st):
                        if what in ("K0", "K1"):
                            bank(what)
                            if what == "K0":
                                if first:
                                    pe.wait_ge(kv_in, 16)
                                    pe.wait_ge(w_in[0], 16)
                                elif st.off in (1, 3):
                                    pe.wait_ge(w_in[wk], 16 * (st.by2 // 2 + 1) if isinstance(st.by2, int) else
                                               16 * (2 * st.b + st.batch_half) + (16 if st.off == 1 else 32))
                                    if st.off == 3:
                                        pe.wait_ge(kv_in, 16 * (st.b + st.batch_half + 1))
                            project(0, n if False else int(what[1]))
                        elif what == "Q":
                            bank(what)
                            project(2, 1)
                        elif what[0] == "V":
                            i = int(what[1])
                            bank(what)
                            for t in range(2):
                                kt = 2 * i + t
                                for c in range(DC):
                                    for m, (xp, wp) in enumerate(PASSES):
                                        last = pe.matmul(pm[:, t * 256:(t + 1) * 256],
                                                         kv[:, xp, c, kt * P:(kt + 1) * P], W[wk][:, wp, 1, c, :],
                                                         start=(c == 0 and m == 0),
                                                         stop=(c == DC - 1 and m == len(PASSES) - 1))
                            last.then_inc(misc_done, 1)
                        elif what == "S":
                            h, qt = divmod(n, TPB)
                            if n == 0:
                                pe.wait_ge(copies[j], NCOPY * (by2 + 1))
                                if not first:
                                    pe.wait_ge(m_copied, 2 * gp)
                            if n or not first:
                                pe.wait_ge(max_done, 8 * gp + n)
                            for m in range(2):
                                last = pe.matmul(pS[:, m, :], Q0[j][h][:, qt * P:(qt + 1) * P],
                                                 K2[j][h][:, m * S:(m + 1) * S], start=True, stop=True)
                            last.then_inc(s_done, 1)
                        elif what == "M":
                            pe.wait_ge(max_done, 8 * gp + 8)
                            for h in range(2):
                                for qt in range(TPB):
                                    last = pe.matmul(pS[row0[h]:row0[h] + 1, 0, qt * P:(qt + 1) * P],
                                                     nm[:, j, h * TPB + qt:h * TPB + qt + 1], ident[:, :],
                                                     start=True, stop=True)
                            last.then_inc(m_done, 1)
                        elif what == "ST":
                            s = n
                            if s == 0:
                                pe.wait_ge(m_copied, 2 * st.g + 2)
                                prev = Step(-1, 1, None) if isinstance(st.g, int) and st.g == 0 else (
                                    Step(0, 0, 0) if isinstance(st.g, int) and st.g == 1 else
                                    Step(st.g - 1, 1 - st.parity, None))
                                pe.wait_ge(misc_read, use(prev, "Q"))
                            pe.wait_ge(exp_done, T + s + 1)
                            for h in range(2):
                                pe.matmul(pT[s % 2][:, h, :], K1[q][h][:, s * P:(s + 1) * P], Q1[q][h][:, :],
                                          start=True, stop=False)
                                last = pe.matmul(pT[s % 2][:, h, :], K2[q][h][:, s * P:(s + 1) * P], Q2[q][h][:, :],
                                                 start=False, stop=True)
                            last.then_inc(st_done, 1)
                        elif what == "PV":
                            if n == 0:
                                pe.wait_ge(o_copied, st.g + 1)
                            outputs(q, n, T + n, vb_now)
                        elif what == "PVlast":
                            outputs(1 - q, NKT - 1, T - 1, vb_last)
                        elif what == "den":
                            bank(what)
                            pe.wait_ge(acc_done, 7 * st.g + 7)
                            for h in range(2):
                                for qt in range(TPB):
                                    last = pe.matmul(pm[:, h * TPB + qt:h * TPB + qt + 1],
                                                     acc[:, 1 - q, h, qt * P:(qt + 1) * P], ones[:, 0:1],
                                                     start=True, stop=True)
                            last.then_inc(misc_done, 1)
                        elif what == "R":
                            bank(what)
                            pe.wait_ge(misc_read, use(st, "den"))
                            for h in range(2):
                                for qt in range(TPB):
                                    c8 = h * TPB + qt
                                    last = pe.matmul(pm[own[h], qt * P:(qt + 1) * P],
                                                     rc[:, 1 - q, c8:c8 + 1].to_broadcast([P, HD1]), ident[:, :],
                                                     start=True, stop=True)
                            last.then_inc(misc_done, 1)
                        elif what[0] == "Y":
                            i = int(what[1])
                            bank(what)
                            pe.wait_ge(ot_done, st.g + 2)
                            wo = Wo[:, bass.ds(4 * st.batch_half + st.off - 1, 1), :].rearrange("p a d -> p (a d)")
                            for t in range(2):
                                tt = 2 * i + t
                                last = pe.matmul(pm[:, t * D:(t + 1) * D], OT[:, 1 - q, tt * P:(tt + 1) * P], wo,
                                                 start=True, stop=True)
                            last.then_inc(misc_done, 1)
                for_steps(pe, emit)

            @block.scalar
            def _(act):
                for k in range(2):
                    act.copy(ahead[:, k:k + 1], ident[:, 0:1]).then_inc(exp_done, 1)
                act.copy(ahead[:, 2:3], ident[:, 0:1]).then_inc(o_copied, 1)

                def emit(st):
                    first = isinstance(st.g, int) and st.g == -1
                    j, gp, by2 = pair(st)
                    q = st.parity
                    for what, n in order(st):
                        if what in ("K0", "K1"):
                            i = int(what[1])
                            act.wait_ge(misc_done, use(st, what))
                            if not (isinstance(st.g, int) and st.g <= 0):
                                act.wait_ge(st_done, NKT * st.g)
                            for h in range(2):
                                act.copy(K1[j][h][own[h], i * S:(i + 1) * S], pm[own[h], :]).then_inc(k_hi, 1)
                        elif what == "Q":
                            act.wait_ge(misc_done, use(st, what))
                            for h in range(2):
                                act.mul(Q1[j][h][own[h], :], pm[own[h], :], SCALE1).then_inc(q_hi, 1)
                        elif what[0] == "V":
                            i = int(what[1])
                            vb = 0 if first else {1: 1, 3: 0}[st.off]
                            act.wait_ge(misc_done, use(st, what))
                            if not first:
                                act.wait_ge(pv_done, NKT * st.g + PT)
                            act.copy(V[vb][:, 2 * i:2 * i + 2, :].rearrange("p a n -> p (a n)"), pm[:, :]
                                     ).then_inc(misc_read, 1)
                        elif what == "M":
                            act.wait_ge(m_done, gp + 1)
                            for h in range(2):
                                act.copy(Q2[j][h][row0[h]:row0[h] + 1, :], pS[row0[h]:row0[h] + 1, 0, :]
                                         ).then_inc(m_copied, 1)
                        elif what == "ST":
                            T = NKT * st.g + n
                            act.wait_ge(st_done, T + 1)
                            act.wait_ge(pv_done, T + 1)
                            act.wait_ge(acc_done, 7 * st.g + 7 + (n - 3 if n < 4 else max(n - 4, 1)))
                            act.activation(pr[:, n % PT, :, :], pT[n % 2][:, :, :], ACT.Exp).then_inc(exp_done, 1)
                        elif what == "O":
                            act.wait_ge(pv_done, NKT * st.g + PT)
                            act.wait_ge(ot_done, st.g)
                            act.copy(osb[:, 1 - q, :], pO[:, :]).then_inc(o_copied, 1)
                        elif what == "R":
                            act.wait_ge(misc_done, use(st, what))
                            act.wait_ge(ot_done, st.g + 1)
                            act.copy(rb[:, :], pm[:, :]).then_inc(misc_read, 1)
                for_steps(act, emit)

            @block.vector
            def _(dve):
                for k in range(2):
                    dve.memset(ahead[:, 3 + k:4 + k], 0.0).then_inc(ot_done, 1)

                def emit(st):
                    j, gp, by2 = pair(st)
                    q = st.parity
                    for what, n in order(st):
                        if what in ("K0", "K1"):
                            i = int(what[1])
                            for h in range(2):
                                dve.wait_ge(k_hi, 4 * gp + 2 * i + h + 1)
                                ins = dve.tensor_tensor(K1[j][h][other[h], i * S:(i + 1) * S], pm[own[h], :],
                                                        K1[j][h][own[h], i * S:(i + 1) * S].bitcast(F32),
                                                        ALU.subtract)
                            ins.then_inc(misc_read, 1)
                        elif what == "Q":
                            for h in range(2):
                                dve.wait_ge(q_hi, 2 * gp + h + 1)
                                ins = dve.scalar_tensor_tensor(Q2[j][h][own[h], :], pm[own[h], :], SCALE1,
                                                               Q1[j][h][own[h], :].bitcast(F32), ALU.mult,
                                                               ALU.subtract)
                            ins.then_inc(misc_read, 1)
                        elif what == "S":
                            dve.wait_ge(s_done, 8 * gp + n + 1)
                            dve.tensor_reduce(nm[:, j, n:n + 1], pS[:, :, :].rearrange("p m n -> p (m n)"), AX.X,
                                              ALU.max, negate=True).then_inc(max_done, 1)
                        elif what == "den":
                            dve.wait_ge(misc_done, use(st, what))
                            dve.reciprocal(rc[:, 1 - q, :], pm[:, 0:8]).then_inc(misc_read, 1)
                        elif what == "R":
                            dve.wait_ge(misc_read, use(st, what))
                            dve.wait_ge(o_copied, st.g + 1)
                            dve.tensor_tensor(OT[:, 1 - q, :], osb[:, 1 - q, :], rb[:, :], ALU.mult
                                              ).then_inc(ot_done, 1)
                        elif what[0] == "Y":
                            i = int(what[1])
                            dve.wait_ge(misc_done, use(st, what))
                            r = res[:, bass.ds(TPB * st.b + 2 * i, 2), :]
                            dve.tensor_tensor(r, r, pm[:, :].rearrange("p (t d) -> p t d", d=D), ALU.add
                                              ).then_inc(misc_read, 1)
                for_steps(dve, emit)

            @block.gpsimd
            def _(pool):
                for j in range(2):
                    for h in range(2):
                        for b_ in (K2, Q0, Q2):
                            pool.memset(b_[j][h][:, :].bitcast(F32), 0.0).then_inc(set_up, 1)
                pool.memset(onerow[:, :].bitcast(F32), 1.0).then_inc(set_up, 1)
                pool.memset(ones[:, :], 1.0).then_inc(set_up, 1)
                pool.memset(ahead[:, 6:7], 0.0).then_inc(pv_done, PT)
                pool.memset(ahead[:, 7:8], 0.0).then_inc(acc_done, 7)

                def emit(st):
                    if isinstance(st.g, int) and st.g in (-1, NSTEP):
                        return
                    q = st.parity
                    for s in range(1, NKT):
                        T = NKT * st.g + s
                        pool.wait_ge(exp_done, T + 1 + 2)
                        if s == 1:
                            if not (isinstance(st.g, int) and st.g < 2):
                                prev = Step(st.g - 1, 1 - q, None)
                                pool.wait_ge(misc_done, use(prev, "den"))
                            a = pr[:, 0, :, :]
                        else:
                            pool.wait_ge(acc_done, 7 * st.g + s - 1 + 7)
                            a = acc[:, q, :, :]
                        pool.tensor_tensor(acc[:, q, :, :], a, pr[:, s % PT, :, :], ALU.add).then_inc(acc_done, 1)
                for_steps(pool, emit)


def layer1_attention(nc, io, res, ident):
    kv = nc.dram_tensor("kv_split", (B, P, 2, DC, KEYS), F32, kind="Internal").ap()
    wsp = nc.dram_tensor("w_split", (NQUAD, P, 2, 3, DC, 256), F32, kind="Internal").ap()
    mb = nc.dram_tensor("mask_bias", (B, KEYS), F32, kind="Internal").ap()
    layer1_keys_in(nc, io, res, ident, kv, wsp, mb)
    layer1_pairs(nc, io, res, ident, kv, wsp, mb)


PHASES = [layer0_attention, layer0_ffn, layer1_attention, layer1_ffn]


def network(nc, io, out):
    with ExitStack() as ctx:
        sb, ps, sem = scope(nc, ctx)
        res = sb("res", [P, NT, D])
        ident = sb("ident", [P, P])
        id_ready = sem("id_ready")
        stored = sem("stored")
        with nc.Block() as block:
            @block.gpsimd
            def _(pool):
                pool.memset(ident[:, :], 0.0).then_inc(id_ready, 1)
                pool.wait_ge(id_ready, 1)
                pool.affine_select(out=ident[:, :], in_=ident[:, :], compare_op=ALU.not_equal, fill=1.0, base=0,
                                   pattern=[[-1, P]], channel_multiplier=1).then_inc(id_ready, 1)
        for phase in PHASES:
            phase(nc, io, res, ident)
        with nc.Block() as block:
            @block.sync
            def _(sp):
                sp.dma_start(out.rearrange("b (t p) d -> p (b t) d", p=P), res[:, :, :]).then_inc(stored, 16)
                sp.wait_ge(stored, 16)


def _rows(a):
    return a.reshape(-1, P, a.shape[-1]).transpose(1, 0, 2)


def _gate_up(np, parts):
    out = []
    for ws in parts:
        w = np.concatenate(ws).transpose(0, 2, 1)
        out.append(w.reshape(w.shape[0], DC, P, -1).transpose(0, 2, 1, 3).reshape(w.shape[0], P, -1))
    return np.concatenate(out, axis=2)


def _widths(w):
    return w.reshape(D, NS1, F1).transpose(1, 2, 0)


def laid_out(np, a):
    z = {"x": a["x"], "ctx": a["ctx_1024"]}
    for n in "qkvo":
        z[f"w{n}0"] = _rows(a[f"L0_xattn_W{n}"].T)
    for n in "qkv":
        z[f"b{n}0"] = a[f"L0_xattn_b{n}"].reshape(DC, P).T
    z["bo0"] = a["L0_xattn_bo"]
    z["ebias"] = a["L0_ffn_e_bias"]
    z["m0_gate"] = _rows(a["L0_ffn_gate_w"].T)
    z["e0_gu"] = _gate_up(np, [[a["L0_ffn_gate_proj"], a["L0_ffn_shared_gate_w"][None]],
                               [a["L0_ffn_up_proj"], a["L0_ffn_shared_up_w"][None]]])
    z["e0_d"] = np.concatenate([a["L0_ffn_down_proj"], a["L0_ffn_shared_down_w"][None]]).transpose(0, 2, 1)
    for n in "kvq":
        z[f"w{n}1"] = _rows(a[f"L1_xattn_W{n}"])
    z["wo1"] = _rows(a["L1_xattn_Wo"])
    z["gb1"] = np.stack([np.stack([a[f"L1_xattn_{p}{m}"].reshape(DC, P) for p in "gb"]) for m in "ml"]
                        ).transpose(3, 0, 1, 2)
    z["mask"] = a["mask_BxS2_bf1"].view(np.uint8)
    z["m1_gate"] = _rows(a["L1_ffn_gate_w"].T)
    z["e1_gu"] = _gate_up(np, [[a["L1_ffn_w_gate"].transpose(0, 2, 1), _widths(a["L1_ffn_sw_gate"])],
                               [a["L1_ffn_w_up"].transpose(0, 2, 1), _widths(a["L1_ffn_sw_up"])]])
    z["e1_d"] = np.concatenate([a["L1_ffn_w_down"], a["L1_ffn_sw_down"].reshape(NS1, F1, D)])
    return {k: np.ascontiguousarray(v) for k, v in z.items()}


def kernel(**inputs):
    import numpy as _np
    import concourse.bacc as _bacc
    from concourse import mybir as _mybir
    from concourse.bass_utils import run_bass_kernel_spmd as _run

    nc = _bacc.Bacc("TRN2", target_bir_lowering=False, num_devices=1)
    arrays, io = {}, {}
    for name, a in laid_out(_np, {k: _np.asarray(v) for k, v in inputs.items()}).items():
        arrays[f"in_{name}_dram"] = a
        io[name] = nc.dram_tensor(f"in_{name}_dram", a.shape, _mybir.dt.from_np(a.dtype), kind="ExternalInput").ap()
    out = nc.dram_tensor("out_0_dram", (B, S, D), F32, kind="ExternalOutput").ap()
    network(nc, io, out)
    r = _run(nc, [arrays], core_ids=[0])
    return r.results[0]["out_0_dram"]
```

```python
from contextlib import ExitStack

import concourse.bass as bass
from concourse import mybir

P = 128
B, S, D = 8, 512, 256
TPB = S // P
NT = B * TPB
DC = D // P
EPS = 1e-5

H0 = 16
HD0 = D // H0
STRIDE = 16
KPH = S // STRIDE
SCALE0 = HD0 ** -0.5

E0, G0, I0 = 16, 4, 128
PG0 = E0 // G0
TOPG0, TOPK0 = 2, 4
N0 = E0 + 1

H1, HD1 = 16, 64
INNER = H1 * HD1
KEYS = 2 * S
NKT = KEYS // P
SCALE1 = HD1 ** -0.5
NPAIR = H1 // 2
NQUAD = H1 // 4
MASKED = 1.0e30

E1, F1, NS1 = 8, 352, 2
TOPK1 = 2
N1 = E1 + NS1
FCH1 = [(0, 128), (128, 128), (256, 96)]
ROUTE_SCALE = 2.5

F32 = mybir.dt.float32
F32R = mybir.dt.float32r
U8 = mybir.dt.uint8
ALU = mybir.AluOpType
ACT = mybir.ActivationFunctionType
AX = mybir.AxisListType

HI, LO = 0, 1
PASSES = [(LO, HI), (HI, LO), (HI, HI)]


class Counted:

    def __init__(self, sem, base=0):
        self.sem, self.base, self.n = sem, base, 0

    def done(self, instruction, by=1):
        instruction.then_inc(self.sem, by)
        self.n += by
        return self.base + self.n

    def now(self):
        return self.base + self.n


def scope(nc, ctx):
    def sb(name, shape, dt=F32):
        return ctx.enter_context(nc.sbuf_tensor(name, shape, dt))

    def ps(name, shape, dt=F32):
        return ctx.enter_context(nc.psum_tensor(name, shape, dt))

    def sem(name):
        return ctx.enter_context(nc.semaphore(name))

    return sb, ps, sem


def ln_sems(sem, tag):
    return {n: sem(f"{tag}_{n}") for n in ("stats", "cleared", "moments", "var", "sd", "rstd", "xhat")}


LN_STATS, LN_ONE = TPB, 1


def ln_vector(dve, s, n, src, st, mv, ve, rs, dst):
    for t in range(TPB):
        dve.bn_stats(st[:, t, :], src(t)).then_inc(s["stats"], 1)
    dve.wait_ge(s["stats"], n * TPB + TPB)
    dve.memset(ve[:, :], 0.0).then_inc(s["cleared"], 1)
    for t in range(TPB):
        dve.bn_aggr(mv[:, t, :], st[:, t, :]).then_inc(s["moments"], 1)
    dve.wait_ge(s["moments"], n * TPB + TPB)
    dve.wait_ge(s["cleared"], n + 1)
    dve.tensor_scalar(ve[:, :], mv[:, :, 1], EPS, None, ALU.add).then_inc(s["var"], 1)
    dve.wait_ge(s["sd"], n + 1)
    dve.reciprocal(rs[:, :], ve[:, :]).then_inc(s["rstd"], 1)
    dve.wait_ge(s["rstd"], n + 1)
    for t in range(TPB):
        dve.tensor_scalar(dst(t), src(t), mv[:, t, 0:1], rs[:, t:t + 1], ALU.subtract,
                          ALU.mult).then_inc(s["xhat"], 1)


def ln_scalar(act, s, n, ve):
    act.wait_ge(s["var"], n + 1)
    act.activation(ve[:, :], ve[:, :], ACT.Sqrt).then_inc(s["sd"], 1)


def layer0_attention(nc, io, res, ident):
    with ExitStack() as ctx:
        sb, ps, sem = scope(nc, ctx)
        xT = sb("a_xT", [P, DC, B * S])
        cT = sb("a_cT", [P, DC, B * S])

        with ExitStack() as inner:
            sb1, ps1, sem1 = scope(nc, inner)
            cin = sb1("a_cin", [P, 2, TPB, D])
            xh = sb1("a_xh", [P, 2, TPB, D])
            ahead = sb1("a_ahead", [P, 4])
            st = sb1("a_st", [P, TPB, 6])
            mv = sb1("a_mv", [P, TPB, 2])
            ve = sb1("a_ve", [P, TPB])
            rs = sb1("a_rs", [P, TPB])
            px = [ps1(f"a_px{k}", [P, DC, S]) for k in range(2)]
            pc = [ps1(f"a_pc{k}", [P, DC, S]) for k in range(2)]
            x_in = [sem1(f"a_x_in{k}") for k in range(2)]
            c_in = [sem1(f"a_c_in{k}") for k in range(2)]
            ls = ln_sems(sem1, "a")
            x_turned, c_turned, x_out, c_out = (sem1(f"a_{n}") for n in ("x_turned", "c_turned", "x_out", "c_out"))

            with nc.Block() as block:
                @block.sync
                def _(sp):
                    with sp.Fori(0, B // 2) as i:
                        for k in range(2):
                            b = 2 * i + k
                            sp.wait_ge(x_out, b + 1)
                            sp.dma_start(res[:, bass.ds(b * TPB, TPB), :],
                                         io["x"][bass.ds(b, 1)].rearrange("b (t p) d -> p (b t) d", p=P)
                                         ).then_inc(x_in[k], 16)

                @block.gpsimd
                def _(pool):
                    with pool.Fori(0, B // 2) as i:
                        for k in range(2):
                            b = 2 * i + k
                            pool.wait_ge(c_out, b + 1)
                            for t in range(TPB):
                                hpt = P // KPH
                                pool.dma_start(cin[:, k, t, :],
                                               io["ctx"][bass.ds(b, 1)].rearrange(
                                                   "b (j h) d -> (b h) j d", h=STRIDE)[t * hpt:(t + 1) * hpt]
                                               ).then_inc(c_in[k], 16)

                @block.vector
                def _(dve):
                    for k in range(2):
                        dve.memset(ahead[:, k:k + 1], 0.0).then_inc(x_out, 1)
                    with dve.Fori(0, B // 2) as i:
                        for k in range(2):
                            b = 2 * i + k
                            dve.wait_ge(x_in[k], 16 * i + 16)
                            ln_vector(dve, ls, b, lambda t: res[:, bass.ds(b * TPB + t, 1), :].rearrange(
                                "p a d -> p (a d)"), st, mv, ve, rs, lambda t: xh[:, k, t, :])
                            dve.wait_ge(x_turned, b + 1)
                            dve.tensor_copy(xT[:, :, bass.ds(b * S, S)], px[k][:, :, :]).then_inc(x_out, 1)

                @block.scalar
                def _(act):
                    for k in range(2):
                        act.copy(ahead[:, 2 + k:3 + k], ident[:, 0:1]).then_inc(c_out, 1)
                    with act.Fori(0, B // 2) as i:
                        for k in range(2):
                            b = 2 * i + k
                            ln_scalar(act, ls, b, ve)
                            act.wait_ge(c_turned, b + 1)
                            act.copy(cT[:, :, bass.ds(b * S, S)], pc[k][:, :, :]).then_inc(c_out, 1)

                @block.tensor
                def _(pe):
                    with pe.Fori(0, B // 2) as i:
                        for k in range(2):
                            b = 2 * i + k
                            pe.wait_ge(c_in[k], 16 * TPB * (i + 1))
                            pe.wait_ge(c_out, b + 1)
                            for t in range(TPB):
                                for c in range(DC):
                                    last = pe.transpose(pc[k][:, c, t * P:(t + 1) * P],
                                                        cin[:, k, t, c * P:(c + 1) * P], ident[:, :])
                            last.then_inc(c_turned, 1)
                            pe.wait_ge(ls["xhat"], TPB * (b + 1))
                            pe.wait_ge(x_out, b + 1)
                            for t in range(TPB):
                                for c in range(DC):
                                    last = pe.transpose(px[k][:, c, t * P:(t + 1) * P],
                                                        xh[:, k, t, c * P:(c + 1) * P], ident[:, :])
                            last.then_inc(x_turned, 1)

        with ExitStack() as inner:
            sb2, ps2, sem2 = scope(nc, inner)
            w = {n: sb2(f"a_w{n}", [P, DC, D]) for n in "qkvo"}
            bias = {n: sb2(f"a_b{n}", [P, DC]) for n in "qkv"}
            bo = sb2("a_bo", [P, D])
            own = sb2("a_own", [P, S // 2])
            KT = sb2("a_KT", [P, DC, S // 2])
            VT = sb2("a_VT", [P, DC, S // 2])
            QT = sb2("a_QT", [P, DC, S])
            Vk = sb2("a_Vk", [P, 4, P])
            sc = sb2("a_sc", [P, 2, S])
            pr = sb2("a_pr", [P, 2, S])
            PT = sb2("a_PT", [P, 4, S])
            OT = sb2("a_OT", [P, DC, S])
            mx = sb2("a_mx", [P, 2, H0])
            sm = sb2("a_sm", [P, 2, H0])
            rc = sb2("a_rc", [P, 2, H0])
            yb = sb2("a_yb", [P, 2 * D])
            ahead = sb2("a_ahead2", [P, 8])
            pKV = ps2("a_pKV", [P, 2, S])
            pQ = ps2("a_pQ", [P, DC, S])
            pS = ps2("a_pS", [P, 2, S])
            pT = ps2("a_pT", [P, 2, S])
            names = ("w_in own_ready kv_done kv_used q_done q_ready v_ready vk_turned vk_ready s_done max_ready "
                     "shifted exp_ready sum_ready rcp_ready probs_ready p_turned p_used pv_done o_ready y_done "
                     "y_biased y_added").split()
            (w_in, own_ready, kv_done, k_ready, q_done, q_ready, v_ready, vk_turned, vk_ready, s_done, max_ready,
             shifted, exp_ready, sum_ready, rcp_ready, probs_ready, p_turned, p_ready, pv_done, o_ready, y_done,
             y_biased, y_added) = (sem2("a_" + n) for n in names)

            with nc.Block() as block:
                @block.sync
                def _(sp):
                    for n in "qkvo":
                        sp.dma_start(w[n][:, :, :], io[f"w{n}0"]).then_inc(w_in, 16)
                    for n in "qkv":
                        sp.dma_start(bias[n][:, :], io[f"b{n}0"]).then_inc(w_in, 16)
                    sp.dma_start(bo[:, :], io["bo0"].partition_broadcast(P)).then_inc(w_in, 16)

                @block.gpsimd
                def _(pool):
                    for k, (free, n) in enumerate(((v_ready, 2), (o_ready, 2), (y_added, 2), (p_ready, 1),
                                                   (shifted, 1), (s_done, 1), (vk_turned, 1), (pv_done, 1))):
                        pool.memset(ahead[:, k:k + 1], 0.0).then_inc(free, n)
                    pool.memset(own[:, :], 1.0).then_inc(own_ready, 1)
                    pool.wait_ge(own_ready, 1)
                    v = own[:, :].rearrange("p (h j) -> p h j", j=KPH)
                    pool.affine_select(out=v, in_=v, compare_op=ALU.is_ge, fill=0.0, base=0,
                                       pattern=[[-HD0, H0 // 2], [0, KPH]], channel_multiplier=1).then_inc(own_ready, 1)
                    pool.wait_ge(own_ready, 2)
                    pool.affine_select(out=v, in_=v, compare_op=ALU.is_ge, fill=0.0, base=HD0 - 1,
                                       pattern=[[HD0, H0 // 2], [0, KPH]], channel_multiplier=-1).then_inc(own_ready, 1)

                @block.tensor
                def _(pe):
                    pe.wait_ge(w_in, 128)
                    with pe.Fori(0, B) as b:
                        pe.wait_ge(v_ready, b * 2 + 2)
                        for m, n in enumerate("kv"):
                            for c in range(DC):
                                for k in range(DC):
                                    last = pe.matmul(pKV[:, m, c * 256:(c + 1) * 256],
                                                     w[n][:, k, c * P:(c + 1) * P],
                                                     cT[:, k, bass.ds(b * S + c * 256, 256)],
                                                     start=(k == 0), stop=(k == DC - 1))
                            last.then_inc(kv_done, 1)
                        pe.wait_ge(o_ready, b * 2 + 2)
                        for c in range(DC):
                            for k in range(DC):
                                last = pe.matmul(pQ[:, c, :], w["q"][:, k, c * P:(c + 1) * P],
                                                 xT[:, k, bass.ds(b * S, S)], start=(k == 0), stop=(k == DC - 1))
                            last.then_inc(q_done, 1)
                        pe.wait_ge(v_ready, b * 2 + 4)
                        pe.wait_ge(p_ready, b * TPB + 1)
                        for kc in range(4):
                            last = pe.transpose(pT[:, 0, kc * P:(kc + 1) * P],
                                                VT[:, kc // 2, (kc % 2) * P:(kc % 2 + 1) * P], ident[:, :])
                        last.then_inc(vk_turned, 1)

                        def scores(qt):
                            if qt == 0:
                                pe.wait_ge(k_ready, b * 2 + 2)
                                pe.wait_ge(q_ready, b * 2 + 2)
                                pe.wait_ge(y_added, b * 2 + 2)
                            else:
                                pe.wait_ge(shifted, b * TPB + qt)
                            for c in range(DC):
                                last = pe.matmul(pS[:, qt % 2, c * 256:(c + 1) * 256],
                                                 QT[:, c, qt * P:(qt + 1) * P], KT[:, c, :], start=True, stop=True)
                            last.then_inc(s_done, 1)

                        scores(0)
                        scores(1)
                        for qt in range(TPB):
                            pe.wait_ge(probs_ready, b * TPB + qt + 1)
                            if qt == 0:
                                pe.wait_ge(vk_ready, b + 1)
                            else:
                                pe.wait_ge(p_ready, b * TPB + qt)
                            for kc in range(4):
                                last = pe.transpose(pT[:, (qt + 1) % 2, kc * P:(kc + 1) * P],
                                                    pr[:, qt % 2, kc * P:(kc + 1) * P], ident[:, :])
                            last.then_inc(p_turned, 1)
                            if qt + 2 < TPB:
                                scores(qt + 2)
                        pe.wait_ge(p_ready, b * TPB + TPB + 1)
                        for c in range(DC):
                            for j in range(2):
                                last = pe.matmul(pQ[:, c, :], Vk[:, 2 * c + j, :], PT[:, 2 * c + j, :],
                                                 start=(j == 0), stop=(j == 1))
                            last.then_inc(pv_done, 1)
                        pe.wait_ge(o_ready, b * 2 + 4)
                        pe.wait_ge(shifted, b * TPB + TPB + 1)
                        for t in range(TPB):
                            for c in range(DC):
                                last = pe.matmul(pS[:, t // 2, (t % 2) * D:(t % 2 + 1) * D],
                                                 OT[:, c, t * P:(t + 1) * P], w["o"][:, c, :],
                                                 start=(c == 0), stop=(c == DC - 1))
                            if t % 2:
                                last.then_inc(y_done, 1)

                @block.vector
                def _(dve):
                    dve.wait_ge(w_in, 128)
                    dve.wait_ge(own_ready, 3)
                    with dve.Fori(0, B) as b:
                        for m, (n, out, ready) in enumerate((("k", KT, k_ready), ("v", VT, v_ready))):
                            dve.wait_ge(kv_done, 2 * b + m + 1)
                            if m == 0:
                                dve.wait_ge(s_done, b * TPB + 1)
                            else:
                                dve.wait_ge(vk_turned, b + 1)
                            for c in range(DC):
                                dve.scalar_tensor_tensor(out[:, c, :], pKV[:, m, c * 256:(c + 1) * 256],
                                                         bias[n][:, c:c + 1], own[:, :], ALU.add,
                                                         ALU.mult).then_inc(ready, 1)
                        for c in range(DC):
                            dve.wait_ge(q_done, 2 * b + c + 1)
                            dve.tensor_scalar(QT[:, c, :], pQ[:, c, :], bias["q"][:, c:c + 1], SCALE0, ALU.add,
                                              ALU.mult).then_inc(q_ready, 1)
                        for qt in range(TPB):
                            n = b * TPB + qt + 1
                            k = qt % 2

                            def heads(a):
                                return a.rearrange("p (h j) -> p h j", j=KPH)

                            def each(a):
                                return a.rearrange("p (h o) -> p h o", o=1).to_broadcast([P, H0, KPH])

                            dve.wait_ge(s_done, n + 1)
                            dve.tensor_reduce(mx[:, k, :], heads(pS[:, k, :]), AX.X, ALU.max).then_inc(max_ready, 1)
                            dve.wait_ge(max_ready, n)
                            if qt >= 2:
                                dve.wait_ge(exp_ready, n - 2)
                            dve.tensor_tensor(heads(sc[:, k, :]), heads(pS[:, k, :]), each(mx[:, k, :]),
                                              ALU.subtract).then_inc(shifted, 1)
                            dve.wait_ge(exp_ready, n)
                            dve.tensor_reduce(sm[:, k, :], heads(sc[:, k, :]), AX.X, ALU.add).then_inc(sum_ready, 1)
                            dve.wait_ge(sum_ready, n)
                            dve.reciprocal(rc[:, k, :], sm[:, k, :]).then_inc(rcp_ready, 1)
                            dve.wait_ge(rcp_ready, n)
                            if qt >= 2:
                                dve.wait_ge(p_turned, n - 2)
                            dve.tensor_tensor(heads(pr[:, k, :]), heads(sc[:, k, :]), each(rc[:, k, :]),
                                              ALU.mult).then_inc(probs_ready, 1)
                        for c in range(DC):
                            dve.wait_ge(pv_done, 2 * b + c + 2)
                            dve.tensor_copy(OT[:, c, :], pQ[:, c, :]).then_inc(o_ready, 1)
                        for m in range(2):
                            dve.wait_ge(y_done, 2 * b + m + 1)
                            dve.tensor_tensor(yb[:, :].rearrange("p (t d) -> p t d", d=D),
                                              pS[:, m, :].rearrange("p (t d) -> p t d", d=D),
                                              bo[:, :].rearrange("p (o d) -> p o d", o=1).to_broadcast([P, 2, D]),
                                              ALU.add).then_inc(y_biased, 1)
                            dve.wait_ge(y_biased, 2 * b + m + 1)
                            r = res[:, bass.ds(b * TPB + 2 * m, 2), :]
                            dve.tensor_tensor(r, r, yb[:, :].rearrange("p (t d) -> p t d", d=D),
                                              ALU.add).then_inc(y_added, 1)
                            dve.wait_ge(y_added, 2 * b + m + 3)

                @block.scalar
                def _(act):
                    with act.Fori(0, B) as b:
                        act.wait_ge(vk_turned, b + 2)
                        act.wait_ge(pv_done, 2 * b + 1)
                        act.copy(Vk[:, :, :].rearrange("p a d -> p (a d)"), pT[:, 0, :]).then_inc(vk_ready, 1)
                        for qt in range(TPB):
                            n = b * TPB + qt + 1
                            k = qt % 2
                            act.wait_ge(shifted, n + 1)
                            act.activation(sc[:, k, :], sc[:, k, :], ACT.Exp).then_inc(exp_ready, 1)
                            act.wait_ge(p_turned, n)
                            act.copy(PT[:, :, qt * P:(qt + 1) * P],
                                     pT[:, (qt + 1) % 2, :].rearrange("p (a q) -> p a q", q=P)).then_inc(p_ready, 1)


def moe_routes(nc, io, res, ident, XH, Wt, tag, E, route):
    with ExitStack() as ctx:
        sb, ps, sem = scope(nc, ctx)
        xh = sb(f"{tag}_xh", [P, 2, TPB, D])
        xs = sb(f"{tag}_xs", [P, 2, DC, S])
        gate = sb(f"{tag}_gate", [P, DC, E])
        st = sb(f"{tag}_st", [P, TPB, 6])
        mv = sb(f"{tag}_mv", [P, TPB, 2])
        ve = sb(f"{tag}_ve", [P, TPB])
        rs = sb(f"{tag}_rs", [P, TPB])
        ahead = sb(f"{tag}_ahead", [P, 4])
        px = [ps(f"{tag}_px{k}", [P, DC, S]) for k in range(2)]
        pl = ps(f"{tag}_pl", [P, NT, E])
        ls = ln_sems(sem, tag)
        gate_in, turned, x_copied, hi_done, lo_done, logits_done = (
            sem(f"{tag}_{n}") for n in ("gate_in", "turned", "x_copied", "hi_done", "lo_done", "logits_done"))
        r = route(nc, io, sb, sem, pl, Wt, logits_done, tag)

        with nc.Block() as block:
            @block.sync
            def _(sp):
                sp.dma_start(gate[:, :, :], io[f"{tag}_gate"]).then_inc(gate_in, 16)
                r["sync"](sp)

            @block.vector
            def _(dve):
                with dve.Fori(0, B // 2) as i:
                    for k in range(2):
                        b = 2 * i + k
                        ln_vector(dve, ls, b, lambda t: res[:, bass.ds(b * TPB + t, 1), :].rearrange(
                            "p a d -> p (a d)"), st, mv, ve, rs, lambda t: xh[:, k, t, :])
                        dve.wait_ge(x_copied, b + 3)
                        dve.tensor_copy(XH[:, HI, :, bass.ds(b * S, S)], xs[:, k, :, :]).then_inc(hi_done, 1)
                r["vector"](dve)

            @block.gpsimd
            def _(pool):
                for k in range(2):
                    pool.memset(ahead[:, k:k + 1], 0.0).then_inc(lo_done, 1)
                with pool.Fori(0, B // 2) as i:
                    for k in range(2):
                        b = 2 * i + k
                        pool.wait_ge(hi_done, b + 1)
                        for c in range(DC):
                            ins = pool.tensor_tensor(XH[:, LO, c, bass.ds(b * S, S)], xs[:, k, c, :],
                                                     XH[:, HI, c, bass.ds(b * S, S)].bitcast(F32), ALU.subtract)
                        ins.then_inc(lo_done, 1)
                r["gpsimd"](pool)

            @block.scalar
            def _(act):
                for k in range(2):
                    act.copy(ahead[:, 2 + k:3 + k], ident[:, 0:1]).then_inc(x_copied, 1)
                with act.Fori(0, B // 2) as i:
                    for k in range(2):
                        b = 2 * i + k
                        ln_scalar(act, ls, b, ve)
                        act.wait_ge(turned, b + 1)
                        act.wait_ge(lo_done, b + 1)
                        act.wait_ge(logits_done, b + 1)
                        act.copy(xs[:, k, :, :], px[k][:, :, :]).then_inc(x_copied, 1)
                r["scalar"](act)

            @block.tensor
            def _(pe):
                pe.wait_ge(gate_in, 16)
                for k in range(2):
                    pe.matmul(px[k][0:E, 0, 0:E], gate[:, 0, :], gate[:, 0, :], start=True,
                              stop=True).then_inc(logits_done, 1)
                pe.wait_ge(logits_done, 2)
                with pe.Fori(0, B // 2) as i:
                    for k in range(2):
                        b = 2 * i + k
                        pe.wait_ge(ls["xhat"], TPB * (b + 1))
                        pe.wait_ge(x_copied, b + 1)
                        for t in range(TPB):
                            for c in range(DC):
                                last = pe.transpose(px[k][:, c, t * P:(t + 1) * P],
                                                    xh[:, k, t, c * P:(c + 1) * P], ident[:, :])
                        last.then_inc(turned, 1)
                        pe.wait_ge(x_copied, b + 3)
                        for t in range(TPB):
                            for c in range(DC):
                                last = pe.matmul(pl[:, bass.ds(b * TPB + t, 1), :], xs[:, k, c, t * P:(t + 1) * P],
                                                 gate[:, c, :], start=(c == 0), stop=(c == DC - 1))
                        last.then_inc(logits_done, 1)


def over(a, n, axis):
    if axis == "last":
        return a.rearrange("p (m o) -> p m o", o=1).to_broadcast([P, a.shape[1], n])
    return a.rearrange("p (o m) -> p o m", o=1).to_broadcast([P, n, a.shape[1]])


def chosen(dve, c, v, G, E, top, before, wins, ties, rank, sel):
    a = v.rearrange("p (m o) -> p m o", o=1).to_broadcast([P, G * E, E])
    o = [x[:, 0:G * E * E].rearrange("p (m e) -> p m e", e=E) for x in (wins, ties)]
    for g0 in range(0, G, NT):
        pass
    w4 = [x[:, 0:G * E * E].rearrange("p (g e f) -> p g e f", e=E, f=E) for x in (wins, ties)]
    b4 = v.rearrange("p (g o f) -> p g o f", o=1, f=E).to_broadcast([P, G, E, E])
    a4 = v.rearrange("p (g e o) -> p g e o", e=E, o=1).to_broadcast([P, G, E, E])
    c.done(dve.tensor_tensor(w4[0], b4, a4, ALU.is_gt))
    n = c.done(dve.tensor_tensor(w4[1], b4, a4, ALU.is_equal))
    dve.wait_ge(c.sem, n)
    bf = before[:, 0:E, 0:E].rearrange("p (o e) f -> p o e f", o=1).to_broadcast([P, G, E, E])
    n = c.done(dve.tensor_tensor(w4[1], w4[1], bf, ALU.mult))
    dve.wait_ge(c.sem, n)
    n = c.done(dve.tensor_tensor(wins[:, 0:G * E * E], wins[:, 0:G * E * E], ties[:, 0:G * E * E], ALU.add))
    dve.wait_ge(c.sem, n)
    n = c.done(dve.tensor_reduce(rank, o[0], AX.X, ALU.add))
    dve.wait_ge(c.sem, n)
    n = c.done(dve.tensor_scalar(sel, rank, float(top), None, ALU.is_lt))
    dve.wait_ge(c.sem, n)


def weigh(dve, c, scores, sel, E, tot, Wt, shared):
    n = c.done(dve.tensor_tensor(sel, scores, sel, ALU.mult))
    dve.wait_ge(c.sem, n)
    n = c.done(dve.tensor_reduce(tot, sel.rearrange("p (t e) -> p t e", e=E), AX.X, ALU.add))
    dve.wait_ge(c.sem, n)
    n = c.done(dve.tensor_scalar(tot, tot, 1e-20, None, ALU.add))
    dve.wait_ge(c.sem, n)
    n = c.done(dve.reciprocal(tot, tot))
    dve.wait_ge(c.sem, n)
    n = c.done(dve.tensor_scalar(tot, tot, ROUTE_SCALE, None, ALU.mult))
    dve.wait_ge(c.sem, n)
    c.done(dve.memset(Wt[:, :, E:E + shared], 1.0))
    n = c.done(dve.tensor_tensor(Wt[:, :, 0:E], sel.rearrange("p (t e) -> p t e", e=E), over(tot, E, "last"),
                                 ALU.mult))
    dve.wait_ge(c.sem, n)


def make_before(pool, before, E, s):
    pool.memset(before[:, :, :], 1.0).then_inc(s, 1)
    pool.wait_ge(s, 1)
    pool.affine_select(out=before[:, :, :], in_=before[:, :, :], compare_op=ALU.is_ge, fill=0.0, base=-1,
                       pattern=[[1, E], [-1, E]], channel_multiplier=0).then_inc(s, 1)


def route0(nc, io, sb, sem, pl, Wt, logits_done, tag):
    sg, ch, sel, rank = (sb(f"{tag}_{n}", [P, NT * E0]) for n in ("sg", "ch", "sel", "rank"))
    pairs = sb(f"{tag}_pairs", [P, NT * G0, 6])
    gs, gsel, grank = (sb(f"{tag}_{n}", [P, NT * G0]) for n in ("gs", "gsel", "grank"))
    wins, ties = (sb(f"{tag}_{n}", [P, NT * E0 * E0]) for n in ("wins", "ties"))
    tot = sb(f"{tag}_tot", [P, NT])
    ebias = sb(f"{tag}_ebias", [P, E0])
    before = sb(f"{tag}_before", [P, E0, E0])
    bias_in, before_done, scored, steps = (sem(f"{tag}_{n}") for n in ("bias_in", "before_done", "scored", "steps"))

    def sync(sp):
        sp.dma_start(ebias[:, :], io["ebias"].partition_broadcast(P)).then_inc(bias_in, 16)

    def gpsimd(pool):
        make_before(pool, before, E0, before_done)

    def scalar(act):
        act.wait_ge(logits_done, B + 2)
        act.activation(sg[:, :], pl[:, :, :].rearrange("p t e -> p (t e)"), ACT.Sigmoid).then_inc(scored, 1)

    def vector(dve):
        c = Counted(steps)
        dve.wait_ge(scored, 1)
        dve.wait_ge(bias_in, 16)
        n = c.done(dve.tensor_tensor(ch[:, :].rearrange("p (t e) -> p t e", e=E0),
                                     sg[:, :].rearrange("p (t e) -> p t e", e=E0), over(ebias[:, :], NT, "ahead"),
                                     ALU.add))
        dve.wait_ge(c.sem, n)
        g = ch[:, :].rearrange("p (g e) -> p g e", e=PG0)
        c.done(dve.tensor_tensor(pairs[:, :, 0:3], g[:, :, 0:3], g[:, :, 1:4], ALU.add))
        c.done(dve.tensor_tensor(pairs[:, :, 3:5], g[:, :, 0:2], g[:, :, 2:4], ALU.add))
        n = c.done(dve.tensor_tensor(pairs[:, :, 5:6], g[:, :, 0:1], g[:, :, 3:4], ALU.add))
        dve.wait_ge(c.sem, n)
        n = c.done(dve.tensor_reduce(gs[:, :], pairs[:, :, :], AX.X, ALU.max))
        dve.wait_ge(c.sem, n)
        dve.wait_ge(before_done, 2)
        chosen(dve, c, gs[:, :], NT, G0, TOPG0, before, wins, ties, grank[:, :], gsel[:, :])
        n = c.done(dve.tensor_tensor(g, g, over(gsel[:, :], PG0, "last"), ALU.mult))
        dve.wait_ge(c.sem, n)
        chosen(dve, c, ch[:, :], NT, E0, TOPK0, before, wins, ties, rank[:, :], sel[:, :])
        weigh(dve, c, sg[:, :], sel[:, :], E0, tot[:, :], Wt, 1)

    return {"sync": sync, "gpsimd": gpsimd, "scalar": scalar, "vector": vector}


def moe_experts(nc, io, res, ident, XH, Wt, tag, NX, F):
    fch = [(f, min(P, F - f)) for f in range(0, F, P)]
    NF = len(fch)
    UPE = B * NF
    GU = 2 * DC * F
    whole = F // P
    nsplit = 2 if F % P else 1
    AHEAD = 2
    with ExitStack() as ctx:
        sb, ps, sem = scope(nc, ctx)
        raw_gu = sb(f"{tag}_raw_gu", [P, GU])
        raw_d = sb(f"{tag}_raw_d", [P, NF, D])
        Wgu = [sb(f"{tag}_Wgu{k}", [P, 2, GU], F32R) for k in range(2)]
        Wd = [sb(f"{tag}_Wd{k}", [P, 2, NF, D], F32R) for k in range(2)]
        sl = sb(f"{tag}_sl", [P, 2, S])
        hf = sb(f"{tag}_hf", [P, 2, S])
        hs = sb(f"{tag}_hs", [P, 2, 2, S], F32R)
        ahead = sb(f"{tag}_ahead", [P, 16])
        pG = [ps(f"{tag}_pG{k}", [P, S]) for k in range(2)]
        pU = [ps(f"{tag}_pU{k}", [P, S]) for k in range(2)]
        pY = [ps(f"{tag}_pY{k}", [P, TPB, D]) for k in range(2)]
        (raw_in, w_hi, w_lo, gu_done, silu_done, mult_done, hi_done, lo_done, d_done, added) = (
            sem(f"{tag}_{n}") for n in ("raw_in", "w_hi", "w_lo", "gu_done", "silu_done", "mult_done", "hi_done",
                                        "lo_done", "d_done", "added"))
        NW = 1 + nsplit
        LOADS = 2 + (nsplit - 1)

        def gu_view(w, g, k):
            return w[(g * DC + k) * F:(g * DC + k + 1) * F]

        def pieces(e2):
            k = e2 % 2
            yield Wgu[k][:, :, :], raw_gu[:, :], P
            if whole:
                yield (Wd[k][:, :, 0:whole, :].rearrange("p a f d -> p a (f d)"),
                       raw_d[:, 0:whole, :].rearrange("p f d -> p (f d)"), P)
            if F % P:
                yield Wd[k][0:F % P, :, whole, :], raw_d[0:F % P, whole, :], F % P

        def segments():
            tail = NX % 2 or 2
            return (NX - tail) // 2, tail

        loops, tail = segments()

        def for_units(eng, emit):
            with eng.Fori(0, loops) as i:
                for j in range(2):
                    for u in range(UPE):
                        emit(2 * i + j, j, u, False)
            for j in range(tail):
                for u in range(UPE):
                    emit(NX - tail + j, j, u, j == tail - 1 and u == UPE - 1)

        with nc.Block() as block:
            @block.sync
            def _(sp):
                def load(e, first=False):
                    if not first:
                        sp.wait_ge(w_lo, NW * e)
                    sp.dma_start(raw_gu[:, :], io[f"{tag}_gu"][bass.ds(e, 1)].rearrange("a p n -> (a p) n")
                                 ).then_inc(raw_in, 16)
                    if whole:
                        sp.dma_start(raw_d[:, 0:whole, :], io[f"{tag}_d"][bass.ds(e, 1), 0:whole * P].rearrange(
                            "a (f p) d -> p (a f) d", p=P)).then_inc(raw_in, 16)
                    if F % P:
                        sp.dma_start(raw_d[0:F % P, whole:whole + 1, :], io[f"{tag}_d"][
                            bass.ds(e, 1), whole * P:F].rearrange("a p d -> p a d")).then_inc(raw_in, 16)

                load(0, True)
                with sp.Fori(1, NX) as e:
                    load(e)

            def next_pair(e, j, u):
                return (e + 1, (j + 1) % 2, 0) if u == UPE - 1 else (e, j, u + 1)

            @block.tensor
            def _(pe):
                def gate_up(e, j, u):
                    n, f = divmod(u, NF)
                    f0, fw = fch[f]
                    U = e * UPE + u
                    if u == 0:
                        pe.wait_ge(w_lo, NW * (e + 1))
                    pe.wait_ge(mult_done, U + 1)
                    for g, out in enumerate((pG, pU)):
                        first = True
                        for k in range(DC):
                            for wp, xp in PASSES:
                                lhsT = Wgu[j][:, wp, (g * DC + k) * F + f0:(g * DC + k) * F + f0 + fw]
                                last = pe.matmul(out[u % 2][0:fw, :], lhsT, XH[:, xp, k, n * S:(n + 1) * S],
                                                 start=first, stop=(k == DC - 1 and (wp, xp) == PASSES[-1]))
                                first = False
                    last.then_inc(gu_done, 1)

                def down(e, j, u):
                    n, f = divmod(u, NF)
                    f0, fw = fch[f]
                    U = e * UPE + u
                    pe.wait_ge(lo_done, U + 1 + AHEAD)
                    if f == 0:
                        pe.wait_ge(added, TPB * (e * B + n) + TPB)
                    for t in range(TPB):
                        for m, (hp, wp) in enumerate(PASSES):
                            last = pe.matmul(pY[n % 2][:, t, :], hs[0:fw, u % 2, hp, t * P:(t + 1) * P],
                                             Wd[j][0:fw, wp, f, :],
                                             start=(f == 0 and m == 0 and t % 2 == 0),
                                             stop=(f == NF - 1 and m == len(PASSES) - 1),
                                             skip_group_check=True)
                    last.then_inc(d_done, 1)

                for k in range(2):
                    pe.matmul(pY[k][:, 0, 0:P], ident[:, :], ident[:, :], start=True, stop=True).then_inc(d_done, 1)
                pe.wait_ge(d_done, 2)
                gate_up(0, 0, 0)

                def emit(e, j, u, last):
                    if not last:
                        gate_up(*next_pair(e, j, u))
                    down(e, j, u)
                for_units(pe, emit)

            @block.scalar
            def _(act):
                def split(e, j):
                    act.wait_ge(raw_in, 16 * LOADS * (e + 1))
                    act.wait_ge(d_done, e * UPE - UPE + AHEAD if not isinstance(e, int) or e > 1 else AHEAD)
                    for out, raw, rows in pieces(j):
                        act.copy(out[:, HI, :], raw).then_inc(w_hi, 1)

                split(0, 0)

                def emit(e, j, u, last):
                    n, f = divmod(u, NF)
                    fw = fch[f][1]
                    U = e * UPE + u
                    act.wait_ge(gu_done, U + 1)
                    act.wait_ge(mult_done, U + 1)
                    act.activation(sl[0:fw, u % 2, :], pG[u % 2][0:fw, :], ACT.Silu).then_inc(silu_done, 1)
                    act.wait_ge(mult_done, U + 1 + AHEAD)
                    act.wait_ge(d_done, U + 1)
                    act.copy(hs[0:fw, u % 2, HI, :], hf[0:fw, u % 2, :]).then_inc(hi_done, 1)
                    if u == 1 and not (isinstance(e, int) and e == NX - 1):
                        split(e + 1, (j + 1) % 2)
                for_units(act, emit)

            @block.gpsimd
            def _(pool):
                for k in range(AHEAD):
                    pool.memset(ahead[:, k:k + 1], 0.0).then_inc(lo_done, 1)

                def split(e, j):
                    for m, (out, raw, rows) in enumerate(pieces(j)):
                        pool.wait_ge(w_hi, NW * e + m + 1)
                        pool.tensor_tensor(out[:, LO, :], raw, out[:, HI, :].bitcast(F32), ALU.subtract
                                           ).then_inc(w_lo, 1)

                split(0, 0)

                def emit(e, j, u, last):
                    n, f = divmod(u, NF)
                    fw = fch[f][1]
                    U = e * UPE + u
                    pool.wait_ge(hi_done, U + 1)
                    pool.tensor_tensor(hs[0:fw, u % 2, LO, :], hf[0:fw, u % 2, :],
                                       hs[0:fw, u % 2, HI, :].bitcast(F32), ALU.subtract).then_inc(lo_done, 1)
                    if u == 1 and not (isinstance(e, int) and e == NX - 1):
                        split(e + 1, (j + 1) % 2)
                for_units(pool, emit)

            @block.vector
            def _(dve):
                for k in range(AHEAD):
                    dve.memset(ahead[:, 2 + k:3 + k], 0.0).then_inc(mult_done, 1)
                for k in range(2 * TPB):
                    dve.memset(ahead[:, 4 + k:5 + k], 0.0).then_inc(added, 1)

                def mult(e, j, u):
                    n, f = divmod(u, NF)
                    fw = fch[f][1]
                    U = e * UPE + u
                    dve.wait_ge(silu_done, U + 1)
                    dve.wait_ge(lo_done, U + 1)
                    dve.tensor_tensor(hf[0:fw, u % 2, :], sl[0:fw, u % 2, :], pU[u % 2][0:fw, :], ALU.mult
                                      ).then_inc(mult_done, 1)

                def add(e, n):
                    dve.wait_ge(d_done, e * UPE + NF * (n + 1) + AHEAD)
                    dve.wait_ge(added, TPB * (e * B + n) + 2 * TPB)
                    for t in range(TPB):
                        tile = n * TPB + t
                        dve.scalar_tensor_tensor(res[:, tile, :], pY[n % 2][:, t, :], Wt[:, tile, bass.ds(e, 1)],
                                                 res[:, tile, :], ALU.mult, ALU.add).then_inc(added, 1)

                mult(0, 0, 0)

                def emit(e, j, u, last):
                    if not last:
                        mult(*next_pair(e, j, u))
                    if u % NF == NF - 1:
                        add(e, u // NF)
                for_units(dve, emit)


def layer0_ffn(nc, io, res, ident):
    with ExitStack() as ctx:
        sb, ps, sem = scope(nc, ctx)
        Wt = sb("m0_Wt", [P, NT, N0])
        XH = sb("m0_XH", [P, 2, DC, B * S], F32R)
        moe_routes(nc, io, res, ident, XH, Wt, "m0", E0, route0)
        moe_experts(nc, io, res, ident, XH, Wt, "e0", N0, I0)


def route1(nc, io, sb, sem, pl, Wt, logits_done, tag):
    lg, sel, rank = (sb(f"{tag}_{n}", [P, NT * E1]) for n in ("lg", "sel", "rank"))
    wins, ties = (sb(f"{tag}_{n}", [P, NT * E1 * E1]) for n in ("wins", "ties"))
    tot = sb(f"{tag}_tot", [P, NT])
    before = sb(f"{tag}_before", [P, E1, E1])
    before_done, shifted, exp_done, steps = (sem(f"{tag}_{n}") for n in ("before_done", "shifted", "exp_done", "steps"))

    def sync(sp):
        pass

    def gpsimd(pool):
        make_before(pool, before, E1, before_done)

    def scalar(act):
        act.wait_ge(shifted, 1)
        act.activation(lg[:, :], lg[:, :], ACT.Exp).then_inc(exp_done, 1)

    def vector(dve):
        c = Counted(steps)
        by_token = lg[:, :].rearrange("p (t e) -> p t e", e=E1)
        dve.wait_ge(logits_done, B + 2)
        n = c.done(dve.tensor_reduce(tot[:, :], pl[:, :, :], AX.X, ALU.max))
        dve.wait_ge(c.sem, n)
        dve.tensor_tensor(by_token, pl[:, :, :], over(tot[:, :], E1, "last"), ALU.subtract).then_inc(shifted, 1)
        dve.wait_ge(exp_done, 1)
        n = c.done(dve.tensor_reduce(tot[:, :], by_token, AX.X, ALU.add))
        dve.wait_ge(c.sem, n)
        n = c.done(dve.reciprocal(tot[:, :], tot[:, :]))
        dve.wait_ge(c.sem, n)
        n = c.done(dve.tensor_tensor(by_token, by_token, over(tot[:, :], E1, "last"), ALU.mult))
        dve.wait_ge(c.sem, n)
        dve.wait_ge(before_done, 2)
        chosen(dve, c, lg[:, :], NT, E1, TOPK1, before, wins, ties, rank[:, :], sel[:, :])
        weigh(dve, c, lg[:, :], sel[:, :], E1, tot[:, :], Wt, NS1)

    return {"sync": sync, "gpsimd": gpsimd, "scalar": scalar, "vector": vector}


def layer1_ffn(nc, io, res, ident):
    with ExitStack() as ctx:
        sb, ps, sem = scope(nc, ctx)
        Wt = sb("m1_Wt", [P, NT, N1])
        XH = sb("m1_XH", [P, 2, DC, B * S], F32R)
        moe_routes(nc, io, res, ident, XH, Wt, "m1", E1, route1)
        moe_experts(nc, io, res, ident, XH, Wt, "e1", N1, F1)


def for_batches(eng, emit):
    for k in range(2):
        emit(k, 0, k)
    with eng.Fori(1, B // 2 - 1) as i:
        for k in range(2):
            emit(2 * i + k, i, k)
    for k in range(2):
        emit(B - 2 + k, B // 2 - 1, k)


def layer1_keys_in(nc, io, res, ident, kv, wsp, mb):
    with ExitStack() as ctx:
        sb, ps, sem = scope(nc, ctx)
        cin = sb("c_cin", [P, 2, TPB, D])
        xh = sb("c_xh", [P, 2, 2, TPB, D])
        st = sb("c_st", [P, 2, TPB, 6])
        mv = sb("c_mv", [P, 2, TPB, 2])
        ve = sb("c_ve", [P, 2, TPB])
        rs = sb("c_rs", [P, 2, TPB])
        gb = sb("c_gb", [P, 2, 2, DC])
        yf = sb("c_yf", [P, 2, 2, DC, S])
        ys = sb("c_ys", [P, 2, 2, 2, DC, S], F32R)
        wr = sb("c_wr", [P, 3, DC, INNER])
        wq = sb("c_wq", [P, 2, 3, DC, 256], F32R)
        m8 = sb("c_m8", [B, S], U8)
        mrow = sb("c_mrow", [B, KEYS], F32R)
        px = [[ps(f"c_px{k}{m}", [P, DC, S]) for m in range(2)] for k in range(2)]
        (gb_in, w_in, m_in, m_ready, stats, moments, var, sd, rstd, xhat, turned, y_done, y_hi, y_lo, wq_hi,
         wq_lo, wq_out, m_out) = (sem("c_" + n) for n in (
             "gb_in w_in m_in m_ready stats moments var sd rstd xhat turned y_done y_hi y_lo wq_hi wq_lo wq_out "
             "m_out").split())
        cin_s = [sem(f"c_cin_in{k}") for k in range(2)]
        kv_out = [sem(f"c_kv_out{k}") for k in range(2)]

        with nc.Block() as block:
            @block.sync
            def _(sp):
                def load(b, k):
                    hpt = P // KPH
                    src = io["ctx"][bass.ds(b, 1)].rearrange("b (j h) d -> (b h) j d", h=STRIDE)
                    for t in range(TPB):
                        sp.dma_start(cin[:, k, t, :], src[t * hpt:(t + 1) * hpt]).then_inc(cin_s[k], 16)

                load(0, 0)
                load(1, 1)
                sp.dma_start(gb[:, :, :, :], io["gb1"]).then_inc(gb_in, 16)

                def emit(b, i, k):
                    if not (isinstance(b, int) and b >= B - 2):
                        sp.wait_ge(xhat, 2 * TPB * (b + 1))
                        load(b + 2, k)
                    for m in range(2):
                        sp.wait_ge(y_lo, 2 * b + m + 1)
                        sp.dma_start(kv[bass.ds(b, 1), :, :, :, m * S:(m + 1) * S].rearrange(
                            "b p a c n -> p (b a) c n"), ys[:, k, m, :, :, :].bitcast(F32)).then_inc(kv_out[k], 16)

                for_batches(sp, emit)
                for k in range(2):
                    sp.wait_ge(kv_out[k], 32 * (B // 2))

            @block.gpsimd
            def _(pool):
                pool.dma_start(m8[:, :], io["mask"]).then_inc(m_in, 16)
                pool.wait_ge(m_in, 16)
                pool.memset(mrow[:, S:KEYS].bitcast(F32), 0.0).then_inc(m_ready, 1)
                pool.tensor_scalar(mrow[:, 0:S].rearrange("b (h j) -> b j h", j=KPH),
                                   m8[:, :].rearrange("b (j h) -> b j h", h=STRIDE), -1.0, MASKED, ALU.add, ALU.mult
                                   ).then_inc(m_ready, 1)
                pool.wait_ge(m_ready, 2)
                pool.dma_start(mb, mrow[:, :].bitcast(F32)).then_inc(m_out, 16)
                pool.wait_ge(w_in, 48)
                for q in range(NQUAD):
                    hi = wq[:, HI, :, :, :].rearrange("p w c n -> p (w c) n")
                    src = wr[:, :, :, q * 256:(q + 1) * 256].rearrange("p w c n -> p (w c) n")
                    if q:
                        pool.wait_ge(wq_out, 16 * q)
                    pool.tensor_copy(hi, src).then_inc(wq_hi, 1)
                    pool.wait_ge(wq_hi, q + 1)
                    pool.tensor_tensor(wq[:, LO, :, :, :].rearrange("p w c n -> p (w c) n"), src, hi.bitcast(F32),
                                       ALU.subtract).then_inc(wq_lo, 1)
                    pool.wait_ge(wq_lo, q + 1)
                    pool.dma_start(wsp[q].rearrange("p a w c n -> p (a w c n)"),
                                   wq[:, :, :, :, :].rearrange("p a w c n -> p (a w c n)").bitcast(F32)).then_inc(wq_out, 16)
                pool.wait_ge(m_out, 16)
                pool.wait_ge(wq_out, 16 * NQUAD)

            @block.scalar
            def _(act):
                for m, n in enumerate("kvq"):
                    act.dma_start(wr[:, m, :, :], io[f"w{n}1"]).then_inc(w_in, 16)

                def root(b):
                    act.wait_ge(var, 2 * b + 2)
                    act.activation(ve[:, :, :], ve[:, :, :], ACT.Sqrt).then_inc(sd, 1)

                def emit(b, i, k):
                    if isinstance(b, int) and b == 0:
                        root(0)
                        act.wait_ge(gb_in, 16)
                    if not (isinstance(b, int) and b == B - 1):
                        root(b + 1)
                    if not (isinstance(i, int) and i == 0):
                        act.wait_ge(kv_out[k], 32 * i)
                    for m in range(2):
                        act.wait_ge(turned, 2 * b + m + 1)
                        for c in range(DC):
                            act.activation(yf[:, k, m, c, :], px[k][m][:, c, :], ACT.Identity,
                                           bias=gb[:, m, 1, c:c + 1], scale=gb[:, m, 0, c:c + 1]).then_inc(y_done, 1)
                        act.wait_ge(y_done, DC * (2 * b + m + 1))
                        act.copy(ys[:, k, m, HI, :, :], yf[:, k, m, :, :]).then_inc(y_hi, 1)

                for_batches(act, emit)

            @block.vector
            def _(dve):
                def normalise(b, i, k):
                    src = [lambda t: cin[:, k, t, :],
                           lambda t: res[:, bass.ds(b * TPB + t, 1), :].rearrange("p a d -> p (a d)")]
                    for m in (1, 0):
                        if m == 0:
                            dve.wait_ge(cin_s[k], 16 * TPB * (i + 1))
                        for t in range(TPB):
                            dve.bn_stats(st[:, m, t, :], src[m](t)).then_inc(stats, 1)
                    dve.wait_ge(stats, 2 * TPB * (b + 1))
                    dve.memset(rs[:, 0, 0:1], 0.0)
                    for m in range(2):
                        for t in range(TPB):
                            dve.bn_aggr(mv[:, m, t, :], st[:, m, t, :]).then_inc(moments, 1)
                    dve.wait_ge(moments, 2 * TPB * (b + 1))
                    dve.tensor_scalar(ve[:, 0, :], mv[:, 0, :, 1], EPS, None, ALU.add).then_inc(var, 1)
                    dve.tensor_scalar(ve[:, 1, :], mv[:, 1, :, 1], 1.0 + EPS, EPS * EPS, ALU.mult, ALU.add
                                      ).then_inc(var, 1)
                    dve.wait_ge(sd, b + 1)
                    dve.reciprocal(rs[:, :, :], ve[:, :, :]).then_inc(rstd, 1)
                    dve.wait_ge(rstd, b + 1)
                    if not (isinstance(b, int) and b < 2):
                        dve.wait_ge(turned, 2 * b - 2)
                    for m in range(2):
                        for t in range(TPB):
                            dve.tensor_scalar(xh[:, k, m, t, :], src[m](t), mv[:, m, t, 0:1], rs[:, m, t:t + 1],
                                              ALU.subtract, ALU.mult).then_inc(xhat, 1)

                def emit(b, i, k):
                    if isinstance(b, int) and b == 0:
                        normalise(0, 0, 0)
                    if not (isinstance(b, int) and b == B - 1):
                        normalise(b + 1, i + k, 1 - k)
                    for m in range(2):
                        dve.wait_ge(y_hi, 2 * b + m + 1)
                        dve.tensor_tensor(ys[:, k, m, LO, :, :], yf[:, k, m, :, :], ys[:, k, m, HI, :, :].bitcast(F32),
                                          ALU.subtract).then_inc(y_lo, 1)

                for_batches(dve, emit)

            @block.tensor
            def _(pe):
                def emit(b, i, k):
                    pe.wait_ge(xhat, 2 * TPB * (b + 1))
                    if not (isinstance(i, int) and i == 0):
                        pe.wait_ge(y_done, 2 * DC * (b - 1))
                    for m in range(2):
                        for t in range(TPB):
                            for c in range(DC):
                                last = pe.transpose(px[k][m][:, c, t * P:(t + 1) * P],
                                                    xh[:, k, m, t, c * P:(c + 1) * P], ident[:, :])
                        last.then_inc(turned, 1)

                for_batches(pe, emit)


WHOLE = (
    """M K0 ST0 ST1 PV0 den ST2 r0 r1 K1 PV1 ST3 r2 r3 PV2 Q ST4 PV3 Y0 S0 S1 ST5 S2 Y1 S3 PV4 S4 S5
       ST6 S6 S7 PV5 S8 S9 ST7 S10 S11 PV6 S12 S13 S14 S15 PV7 N O""".split(),
    """M K0 ST0 ST1 PV0 den ST2 r0 r1 K1 PV1 ST3 r2 r3 PV2 Q ST4 PV3 Y0 S0 S1 V0 S2 ST5 S3 Y1 S4 PV4
       S5 V1 S6 ST6 S7 V2 S8 PV5 S9 V3 S10 ST7 S11 S12 PV6 S13 S14 S15 PV7 N O""".split())
SHARED = ("K0", "K1", "Q", "V0", "V1", "V2", "V3", "den", "Y0", "Y1")


class Step:

    def __init__(self, g, parity, half, b=None, batch_half=None, off=None):
        self.g, self.parity, self.by2, self.b, self.batch_half, self.off = g, parity, half, b, batch_half, off


NSTEP = B * NPAIR


def misc_uses(g0, parity):
    last = isinstance(g0, int) and g0 >= NSTEP - 1
    return [u for u in WHOLE[parity] if u in SHARED and not (g0 == 0 and u[0] in "dY")
            and not (last and u[0] in "KQV")]


PROLOGUE = ["K0", "K1", "Q", "V0", "V1", "V2", "V3"]


def use_before(st):
    if isinstance(st.g, int):
        if st.g == -1:
            return 0
        if st.g == 0:
            return len(PROLOGUE)
        if st.g == NSTEP:
            return 8 * (NSTEP - 1) + 2 + 3
    return 8 * st.g + (2 if st.parity else 4)


def uses_of(st):
    if isinstance(st.g, int):
        if st.g == -1:
            return PROLOGUE
        if st.g in (0, NSTEP - 1, NSTEP):
            return misc_uses(st.g, st.parity)
    return misc_uses(None, st.parity)


def use(st, name):
    return use_before(st) + uses_of(st).index(name) + 1


def order(st):
    if isinstance(st.g, int) and st.g == -1:
        return [(u, 0) for u in PROLOGUE] + [("S", c) for c in range(4 * TPB)] + [("N", 0)]
    uses = uses_of(st)
    epilogue = isinstance(st.g, int) and st.g == NSTEP
    out = []
    for u in WHOLE[st.parity]:
        if u in SHARED:
            if u in uses:
                out.append((u, 0))
        elif u[:2] in ("ST", "PV"):
            if not epilogue:
                out.append((u[:2], int(u[2:])))
        elif u[0] == "r":
            if "den" in uses:
                out.append(("r", int(u[1:])))
        elif u[0] in "SN":
            if "K0" in uses:
                out.append((u[0], int(u[1:] or 0)))
        elif not epilogue:
            out.append((u, 0))
    return out


def for_steps(eng, emit, unroll_halves=False):
    emit(Step(-1, 1, None))
    emit(Step(0, 0, 0, 0, 0, 0))

    def four(b, h):
        for off in range(1, 5):
            emit(Step(8 * b + 4 * h + off, off % 2, 4 * b + 2 * h + off // 2, b, h, off))

    with eng.Fori(0, B - 1) as b:
        if unroll_halves:
            four(b, 0)
            four(b, 1)
        else:
            with eng.Fori(0, 2) as h:
                four(b, h)
    four(B - 1, 0)
    for off in range(1, 4):
        emit(Step(NSTEP - 4 + off, off % 2, NSTEP // 2 - 2 + off // 2, B - 1, 1, off))
    emit(Step(NSTEP, 0, NSTEP // 2, B - 1, 1, 4))


def layer1_pairs(nc, io, res, ident, kv_d, wsp, mb):
    with ExitStack() as ctx:
        sb, ps, sem = scope(nc, ctx)
        kv = sb("d_kv", [P, 2, DC, KEYS], F32R)
        W = [sb(f"d_W{k}", [P, 2, 3, DC, 256], F32R) for k in range(2)]
        K1, K2 = ([[sb(f"d_{n}{j}{h}", [P, KEYS], F32R) for h in range(2)] for j in range(2)] for n in ("K1", "K2"))
        Q0, Q1, Q2 = ([[sb(f"d_{n}{j}{h}", [P, S], F32R) for h in range(2)] for j in range(2)]
                      for n in ("Q0", "Q1", "Q2"))
        V = [sb(f"d_V{k}", [P, NKT, 256]) for k in range(2)]
        pr = sb("d_pr", [P, 4, 2, S])
        acc = sb("d_acc", [P, 2, 2, S])
        osb = sb("d_osb", [P, 2, S])
        rb = sb("d_rb", [P, S])
        OT = sb("d_OT", [P, 2, S])
        Wo = sb("d_Wo", [P, NPAIR, D])
        nm2 = sb("d_nm2", [P, 2, 8, 2])
        nm = sb("d_nm", [P, 2, 8])
        ones = sb("d_ones", [P, HD1])
        onerow = sb("d_onerow", [1, KEYS], F32R)
        ahead = sb("d_ahead", [P, 8])
        pT = [ps(f"d_pT{k}", [P, 2, S]) for k in range(2)]
        pS = ps("d_pS", [P, 2, S])
        pO = ps("d_pO", [P, S])
        pm = ps("d_pm", [P, S])
        (set_up, set_rows, wo_in, kv_in, misc_done, misc_read, k_hi, q_hi, s_done, max_done, m_done, m_copied,
         st_done, exp_done, pv_done, acc_done, o_copied, ot_done, r_done) = (sem("d_" + n) for n in (
             "set_up set_rows wo_in kv_in misc_done misc_read k_hi q_hi s_done max_done m_done m_copied st_done "
             "exp_done pv_done acc_done o_copied ot_done r_done").split())
        w_in = [sem(f"d_w_in{k}") for k in range(2)]
        mask_in = [sem(f"d_mask_in{k}") for k in range(2)]
        copied = sem("d_copied")

        own = (slice(0, HD1), slice(HD1, P))
        other = (slice(HD1, P), slice(0, HD1))
        row0 = (HD1, 0)
        NCOPY = 6
        PT = 4
        tiles = {h: h for h in range(2)}

        def pair(st):
            if isinstance(st.g, int) and st.g == -1:
                return 0, 0, 0
            return (st.parity + 1) % 2, st.g + 1, st.by2 + (1 if st.parity else 0)

        with nc.Block() as block:
            @block.sync
            def _(sp):
                sp.dma_start(kv[:, :, :, :].bitcast(F32), kv_d[0]).then_inc(kv_in, 16)
                for k in range(2):
                    sp.dma_start(W[k][:, :, :, :, :].bitcast(F32), wsp[k]).then_inc(w_in[k], 16)
                sp.dma_start(Wo[:, :, :], io["wo1"]).then_inc(wo_in, 16)
                sp.wait_ge(set_up, 14)
                for j in range(2):
                    for h in range(2):
                        sp.dma_start(K2[j][h][row0[h]:row0[h] + 1, :].bitcast(F32), onerow[:, :].bitcast(F32)).then_inc(set_rows, 16)
                        for q in (Q0, Q2):
                            sp.dma_start(q[j][h][row0[h] + 1:row0[h] + 2, :].bitcast(F32), onerow[:, 0:S].bitcast(F32)).then_inc(set_rows, 16)
                sp.wait_ge(set_rows, 12 * 16)

                def emit(st):
                    j, gp, by2 = pair(st)
                    first = isinstance(st.g, int) and st.g == -1
                    for what, _ in order(st):
                        if what == "K1":
                            if first or st.off == 0:
                                bb = 0
                            elif st.batch_half == 1 and st.off == 3:
                                bb = st.b + 1
                            elif st.batch_half == 1 and st.off == 4:
                                bb = st.b + 1
                            else:
                                bb = st.b
                            sp.wait_ge(k_hi, 4 * gp + 4)
                            for h in range(2):
                                sp.dma_start(K2[j][h][row0[h] + 1:row0[h] + 2, :].bitcast(F32),
                                             mb[bass.ds(bb, 1), :]).then_inc(mask_in[j], 16)
                        if what == "Q":
                            if not first and not st.parity and st.off:
                                k = 1 if st.off == 2 else 0
                                nq = (2 * st.batch_half + (3 if st.off == 2 else 4)) % NQUAD
                                sp.wait_ge(misc_done, use(st, "Q"))
                                if not (isinstance(st.g, int) and st.g >= NSTEP - 4 + 2):
                                    sp.dma_start(W[k][:, :, :, :, :].bitcast(F32), wsp[nq]).then_inc(w_in[k], 16)
                                if st.batch_half == 1 and st.off == 2 and not isinstance(st.b, int):
                                    sp.dma_start(kv[:, :, :, :].bitcast(F32), kv_d[bass.ds(st.b + 1, 1)].rearrange(
                                        "b p a c n -> (b p) a c n")).then_inc(kv_in, 16)
                            if not first and st.off == 0:
                                sp.wait_ge(misc_done, use(st, "Q"))
                                sp.dma_start(W[0][:, :, :, :, :].bitcast(F32), wsp[2]).then_inc(w_in[0], 16)
                for_steps(sp, emit, unroll_halves=True)

            @block.tensor
            def _(pe):
                pe.wait_ge(set_rows, 12 * 16)
                pe.wait_ge(set_up, 14)
                pe.wait_ge(wo_in, 16)

                def emit(st):
                    first = isinstance(st.g, int) and st.g == -1
                    j, gp, by2 = pair(st)
                    nq = 0 if first else (gp_quad := None)
                    names = uses_of(st)
                    T = None if first else NKT * st.g
                    q = st.parity

                    def bank(name):
                        n = use(st, name)
                        if not (isinstance(n, int) and n == 1):
                            pe.wait_ge(misc_read, n - 1)

                    if first or st.off == 0:
                        wk = 0
                    else:
                        wk = {1: 1, 2: 1, 3: 0, 4: 0}[st.off]

                    def project(w, i):
                        for c in range(DC):
                            for n, (wp, xp) in enumerate(PASSES):
                                last = pe.matmul(pm[:, :], W[wk][:, wp, w, c, j * P:(j + 1) * P],
                                                 kv[:, xp, c, i * S:(i + 1) * S], start=(c == 0 and n == 0),
                                                 stop=(c == DC - 1 and n == len(PASSES) - 1))
                        last.then_inc(misc_done, 1)

                    def outputs(par, s, tt, vb):
                        pe.wait_ge(exp_done, tt + 1 + 2)
                        for h in range(2):
                            last = pe.matmul(pO[own[h], :], V[vb][:, s, par * P + h * HD1:par * P + (h + 1) * HD1],
                                             pr[:, s % PT, h, :], start=(s == 0), stop=(s == NKT - 1),
                                             skip_group_check=True)
                        last.then_inc(pv_done, 1)

                    if not first:
                        vb_now = {0: 0, 1: 0, 2: 1, 3: 1, 4: 0}[st.off]
                    for what, n in order(st):
                        if what in ("K0", "K1"):
                            bank(what)
                            if what == "K0":
                                if first:
                                    pe.wait_ge(kv_in, 16)
                                    pe.wait_ge(w_in[0], 16)
                                elif st.off in (1, 3):
                                    pe.wait_ge(w_in[wk], 16 * (2 * st.b + st.batch_half) + (16 if st.off == 1 else 32))
                                    if st.off == 3:
                                        pe.wait_ge(kv_in, 16 * (st.b + st.batch_half + 1))
                            project(0, n if False else int(what[1]))
                        elif what == "Q":
                            bank(what)
                            project(2, 1)
                        elif what[0] == "V":
                            i = int(what[1])
                            bank(what)
                            for t in range(2):
                                kt = 2 * i + t
                                for c in range(DC):
                                    for m, (xp, wp) in enumerate(PASSES):
                                        last = pe.matmul(pm[:, t * 256:(t + 1) * 256],
                                                         kv[:, xp, c, kt * P:(kt + 1) * P], W[wk][:, wp, 1, c, :],
                                                         start=(c == 0 and m == 0),
                                                         stop=(c == DC - 1 and m == len(PASSES) - 1))
                            last.then_inc(misc_done, 1)
                        elif what == "S":
                            m, (h, qt) = n % 2, divmod(n // 2, TPB)
                            if n == 0:
                                pe.wait_ge(copied, NCOPY * gp + NCOPY)
                                pe.wait_ge(mask_in[j], 32 * by2 + 32)
                                if not first:
                                    pe.wait_ge(m_copied, 2 * gp)
                            if n > 1:
                                pe.wait_ge(max_done, 17 * gp + n - 1)
                            pe.matmul(pS[:, m, :], Q0[j][h][:, qt * P:(qt + 1) * P],
                                      K2[j][h][:, m * S:(m + 1) * S], start=True, stop=True).then_inc(s_done, 1)
                        elif what == "M":
                            pe.wait_ge(max_done, 17 * st.g + 17)
                            for h in range(2):
                                for qt in range(TPB):
                                    last = pe.matmul(pS[row0[h]:row0[h] + 1, 0, qt * P:(qt + 1) * P],
                                                     nm[:, q, h * TPB + qt:h * TPB + qt + 1], ident[:, :],
                                                     start=True, stop=True)
                            last.then_inc(m_done, 1)
                        elif what == "ST":
                            s = n
                            if s == 0:
                                pe.wait_ge(m_copied, 2 * st.g + 2)
                                prev = Step(-1, 1, None) if isinstance(st.g, int) and st.g == 0 else (
                                    Step(0, 0, 0) if isinstance(st.g, int) and st.g == 1 else
                                    Step(st.g - 1, 1 - st.parity, None))
                                pe.wait_ge(misc_read, use(prev, "Q"))
                            pe.wait_ge(exp_done, T + s + 1)
                            for h in range(2):
                                pe.matmul(pT[s % 2][:, h, :], K1[q][h][:, s * P:(s + 1) * P], Q1[q][h][:, :],
                                          start=True, stop=False)
                                last = pe.matmul(pT[s % 2][:, h, :], K2[q][h][:, s * P:(s + 1) * P], Q2[q][h][:, :],
                                                 start=False, stop=True)
                            last.then_inc(st_done, 1)
                        elif what == "PV":
                            if n == 0:
                                pe.wait_ge(o_copied, st.g + 1)
                            outputs(q, n, T + n, vb_now)
                        elif what == "den":
                            bank(what)
                            pe.wait_ge(acc_done, 7 * st.g + 7)
                            for h in range(2):
                                last = pe.matmul(pm[own[h], :], ones[:, :], acc[:, 1 - q, h, :],
                                                 start=True, stop=True, skip_group_check=True)
                            last.then_inc(misc_done, 1)
                        elif what[0] == "Y":
                            i = int(what[1])
                            bank(what)
                            pe.wait_ge(ot_done, st.g + 2)
                            wo = Wo[:, bass.ds(4 * st.batch_half + st.off - 1, 1), :].rearrange("p a d -> p (a d)")
                            for t in range(2):
                                tt = 2 * i + t
                                last = pe.matmul(pm[:, t * D:(t + 1) * D], OT[:, 1 - q, tt * P:(tt + 1) * P], wo,
                                                 start=True, stop=True)
                            last.then_inc(misc_done, 1)
                for_steps(pe, emit)

            @block.scalar
            def _(act):
                for k in range(2):
                    act.copy(ahead[:, k:k + 1], ident[:, 0:1]).then_inc(exp_done, 1)
                act.copy(ahead[:, 2:3], ident[:, 0:1]).then_inc(o_copied, 1)

                def emit(st):
                    first = isinstance(st.g, int) and st.g == -1
                    j, gp, by2 = pair(st)
                    q = st.parity
                    for what, n in order(st):
                        if what in ("K0", "K1"):
                            i = int(what[1])
                            act.wait_ge(misc_done, use(st, what))
                            if not (isinstance(st.g, int) and st.g <= 0):
                                act.wait_ge(st_done, NKT * st.g)
                            for h in range(2):
                                act.copy(K1[j][h][own[h], i * S:(i + 1) * S], pm[own[h], :]).then_inc(k_hi, 1)
                            if i:
                                for h in range(2):
                                    act.wait_ge(k_hi, 4 * gp + 3 + h)
                                    act.copy(K2[j][h][own[h], :], K1[j][h][own[h], :].bitcast(F32)).then_inc(copied, 1)
                        elif what == "Q":
                            act.wait_ge(misc_done, use(st, what))
                            for h in range(2):
                                act.mul(Q1[j][h][own[h], :], pm[own[h], :], SCALE1).then_inc(q_hi, 1)
                            for q_, rows in ((Q0, own), (Q1, other)):
                                for h in range(2):
                                    act.wait_ge(q_hi, 2 * gp + h + 1)
                                    act.copy(q_[j][h][rows[h], :], Q1[j][h][own[h], :].bitcast(F32)).then_inc(copied, 1)
                        elif what[0] == "V":
                            i = int(what[1])
                            vb = 0 if first else {1: 1, 3: 0}[st.off]
                            act.wait_ge(misc_done, use(st, what))
                            if not first:
                                act.wait_ge(pv_done, NKT * st.g + PT)
                            act.copy(V[vb][:, 2 * i:2 * i + 2, :].rearrange("p a n -> p (a n)"), pm[:, :]
                                     ).then_inc(misc_read, 1)
                        elif what == "M":
                            act.wait_ge(m_done, st.g + 1)
                            act.copy(Q2[q][0][row0[0]:row0[0] + 1, :], pS[row0[0]:row0[0] + 1, 0, :]
                                     ).then_inc(m_copied, 1)
                        elif what == "den":
                            act.wait_ge(misc_done, use(st, what))
                            act.wait_ge(ot_done, st.g + 1)
                            act.copy(rb[:, :], pm[:, :]).then_inc(misc_read, 1)
                        elif what == "ST":
                            T = NKT * st.g + n
                            act.wait_ge(st_done, T + 1)
                            act.wait_ge(pv_done, T + 1)
                            act.wait_ge(acc_done, 7 * st.g + 7 + (n - 3 if n < 4 else max(n - 4, 1)))
                            act.activation(pr[:, n % PT, :, :], pT[n % 2][:, :, :], ACT.Exp).then_inc(exp_done, 1)
                        elif what == "O":
                            act.wait_ge(pv_done, NKT * st.g + NKT + PT)
                            act.wait_ge(ot_done, st.g + 1)
                            act.copy(osb[:, q, :], pO[:, :]).then_inc(o_copied, 1)
                for_steps(act, emit)

            @block.vector
            def _(dve):
                for k in range(2):
                    dve.memset(ahead[:, 3 + k:4 + k], 0.0).then_inc(ot_done, 1)

                def emit(st):
                    j, gp, by2 = pair(st)
                    q = st.parity
                    for what, n in order(st):
                        if what in ("K0", "K1"):
                            i = int(what[1])
                            for h in range(2):
                                dve.wait_ge(k_hi, 4 * gp + 2 * i + h + 1)
                                ins = dve.tensor_tensor(K1[j][h][other[h], i * S:(i + 1) * S], pm[own[h], :],
                                                        K1[j][h][own[h], i * S:(i + 1) * S].bitcast(F32),
                                                        ALU.subtract)
                            ins.then_inc(misc_read, 1)
                        elif what == "Q":
                            for h in range(2):
                                dve.wait_ge(q_hi, 2 * gp + h + 1)
                                ins = dve.scalar_tensor_tensor(Q2[j][h][own[h], :], pm[own[h], :], SCALE1,
                                                               Q1[j][h][own[h], :].bitcast(F32), ALU.mult,
                                                               ALU.subtract)
                            ins.then_inc(misc_read, 1)
                        elif what == "S":
                            dve.wait_ge(s_done, 16 * gp + n + 1)
                            dve.tensor_reduce(nm2[:, j, n // 2, n % 2:n % 2 + 1], pS[:, n % 2, :], AX.X,
                                              ALU.max, negate=True).then_inc(max_done, 1)
                        elif what == "N":
                            dve.wait_ge(max_done, 17 * gp + 16)
                            dve.tensor_tensor(nm[:, j, :], nm2[:, j, :, 0], nm2[:, j, :, 1], ALU.min
                                              ).then_inc(max_done, 1)
                        elif what == "M":
                            dve.wait_ge(m_done, st.g + 1)
                            dve.tensor_copy(Q2[q][1][row0[1]:row0[1] + 1, :], pS[row0[1]:row0[1] + 1, 0, :]
                                            ).then_inc(m_copied, 1)
                        elif what == "r":
                            if n == 0:
                                dve.wait_ge(misc_read, use(st, "den"))
                            quarter = slice(n * P, (n + 1) * P)
                            dve.reciprocal(rb[:, quarter], rb[:, quarter]).then_inc(r_done, 1)
                            if n == TPB - 1:
                                dve.wait_ge(r_done, TPB * st.g)
                                dve.wait_ge(o_copied, st.g + 1)
                                dve.tensor_tensor(OT[:, 1 - q, :], osb[:, 1 - q, :], rb[:, :], ALU.mult
                                                  ).then_inc(ot_done, 1)
                        elif what[0] == "Y":
                            i = int(what[1])
                            dve.wait_ge(misc_done, use(st, what))
                            r = res[:, bass.ds(TPB * st.b + 2 * i, 2), :]
                            dve.tensor_tensor(r, r, pm[:, :].rearrange("p (t d) -> p t d", d=D), ALU.add
                                              ).then_inc(misc_read, 1)
                for_steps(dve, emit)

            @block.gpsimd
            def _(pool):
                for j in range(2):
                    for h in range(2):
                        for b_ in (K2, Q0, Q2):
                            pool.memset(b_[j][h][:, :].bitcast(F32), 0.0).then_inc(set_up, 1)
                pool.memset(onerow[:, :].bitcast(F32), 1.0).then_inc(set_up, 1)
                pool.memset(ones[:, :], 1.0).then_inc(set_up, 1)
                pool.memset(ahead[:, 6:7], 0.0).then_inc(pv_done, PT)
                pool.memset(ahead[:, 7:8], 0.0).then_inc(acc_done, 7)

                def emit(st):
                    if isinstance(st.g, int) and st.g in (-1, NSTEP):
                        return
                    q = st.parity
                    for s in range(1, NKT):
                        T = NKT * st.g + s
                        pool.wait_ge(exp_done, T + 1 + 2)
                        if s == 1:
                            if not (isinstance(st.g, int) and st.g < 2):
                                prev = Step(st.g - 1, 1 - q, None)
                                pool.wait_ge(misc_done, use(prev, "den"))
                            a = pr[:, 0, :, :]
                        else:
                            pool.wait_ge(acc_done, 7 * st.g + s - 1 + 7)
                            a = acc[:, q, :, :]
                        pool.tensor_tensor(acc[:, q, :, :], a, pr[:, s % PT, :, :], ALU.add).then_inc(acc_done, 1)
                for_steps(pool, emit)


def layer1_attention(nc, io, res, ident):
    kv = nc.dram_tensor("kv_split", (B, P, 2, DC, KEYS), F32, kind="Internal").ap()
    wsp = nc.dram_tensor("w_split", (NQUAD, P, 2, 3, DC, 256), F32, kind="Internal").ap()
    mb = nc.dram_tensor("mask_bias", (B, KEYS), F32, kind="Internal").ap()
    layer1_keys_in(nc, io, res, ident, kv, wsp, mb)
    layer1_pairs(nc, io, res, ident, kv, wsp, mb)


PHASES = [layer0_attention, layer0_ffn, layer1_attention, layer1_ffn]


def network(nc, io, out):
    with ExitStack() as ctx:
        sb, ps, sem = scope(nc, ctx)
        res = sb("res", [P, NT, D])
        ident = sb("ident", [P, P])
        id_ready = sem("id_ready")
        stored = sem("stored")
        with nc.Block() as block:
            @block.gpsimd
            def _(pool):
                pool.memset(ident[:, :], 0.0).then_inc(id_ready, 1)
                pool.wait_ge(id_ready, 1)
                pool.affine_select(out=ident[:, :], in_=ident[:, :], compare_op=ALU.not_equal, fill=1.0, base=0,
                                   pattern=[[-1, P]], channel_multiplier=1).then_inc(id_ready, 1)
        for phase in PHASES:
            phase(nc, io, res, ident)
        with nc.Block() as block:
            @block.sync
            def _(sp):
                sp.dma_start(out.rearrange("b (t p) d -> p (b t) d", p=P), res[:, :, :]).then_inc(stored, 16)
                sp.wait_ge(stored, 16)


def _rows(a):
    return a.reshape(-1, P, a.shape[-1]).transpose(1, 0, 2)


def _gate_up(np, parts):
    out = []
    for ws in parts:
        w = np.concatenate(ws).transpose(0, 2, 1)
        out.append(w.reshape(w.shape[0], DC, P, -1).transpose(0, 2, 1, 3).reshape(w.shape[0], P, -1))
    return np.concatenate(out, axis=2)


def _widths(w):
    return w.reshape(D, NS1, F1).transpose(1, 2, 0)


def laid_out(np, a):
    z = {"x": a["x"], "ctx": a["ctx_1024"]}
    for n in "qkvo":
        z[f"w{n}0"] = _rows(a[f"L0_xattn_W{n}"].T)
    for n in "qkv":
        z[f"b{n}0"] = a[f"L0_xattn_b{n}"].reshape(DC, P).T
    z["bo0"] = a["L0_xattn_bo"]
    z["ebias"] = a["L0_ffn_e_bias"]
    z["m0_gate"] = _rows(a["L0_ffn_gate_w"].T)
    z["e0_gu"] = _gate_up(np, [[a["L0_ffn_gate_proj"], a["L0_ffn_shared_gate_w"][None]],
                               [a["L0_ffn_up_proj"], a["L0_ffn_shared_up_w"][None]]])
    z["e0_d"] = np.concatenate([a["L0_ffn_down_proj"], a["L0_ffn_shared_down_w"][None]]).transpose(0, 2, 1)
    for n in "kvq":
        z[f"w{n}1"] = _rows(a[f"L1_xattn_W{n}"])
    z["wo1"] = _rows(a["L1_xattn_Wo"])
    z["gb1"] = np.stack([np.stack([a[f"L1_xattn_{p}{m}"].reshape(DC, P) for p in "gb"]) for m in "ml"]
                        ).transpose(3, 0, 1, 2)
    z["mask"] = a["mask_BxS2_bf1"].view(np.uint8)
    z["m1_gate"] = _rows(a["L1_ffn_gate_w"].T)
    z["e1_gu"] = _gate_up(np, [[a["L1_ffn_w_gate"].transpose(0, 2, 1), _widths(a["L1_ffn_sw_gate"])],
                               [a["L1_ffn_w_up"].transpose(0, 2, 1), _widths(a["L1_ffn_sw_up"])]])
    z["e1_d"] = np.concatenate([a["L1_ffn_w_down"], a["L1_ffn_sw_down"].reshape(NS1, F1, D)])
    return {k: np.ascontiguousarray(v) for k, v in z.items()}


def kernel(**inputs):
    import numpy as _np
    import concourse.bacc as _bacc
    from concourse import mybir as _mybir
    from concourse.bass_utils import run_bass_kernel_spmd as _run

    nc = _bacc.Bacc("TRN2", target_bir_lowering=False, num_devices=1)
    arrays, io = {}, {}
    for name, a in laid_out(_np, {k: _np.asarray(v) for k, v in inputs.items()}).items():
        arrays[f"in_{name}_dram"] = a
        io[name] = nc.dram_tensor(f"in_{name}_dram", a.shape, _mybir.dt.from_np(a.dtype), kind="ExternalInput").ap()
    out = nc.dram_tensor("out_0_dram", (B, S, D), F32, kind="ExternalOutput").ap()
    network(nc, io, out)
    r = _run(nc, [arrays], core_ids=[0])
    return r.results[0]["out_0_dram"]
```

```python
from contextlib import ExitStack

import concourse.bass as bass
from concourse import mybir

P = 128
B, S, D = 8, 512, 256
TPB = S // P
NT = B * TPB
DC = D // P
EPS = 1e-5

H0 = 16
HD0 = D // H0
STRIDE = 16
KPH = S // STRIDE
SCALE0 = HD0 ** -0.5

E0, G0, I0 = 16, 4, 128
PG0 = E0 // G0
TOPG0, TOPK0 = 2, 4
N0 = E0 + 1

H1, HD1 = 16, 64
INNER = H1 * HD1
KEYS = 2 * S
NKT = KEYS // P
SCALE1 = HD1 ** -0.5
NPAIR = H1 // 2
NQUAD = H1 // 4
MASKED = 1.0e30

E1, F1, NS1 = 8, 352, 2
TOPK1 = 2
FCH1 = [(f, min(P, F1 - f)) for f in range(0, F1, P)]
NBLK = (B * S * TOPK1 + E1 * (P - 1)) // P
ROUTE_SCALE = 2.5

F32 = mybir.dt.float32
F32R = mybir.dt.float32r
U8 = mybir.dt.uint8
ALU = mybir.AluOpType
ACT = mybir.ActivationFunctionType
AX = mybir.AxisListType

HI, LO = 0, 1
PASSES = [(LO, HI), (HI, LO), (HI, HI)]


class Counted:

    def __init__(self, sem, base=0):
        self.sem, self.base, self.n = sem, base, 0

    def done(self, instruction, by=1):
        instruction.then_inc(self.sem, by)
        self.n += by
        return self.base + self.n

    def now(self):
        return self.base + self.n


def scope(nc, ctx):
    def sb(name, shape, dt=F32):
        return ctx.enter_context(nc.sbuf_tensor(name, shape, dt))

    def ps(name, shape, dt=F32):
        return ctx.enter_context(nc.psum_tensor(name, shape, dt))

    taken = []

    def sem(name):
        taken.append(nc.alloc_semaphore(name=name))
        return taken[-1]

    def give_back():
        if taken:
            nc.clear_and_free_semaphores(taken)
            nc.all_engine_barrier()

    ctx.callback(give_back)
    return sb, ps, sem


def ln_sems(sem, tag):
    return {n: sem(f"{tag}_{n}") for n in ("stats", "cleared", "moments", "var", "sd", "rstd", "xhat")}


def ln_vector(dve, s, n, src, st, mv, ve, rs, dst):
    for t in range(TPB):
        dve.bn_stats(st[:, t, :], src(t)).then_inc(s["stats"], 1)
    dve.wait_ge(s["stats"], n * TPB + TPB)
    dve.memset(ve[:, :], 0.0).then_inc(s["cleared"], 1)
    for t in range(TPB):
        dve.bn_aggr(mv[:, t, :], st[:, t, :]).then_inc(s["moments"], 1)
    dve.wait_ge(s["moments"], n * TPB + TPB)
    dve.wait_ge(s["cleared"], n + 1)
    dve.tensor_scalar(ve[:, :], mv[:, :, 1], EPS, None, ALU.add).then_inc(s["var"], 1)
    dve.wait_ge(s["sd"], n + 1)
    dve.reciprocal(rs[:, :], ve[:, :]).then_inc(s["rstd"], 1)
    dve.wait_ge(s["rstd"], n + 1)
    for t in range(TPB):
        dve.tensor_scalar(dst(t), src(t), mv[:, t, 0:1], rs[:, t:t + 1], ALU.subtract,
                          ALU.mult).then_inc(s["xhat"], 1)


def ln_scalar(act, s, n, ve):
    act.wait_ge(s["var"], n + 1)
    act.activation(ve[:, :], ve[:, :], ACT.Sqrt).then_inc(s["sd"], 1)


def for_batches(eng, emit):
    for k in range(2):
        emit(k, 0, k)
    with eng.Fori(1, B // 2 - 1) as i:
        for k in range(2):
            emit(2 * i + k, i, k)
    for k in range(2):
        emit(B - 2 + k, B // 2 - 1, k)


def layer0_attention(nc, io, res, ident):
    with ExitStack() as ctx:
        sb, ps, sem = scope(nc, ctx)
        xT = sb("a_xT", [P, DC, B * S])
        cT = sb("a_cT", [P, DC, B * S])

        with ExitStack() as inner:
            sb1, ps1, sem1 = scope(nc, inner)
            cin = sb1("a_cin", [P, 2, TPB, D])
            xh = sb1("a_xh", [P, 2, TPB, D])
            ahead = sb1("a_ahead", [P, 4])
            st = sb1("a_st", [P, TPB, 6])
            mv = sb1("a_mv", [P, TPB, 2])
            ve = sb1("a_ve", [P, TPB])
            rs = sb1("a_rs", [P, TPB])
            px = [ps1(f"a_px{k}", [P, DC, S]) for k in range(2)]
            pc = [ps1(f"a_pc{k}", [P, DC, S]) for k in range(2)]
            x_in = [sem1(f"a_x_in{k}") for k in range(2)]
            c_in = [sem1(f"a_c_in{k}") for k in range(2)]
            ls = ln_sems(sem1, "a")
            x_turned, c_turned, x_out, c_out = (sem1(f"a_{n}") for n in ("x_turned", "c_turned", "x_out", "c_out"))

            with nc.Block() as block:
                @block.sync
                def _(sp):
                    def load(b, k):
                        sp.dma_start(res[:, bass.ds(b * TPB, TPB), :],
                                     io["x"][bass.ds(b, 1)].rearrange("b (t p) d -> p (b t) d", p=P)
                                     ).then_inc(x_in[k], 16)

                    def emit(b, i, k):
                        if not (isinstance(b, int) and b >= B - 2):
                            sp.wait_ge(ls["xhat"], TPB * (b + 1))
                            load(b + 2, k)

                    load(0, 0)
                    load(1, 1)
                    for_batches(sp, emit)

                @block.gpsimd
                def _(pool):
                    with pool.Fori(0, B // 2) as i:
                        for k in range(2):
                            b = 2 * i + k
                            pool.wait_ge(c_out, b + 1)
                            for t in range(TPB):
                                hpt = P // KPH
                                pool.dma_start(cin[:, k, t, :],
                                               io["ctx"][bass.ds(b, 1)].rearrange(
                                                   "b (j h) d -> (b h) j d", h=STRIDE)[t * hpt:(t + 1) * hpt]
                                               ).then_inc(c_in[k], 16)

                @block.vector
                def _(dve):
                    for k in range(2):
                        dve.memset(ahead[:, k:k + 1], 0.0).then_inc(x_out, 1)
                    def normalise(b, i, k):
                        dve.wait_ge(x_in[k], 16 * i + 16)
                        ln_vector(dve, ls, b, lambda t: res[:, bass.ds(b * TPB + t, 1), :].rearrange(
                            "p a d -> p (a d)"), st, mv, ve, rs, lambda t: xh[:, k, t, :])

                    def emit(b, i, k):
                        if not (isinstance(b, int) and b == B - 1):
                            normalise(b + 1, i + k, 1 - k)
                        dve.wait_ge(x_turned, b + 1)
                        dve.tensor_copy(xT[:, :, bass.ds(b * S, S)], px[k][:, :, :]).then_inc(x_out, 1)

                    normalise(0, 0, 0)
                    for_batches(dve, emit)

                @block.scalar
                def _(act):
                    for k in range(2):
                        act.copy(ahead[:, 2 + k:3 + k], ident[:, 0:1]).then_inc(c_out, 1)
                    def emit(b, i, k):
                        if not (isinstance(b, int) and b == B - 1):
                            ln_scalar(act, ls, b + 1, ve)
                        act.wait_ge(c_turned, b + 1)
                        act.copy(cT[:, :, bass.ds(b * S, S)], pc[k][:, :, :]).then_inc(c_out, 1)

                    ln_scalar(act, ls, 0, ve)
                    for_batches(act, emit)

                @block.tensor
                def _(pe):
                    with pe.Fori(0, B // 2) as i:
                        for k in range(2):
                            b = 2 * i + k
                            pe.wait_ge(c_in[k], 16 * TPB * (i + 1))
                            pe.wait_ge(c_out, b + 1)
                            for t in range(TPB):
                                for c in range(DC):
                                    last = pe.transpose(pc[k][:, c, t * P:(t + 1) * P],
                                                        cin[:, k, t, c * P:(c + 1) * P], ident[:, :])
                            last.then_inc(c_turned, 1)
                            pe.wait_ge(ls["xhat"], TPB * (b + 1))
                            pe.wait_ge(x_out, b + 1)
                            for t in range(TPB):
                                for c in range(DC):
                                    last = pe.transpose(px[k][:, c, t * P:(t + 1) * P],
                                                        xh[:, k, t, c * P:(c + 1) * P], ident[:, :])
                            last.then_inc(x_turned, 1)

        with ExitStack() as inner:
            sb2, ps2, sem2 = scope(nc, inner)
            w = {n: sb2(f"a_w{n}", [P, DC, D]) for n in "qkvo"}
            bias = {n: sb2(f"a_b{n}", [P, DC]) for n in "qkv"}
            bqs = sb2("a_bqs", [P, DC])
            bo = sb2("a_bo", [P, D])
            own = sb2("a_own", [P, S // 2])
            KT = sb2("a_KT", [P, 2, DC, S // 2])
            VT = sb2("a_VT", [P, DC, S // 2])
            QT = sb2("a_QT", [P, 2, DC, S])
            Vk = sb2("a_Vk", [P, 2, 4, P])
            sc = sb2("a_sc", [P, 2, S])
            pr = sb2("a_pr", [P, 2, S])
            mx = sb2("a_mx", [P, 2, H0])
            sm = sb2("a_sm", [P, 2, H0])
            rc = sb2("a_rc", [P, 2, H0])
            PT = sb2("a_PT", [P, 4, S])
            OT = sb2("a_OT", [P, DC, S])
            pKV = ps2("a_pKV", [P, 2, S])
            pQ = ps2("a_pQ", [P, DC, S])
            pS = ps2("a_pS", [P, 2, S])
            pT = ps2("a_pT", [P, 2, S])
            (w_in, own_ready, bqs_ready, k_done, k_ready, v_done, v_ready, vk_turned, vk_ready, q_done, q_ready,
             s_done, max_ready, shifted, exp_ready, sum_ready, rcp_ready, probs_ready, p_turned, p_ready, pv_done,
             o_ready, y_done, y_added, biased) = (sem2("a_" + n) for n in (
                 "w_in own_ready bqs_ready k_done k_ready v_done v_ready vk_turned vk_ready q_done q_ready s_done "
                 "max_ready shifted exp_ready sum_ready rcp_ready probs_ready p_turned p_ready pv_done o_ready "
                 "y_done y_added biased").split())

            def known(b, *values):
                return isinstance(b, int) and b in values

            with nc.Block() as block:
                @block.sync
                def _(sp):
                    for n in "qkvo":
                        sp.dma_start(w[n][:, :, :], io[f"w{n}0"]).then_inc(w_in, 16)
                    for n in "qkv":
                        sp.dma_start(bias[n][:, :], io[f"b{n}0"]).then_inc(w_in, 16)
                    sp.dma_start(bo[:, :], io["bo0"].partition_broadcast(P)).then_inc(w_in, 16)

                @block.gpsimd
                def _(pool):
                    pool.memset(own[:, :], 1.0).then_inc(own_ready, 1)
                    pool.wait_ge(own_ready, 1)
                    v = own[:, :].rearrange("p (h j) -> p h j", j=KPH)
                    pool.affine_select(out=v, in_=v, compare_op=ALU.is_ge, fill=0.0, base=0,
                                       pattern=[[-HD0, H0 // 2], [0, KPH]], channel_multiplier=1).then_inc(own_ready, 1)
                    pool.wait_ge(own_ready, 2)
                    pool.affine_select(out=v, in_=v, compare_op=ALU.is_ge, fill=0.0, base=HD0 - 1,
                                       pattern=[[HD0, H0 // 2], [0, KPH]], channel_multiplier=-1).then_inc(own_ready, 1)
                    pool.wait_ge(w_in, 128)
                    for b in range(B):
                        r = res[:, b * TPB:(b + 1) * TPB, :]
                        pool.tensor_tensor(r, r, bo[:, :].rearrange("p (o d) -> p o d", o=1).to_broadcast([P, TPB, D]),
                                           ALU.add).then_inc(biased, 1)

                @block.tensor
                def _(pe):
                    def project_kv(b, m, done):
                        if not known(b, 0):
                            if m == 0:
                                pe.wait_ge(k_ready, 2 * b)
                            else:
                                pe.wait_ge(vk_ready, b)
                        for c in range(DC):
                            for k in range(DC):
                                last = pe.matmul(pKV[:, m, c * 256:(c + 1) * 256],
                                                 w["kv"[m]][:, k, c * P:(c + 1) * P],
                                                 cT[:, k, bass.ds(b * S + c * 256, 256)],
                                                 start=(k == 0), stop=(k == DC - 1))
                        last.then_inc(done, 1)

                    def project_q(b):
                        if not known(b, 0, 1):
                            pe.wait_ge(o_ready, 2 * b - 2)
                        for c in range(DC):
                            for k in range(DC):
                                last = pe.matmul(pQ[:, c, :], w["q"][:, k, c * P:(c + 1) * P],
                                                 xT[:, k, bass.ds(b * S, S)], start=(k == 0), stop=(k == DC - 1))
                        last.then_inc(q_done, 1)

                    def turn_values(b):
                        pe.wait_ge(v_ready, 2 * b + 2)
                        for kc in range(4):
                            last = pe.transpose(pKV[:, 1, kc * P:(kc + 1) * P],
                                                VT[:, kc // 2, (kc % 2) * P:(kc % 2 + 1) * P], ident[:, :])
                        last.then_inc(vk_turned, 1)

                    def scores(b, k, qt):
                        if qt == 0:
                            pe.wait_ge(k_ready, 2 * b + 2)
                            pe.wait_ge(q_ready, 2 * b + 2)
                        if not (known(b, 0) and qt < 2):
                            pe.wait_ge(shifted, TPB * b + qt - 1)
                        for c in range(DC):
                            last = pe.matmul(pS[:, qt % 2, c * 256:(c + 1) * 256],
                                             QT[:, k, c, qt * P:(qt + 1) * P], KT[:, k, c, :], start=True, stop=True)
                        last.then_inc(s_done, 1)

                    def turn(b, qt):
                        pe.wait_ge(probs_ready, TPB * b + qt + 1)
                        if not known(b, 0):
                            if qt < 2:
                                pe.wait_ge(y_added, 2 * b - 1 + qt)
                        if qt >= 2:
                            pe.wait_ge(p_ready, TPB * b + qt - 1)
                        for kc in range(4):
                            last = pe.transpose(pT[:, qt % 2, kc * P:(kc + 1) * P],
                                                pr[:, qt % 2, kc * P:(kc + 1) * P], ident[:, :])
                        last.then_inc(p_turned, 1)

                    pe.wait_ge(w_in, 128)
                    project_kv(0, 0, k_done)
                    project_kv(0, 1, v_done)
                    project_q(0)
                    turn_values(0)
                    scores(0, 0, 0)
                    scores(0, 0, 1)

                    def emit(b, i, k):
                        more = not known(b, B - 1)
                        if more:
                            project_kv(b + 1, 0, k_done)
                        turn(b, 0)
                        scores(b, k, 2)
                        if more:
                            project_kv(b + 1, 1, v_done)
                        turn(b, 1)
                        scores(b, k, 3)
                        if more:
                            project_q(b + 1)
                        turn(b, 2)
                        if more:
                            turn_values(b + 1)
                        turn(b, 3)
                        if more:
                            scores(b + 1, 1 - k, 0)
                            scores(b + 1, 1 - k, 1)
                        pe.wait_ge(p_ready, TPB * b + TPB)
                        pe.wait_ge(vk_ready, b + 1)
                        if more:
                            pe.wait_ge(q_ready, 2 * b + 4)
                        for c in range(DC):
                            for j in range(2):
                                last = pe.matmul(pQ[:, c, :], Vk[:, k, 2 * c + j, :], PT[:, 2 * c + j, :],
                                                 start=(j == 0), stop=(j == 1))
                            last.then_inc(pv_done, 1)
                        pe.wait_ge(o_ready, 2 * b + 2)
                        for t in range(TPB):
                            for c in range(DC):
                                last = pe.matmul(pT[:, t // 2, (t % 2) * D:(t % 2 + 1) * D],
                                                 OT[:, c, t * P:(t + 1) * P], w["o"][:, c, :],
                                                 start=(c == 0), stop=(c == DC - 1))
                            if t % 2:
                                last.then_inc(y_done, 1)

                    for_batches(pe, emit)

                @block.vector
                def _(dve):
                    dve.wait_ge(w_in, 128)
                    dve.wait_ge(own_ready, 3)

                    def heads(a):
                        return a.rearrange("p (h j) -> p h j", j=KPH)

                    def each(a):
                        return a.rearrange("p (h o) -> p h o", o=1).to_broadcast([P, H0, KPH])

                    def keys_values(b, m, done, ready, n, out):
                        dve.wait_ge(done, b + 1)
                        if m and not known(b, 0):
                            dve.wait_ge(vk_turned, b)
                        for c in range(DC):
                            dve.scalar_tensor_tensor(out[:, c, :], pKV[:, m, c * 256:(c + 1) * 256],
                                                     bias[n][:, c:c + 1], own[:, :], ALU.add,
                                                     ALU.mult).then_inc(ready, 1)

                    def shift(b, qt):
                        n, k = TPB * b + qt + 1, qt % 2
                        dve.wait_ge(s_done, n)
                        dve.tensor_reduce(mx[:, k, :], heads(pS[:, k, :]), AX.X, ALU.max).then_inc(max_ready, 1)
                        dve.wait_ge(max_ready, n)
                        dve.tensor_tensor(heads(sc[:, k, :]), heads(pS[:, k, :]), each(mx[:, k, :]),
                                          ALU.subtract).then_inc(shifted, 1)

                    def probabilities(b, qt):
                        n, k = TPB * b + qt + 1, qt % 2
                        dve.wait_ge(exp_ready, n)
                        dve.tensor_reduce(sm[:, k, :], heads(sc[:, k, :]), AX.X, ALU.add).then_inc(sum_ready, 1)
                        dve.wait_ge(sum_ready, n)
                        dve.reciprocal(rc[:, k, :], sm[:, k, :]).then_inc(rcp_ready, 1)
                        dve.wait_ge(rcp_ready, n)
                        if not (known(b, 0) and qt < 2):
                            dve.wait_ge(p_turned, n - 2)
                        dve.tensor_tensor(heads(pr[:, k, :]), heads(sc[:, k, :]), each(rc[:, k, :]),
                                          ALU.mult).then_inc(probs_ready, 1)

                    def add_results(b):
                        dve.wait_ge(biased, b + 1)
                        for m in range(2):
                            dve.wait_ge(y_done, 2 * b + m + 1)
                            r = res[:, bass.ds(b * TPB + 2 * m, 2), :]
                            dve.tensor_tensor(r, r, pT[:, m, :].rearrange("p (t d) -> p t d", d=D),
                                              ALU.add).then_inc(y_added, 1)

                    keys_values(0, 0, k_done, k_ready, "k", KT[:, 0, :, :])
                    keys_values(0, 1, v_done, v_ready, "v", VT)
                    shift(0, 0)
                    shift(0, 1)

                    def emit(b, i, k):
                        more = not known(b, B - 1)
                        probabilities(b, 0)
                        if not known(b, 0):
                            add_results(b - 1)
                        if more:
                            keys_values(b + 1, 0, k_done, k_ready, "k", KT[:, 1 - k, :, :])
                        shift(b, 2)
                        probabilities(b, 1)
                        if more:
                            keys_values(b + 1, 1, v_done, v_ready, "v", VT)
                        shift(b, 3)
                        probabilities(b, 2)
                        probabilities(b, 3)
                        if more:
                            shift(b + 1, 0)
                            shift(b + 1, 1)

                    for_batches(dve, emit)
                    add_results(B - 1)

                @block.scalar
                def _(act):
                    act.wait_ge(w_in, 128)
                    act.mul(bqs[:, :], bias["q"][:, :], SCALE0).then_inc(bqs_ready, 1)
                    act.wait_ge(bqs_ready, 1)

                    def queries(b, k):
                        act.wait_ge(q_done, b + 1)
                        for c in range(DC):
                            act.activation(QT[:, k, c, :], pQ[:, c, :], ACT.Identity, bias=bqs[:, c:c + 1],
                                           scale=SCALE0).then_inc(q_ready, 1)

                    def values(b, k):
                        act.wait_ge(vk_turned, b + 1)
                        act.copy(Vk[:, k, :, :].rearrange("p a d -> p (a d)"), pKV[:, 1, :]).then_inc(vk_ready, 1)

                    def exponentials(b, qt):
                        act.wait_ge(shifted, TPB * b + qt + 1)
                        act.activation(sc[:, qt % 2, :], sc[:, qt % 2, :], ACT.Exp).then_inc(exp_ready, 1)

                    def turned(b, qt):
                        act.wait_ge(p_turned, TPB * b + qt + 1)
                        act.copy(PT[:, :, qt * P:(qt + 1) * P],
                                 pT[:, qt % 2, :].rearrange("p (a q) -> p a q", q=P)).then_inc(p_ready, 1)

                    queries(0, 0)
                    values(0, 0)
                    exponentials(0, 0)
                    exponentials(0, 1)

                    def emit(b, i, k):
                        more = not known(b, B - 1)
                        turned(b, 0)
                        exponentials(b, 2)
                        turned(b, 1)
                        exponentials(b, 3)
                        if more:
                            queries(b + 1, 1 - k)
                        turned(b, 2)
                        if more:
                            values(b + 1, 1 - k)
                        turned(b, 3)
                        if more:
                            exponentials(b + 1, 0)
                            exponentials(b + 1, 1)
                        for c in range(DC):
                            act.wait_ge(pv_done, 2 * b + c + 1)
                            act.copy(OT[:, c, :], pQ[:, c, :]).then_inc(o_ready, 1)

                    for_batches(act, emit)


def moe_routes(nc, io, res, ident, XH, Wt, tag, E, route, rows=None):
    with ExitStack() as ctx:
        sb, ps, sem = scope(nc, ctx)
        xh = sb(f"{tag}_xh", [P, 2, TPB, D])
        xs = sb(f"{tag}_xs", [P, 2, DC, S])
        gate = sb(f"{tag}_gate", [P, DC, E])
        st = sb(f"{tag}_st", [P, TPB, 6])
        mv = sb(f"{tag}_mv", [P, TPB, 2])
        ve = sb(f"{tag}_ve", [P, TPB])
        rs = sb(f"{tag}_rs", [P, TPB])
        ahead = sb(f"{tag}_ahead", [P, 4])
        px = [ps(f"{tag}_px{k}", [P, DC, S]) for k in range(2)]
        pl = ps(f"{tag}_pl", [P, NT, E])
        ls = ln_sems(sem, tag)
        gate_in, turned, x_copied, hi_done, lo_done, logits_done, rows_done = (
            sem(f"{tag}_{n}") for n in ("gate_in", "turned", "x_copied", "hi_done", "lo_done", "logits_done",
                                        "rows_done"))
        r = route(nc, io, sb, sem, pl, Wt, logits_done, tag)

        with nc.Block() as block:
            @block.sync
            def _(sp):
                sp.dma_start(gate[:, :, :], io[f"{tag}_gate"]).then_inc(gate_in, 16)
                r["sync"](sp)

            @block.vector
            def _(dve):
                def emit(b, i, k):
                    if not (isinstance(b, int) and b < 2):
                        dve.wait_ge(turned, b - 1)
                    ln_vector(dve, ls, b, lambda t: res[:, bass.ds(b * TPB + t, 1), :].rearrange(
                        "p a d -> p (a d)"), st, mv, ve, rs, lambda t: xh[:, k, t, :])

                for_batches(dve, emit)
                r["vector"](dve)

            @block.gpsimd
            def _(pool):
                r["gpsimd_first"](pool)
                for k in range(2):
                    pool.memset(ahead[:, k:k + 1], 0.0).then_inc(lo_done, 1)
                with pool.Fori(0, B // 2) as i:
                    for k in range(2):
                        b = 2 * i + k
                        pool.wait_ge(hi_done, b + 1)
                        for c in range(DC):
                            ins = pool.tensor_tensor(XH[:, LO, c, bass.ds(b * S, S)], xs[:, k, c, :],
                                                     XH[:, HI, c, bass.ds(b * S, S)].bitcast(F32), ALU.subtract)
                        ins.then_inc(lo_done, 1)

            @block.scalar
            def _(act):
                for k in range(2):
                    act.copy(ahead[:, 2 + k:3 + k], ident[:, 0:1]).then_inc(x_copied, 1)

                def emit(b, i, k):
                    if not (isinstance(b, int) and b == B - 1):
                        ln_scalar(act, ls, b + 1, ve)
                    act.wait_ge(turned, b + 1)
                    if rows is not None:
                        act.copy(rows[:, bass.ds(b * TPB, TPB), :], xh[:, k, :, :]).then_inc(rows_done, 1)
                    act.wait_ge(lo_done, b + 1)
                    act.wait_ge(logits_done, b + 1)
                    act.copy(xs[:, k, :, :], px[k][:, :, :]).then_inc(x_copied, 1)
                    act.wait_ge(x_copied, b + 3)
                    act.copy(XH[:, HI, :, bass.ds(b * S, S)], xs[:, k, :, :]).then_inc(hi_done, 1)

                ln_scalar(act, ls, 0, ve)
                for_batches(act, emit)
                r["scalar"](act)

            @block.tensor
            def _(pe):
                pe.wait_ge(gate_in, 16)
                for k in range(2):
                    pe.matmul(px[k][0:E, 0, 0:E], gate[:, 0, :], gate[:, 0, :], start=True,
                              stop=True).then_inc(logits_done, 1)
                pe.wait_ge(logits_done, 2)

                def turn(b, k):
                    pe.wait_ge(ls["xhat"], TPB * (b + 1))
                    pe.wait_ge(x_copied, b + 1)
                    for t in range(TPB):
                        for c in range(DC):
                            last = pe.transpose(px[k][:, c, t * P:(t + 1) * P],
                                                xh[:, k, t, c * P:(c + 1) * P], ident[:, :])
                    last.then_inc(turned, 1)

                def emit(b, i, k):
                    if not (isinstance(b, int) and b == B - 1):
                        turn(b + 1, 1 - k)
                    pe.wait_ge(x_copied, b + 3)
                    for t in range(TPB):
                        for c in range(DC):
                            last = pe.matmul(pl[:, bass.ds(b * TPB + t, 1), :], xs[:, k, c, t * P:(t + 1) * P],
                                             gate[:, c, :], start=(c == 0), stop=(c == DC - 1))
                    last.then_inc(logits_done, 1)

                turn(0, 0)
                for_batches(pe, emit)


def over(a, n, axis):
    if axis == "last":
        return a.rearrange("p (m o) -> p m o", o=1).to_broadcast([P, a.shape[1], n])
    return a.rearrange("p (o m) -> p o m", o=1).to_broadcast([P, n, a.shape[1]])


def chosen(dve, c, v, E, top, beats, rank, sel):
    v3, r3 = (x.rearrange("p (g e) -> p g e", e=E) for x in (v, rank))
    for e in range(E):
        n = c.done(dve.memset(r3[:, :, e:e + 1], float(E - 1 - e)))
    G = v3.shape[1]
    for d in range(1, E):
        b3 = beats[d % 2][:, 0:G * (E - d)].rearrange("p (g e) -> p g e", e=E - d)
        m = c.done(dve.tensor_tensor(b3, v3[:, :, 0:E - d], v3[:, :, d:E], ALU.is_ge))
        dve.wait_ge(c.sem, m)
        n = c.done(dve.tensor_tensor(r3[:, :, d:E], r3[:, :, d:E], b3, ALU.add))
        dve.wait_ge(c.sem, n)
        n = c.done(dve.tensor_tensor(r3[:, :, 0:E - d], r3[:, :, 0:E - d], b3, ALU.subtract))
        if d == E - 1:
            dve.wait_ge(c.sem, n)
    n = c.done(dve.tensor_scalar(sel, rank, float(top) - 0.5, None, ALU.is_lt))
    dve.wait_ge(c.sem, n)


def weigh(dve, c, scores, sel, E, tot, Wt, shared):
    n = c.done(dve.tensor_tensor(sel, scores, sel, ALU.mult))
    dve.wait_ge(c.sem, n)
    n = c.done(dve.tensor_reduce(tot, sel.rearrange("p (t e) -> p t e", e=E), AX.X, ALU.add))
    dve.wait_ge(c.sem, n)
    n = c.done(dve.tensor_scalar(tot, tot, 1e-20, None, ALU.add))
    dve.wait_ge(c.sem, n)
    n = c.done(dve.reciprocal(tot, tot))
    dve.wait_ge(c.sem, n)
    n = c.done(dve.tensor_scalar(tot, tot, ROUTE_SCALE, None, ALU.mult))
    dve.wait_ge(c.sem, n)
    c.done(dve.memset(Wt[:, :, E:E + shared], 1.0))
    n = c.done(dve.tensor_tensor(Wt[:, :, 0:E], sel.rearrange("p (t e) -> p t e", e=E), over(tot, E, "last"),
                                 ALU.mult))
    dve.wait_ge(c.sem, n)


def route0(nc, io, sb, sem, pl, Wt, logits_done, tag):
    sg, ch, sel, rank = (sb(f"{tag}_{n}", [P, NT * E0]) for n in ("sg", "ch", "sel", "rank"))
    pairs = sb(f"{tag}_pairs", [P, NT * G0, 6])
    gs, gsel, grank = (sb(f"{tag}_{n}", [P, NT * G0]) for n in ("gs", "gsel", "grank"))
    beats = [sb(f"{tag}_beats{k}", [P, NT * E0]) for k in range(2)]
    tot = sb(f"{tag}_tot", [P, NT])
    ebias = sb(f"{tag}_ebias", [P, E0])
    bias_in, scored, steps = (sem(f"{tag}_{n}") for n in ("bias_in", "scored", "steps"))

    def sync(sp):
        sp.dma_start(ebias[:, :], io["ebias"].partition_broadcast(P)).then_inc(bias_in, 16)

    def gpsimd_first(pool):
        pass

    def scalar(act):
        act.wait_ge(logits_done, B + 2)
        act.activation(sg[:, :], pl[:, :, :].rearrange("p t e -> p (t e)"), ACT.Sigmoid).then_inc(scored, 1)

    def vector(dve):
        c = Counted(steps)
        dve.wait_ge(scored, 1)
        dve.wait_ge(bias_in, 16)
        n = c.done(dve.tensor_tensor(ch[:, :].rearrange("p (t e) -> p t e", e=E0),
                                     sg[:, :].rearrange("p (t e) -> p t e", e=E0), over(ebias[:, :], NT, "ahead"),
                                     ALU.add))
        dve.wait_ge(c.sem, n)
        g = ch[:, :].rearrange("p (g e) -> p g e", e=PG0)
        c.done(dve.tensor_tensor(pairs[:, :, 0:3], g[:, :, 0:3], g[:, :, 1:4], ALU.add))
        c.done(dve.tensor_tensor(pairs[:, :, 3:5], g[:, :, 0:2], g[:, :, 2:4], ALU.add))
        n = c.done(dve.tensor_tensor(pairs[:, :, 5:6], g[:, :, 0:1], g[:, :, 3:4], ALU.add))
        dve.wait_ge(c.sem, n)
        n = c.done(dve.tensor_reduce(gs[:, :], pairs[:, :, :], AX.X, ALU.max))
        dve.wait_ge(c.sem, n)
        chosen(dve, c, gs[:, :], G0, TOPG0, beats, grank[:, :], gsel[:, :])
        n = c.done(dve.tensor_tensor(g, g, over(gsel[:, :], PG0, "last"), ALU.mult))
        dve.wait_ge(c.sem, n)
        chosen(dve, c, ch[:, :], E0, TOPK0, beats, rank[:, :], sel[:, :])
        weigh(dve, c, sg[:, :], sel[:, :], E0, tot[:, :], Wt, 1)

    return {"sync": sync, "gpsimd_first": gpsimd_first, "scalar": scalar, "vector": vector}


class Nothing:
    def sync(self, sp, added, n):
        pass

    def gpsimd(self, pool, u):
        pass

    def vector(self, dve, u, added, n):
        pass

    def before_add(self, dve):
        pass

    def at_end(self, pool):
        pass


def moe_experts(nc, io, res, ident, XH, Wt, tag, NX, F, source=None, skip=0, column=0, beside=Nothing()):
    source = source or tag
    fch = [(f, min(P, F - f)) for f in range(0, F, P)]
    NF = len(fch)
    UPE = B * NF
    GU = 2 * DC * F
    whole = F // P
    nsplit = 2 if F % P else 1
    AHEAD = 2
    with ExitStack() as ctx:
        sb, ps, sem = scope(nc, ctx)
        raw_gu = sb(f"{tag}_raw_gu", [P, GU])
        raw_d = sb(f"{tag}_raw_d", [P, NF, D])
        Wgu = [sb(f"{tag}_Wgu{k}", [P, 2, GU], F32R) for k in range(2)]
        Wd = [sb(f"{tag}_Wd{k}", [P, 2, NF, D], F32R) for k in range(2)]
        sl = sb(f"{tag}_sl", [P, 2, S])
        hf = sb(f"{tag}_hf", [P, 2, S])
        hs = sb(f"{tag}_hs", [P, 2, 2, S], F32R)
        ahead = sb(f"{tag}_ahead", [P, 16])
        pG = [ps(f"{tag}_pG{k}", [P, S]) for k in range(2)]
        pU = [ps(f"{tag}_pU{k}", [P, S]) for k in range(2)]
        pY = [ps(f"{tag}_pY{k}", [P, TPB, D]) for k in range(2)]
        (raw_gu_in, raw_d_in, w_hi, w_lo, gu_done, silu_done, mult_done, hi_done, lo_done, d_done, added) = (
            sem(f"{tag}_{n}") for n in ("raw_gu_in", "raw_d_in", "w_hi", "w_lo", "gu_done", "silu_done",
                                        "mult_done", "hi_done", "lo_done", "d_done", "added"))
        NW = 1 + nsplit

        def pieces(e2):
            k = e2 % 2
            yield Wgu[k][:, :, :], raw_gu[:, :]
            if whole:
                yield (Wd[k][:, :, 0:whole, :].rearrange("p a f d -> p a (f d)"),
                       raw_d[:, 0:whole, :].rearrange("p f d -> p (f d)"))
            if F % P:
                yield Wd[k][0:F % P, :, whole, :], raw_d[0:F % P, whole, :]

        tail = NX % 2 or 2
        loops = (NX - tail) // 2

        def for_units(eng, emit):
            if loops:
                with eng.Fori(0, loops) as i:
                    for j in range(2):
                        for u in range(UPE):
                            emit(2 * i + j, j, u, False)
            for j in range(tail):
                for u in range(UPE):
                    emit(NX - tail + j, j, u, j == tail - 1 and u == UPE - 1)

        with nc.Block() as block:
            @block.sync
            def _(sp):
                def load(e, first=False):
                    if not first:
                        sp.wait_ge(w_lo, NW * e)
                    sp.dma_start(raw_gu[:, :], io[f"{source}_gu"][bass.ds(e + skip, 1)].rearrange("a p n -> (a p) n")
                                 ).then_inc(raw_gu_in, 16)
                    if whole:
                        sp.dma_start(raw_d[:, 0:whole, :],
                                     io[f"{source}_d"][bass.ds(e + skip, 1), 0:whole * P].rearrange(
                                         "a (f p) d -> p (a f) d", p=P)).then_inc(raw_d_in, 16)
                    if F % P:
                        sp.dma_start(raw_d[0:F % P, whole:whole + 1, :], io[f"{source}_d"][
                            bass.ds(e + skip, 1), whole * P:F].rearrange("a p d -> p a d")).then_inc(raw_d_in, 16)

                load(0, True)
                if NX > 1:
                    with sp.Fori(1, NX) as e:
                        load(e)
                beside.sync(sp, added, 2 * TPB)

            def next_pair(e, j, u):
                return (e + 1, (j + 1) % 2, 0) if u == UPE - 1 else (e, j, u + 1)

            @block.tensor
            def _(pe):
                def gate_up(e, j, u):
                    n, f = divmod(u, NF)
                    f0, fw = fch[f]
                    U = e * UPE + u
                    if u == 0:
                        pe.wait_ge(w_lo, NW * e + 1)
                    pe.wait_ge(mult_done, U + 1)
                    for g, out in enumerate((pG, pU)):
                        start = True
                        for k in range(DC):
                            for wp, xp in PASSES:
                                lhsT = Wgu[j][:, wp, (g * DC + k) * F + f0:(g * DC + k) * F + f0 + fw]
                                last = pe.matmul(out[u % 2][0:fw, :], lhsT, XH[:, xp, k, n * S:(n + 1) * S],
                                                 start=start, stop=(k == DC - 1 and (wp, xp) == PASSES[-1]))
                                start = False
                    last.then_inc(gu_done, 1)

                def down(e, j, u):
                    n, f = divmod(u, NF)
                    f0, fw = fch[f]
                    U = e * UPE + u
                    if u == 0:
                        pe.wait_ge(w_lo, NW * (e + 1))
                    pe.wait_ge(lo_done, U + 1 + AHEAD)
                    if f == 0:
                        pe.wait_ge(added, TPB * (e * B + n) + TPB)
                    for t in range(TPB):
                        for m, (hp, wp) in enumerate(PASSES):
                            last = pe.matmul(pY[n % 2][:, t, :], hs[0:fw, u % 2, hp, t * P:(t + 1) * P],
                                             Wd[j][0:fw, wp, f, :],
                                             start=(f == 0 and m == 0 and t % 2 == 0),
                                             stop=(f == NF - 1 and m == len(PASSES) - 1),
                                             skip_group_check=True)
                    last.then_inc(d_done, 1)

                for k in range(2):
                    pe.matmul(pY[k][:, 0, 0:P], ident[:, :], ident[:, :], start=True, stop=True).then_inc(d_done, 1)
                pe.wait_ge(d_done, 2)
                gate_up(0, 0, 0)

                def emit(e, j, u, last):
                    if not last:
                        gate_up(*next_pair(e, j, u))
                    down(e, j, u)
                for_units(pe, emit)

            @block.scalar
            def _(act):
                def split(e, j):
                    act.wait_ge(d_done, e * UPE - UPE + AHEAD if not isinstance(e, int) or e > 1 else AHEAD)
                    act.wait_ge(raw_gu_in, 16 * (e + 1))
                    for m, (out, raw) in enumerate(pieces(j)):
                        if m == 1:
                            act.wait_ge(raw_d_in, 16 * nsplit * (e + 1))
                        act.copy(out[:, HI, :], raw).then_inc(w_hi, 1)

                split(0, 0)

                def emit(e, j, u, last):
                    n, f = divmod(u, NF)
                    fw = fch[f][1]
                    U = e * UPE + u
                    act.wait_ge(gu_done, U + 1)
                    act.wait_ge(mult_done, U + 1)
                    act.activation(sl[0:fw, u % 2, :], pG[u % 2][0:fw, :], ACT.Silu).then_inc(silu_done, 1)
                    act.wait_ge(mult_done, U + 1 + AHEAD)
                    act.wait_ge(d_done, U + 1)
                    act.copy(hs[0:fw, u % 2, HI, :], hf[0:fw, u % 2, :]).then_inc(hi_done, 1)
                    if u == 1 and not (isinstance(e, int) and e == NX - 1):
                        split(e + 1, (j + 1) % 2)
                for_units(act, emit)

            @block.gpsimd
            def _(pool):
                for k in range(AHEAD):
                    pool.memset(ahead[:, k:k + 1], 0.0).then_inc(lo_done, 1)

                def split(e, j):
                    for m, (out, raw) in enumerate(pieces(j)):
                        pool.wait_ge(w_hi, NW * e + m + 1)
                        pool.tensor_tensor(out[:, LO, :], raw, out[:, HI, :].bitcast(F32), ALU.subtract
                                           ).then_inc(w_lo, 1)

                split(0, 0)

                def emit(e, j, u, last):
                    n, f = divmod(u, NF)
                    fw = fch[f][1]
                    U = e * UPE + u
                    pool.wait_ge(hi_done, U + 1)
                    pool.tensor_tensor(hs[0:fw, u % 2, LO, :], hf[0:fw, u % 2, :],
                                       hs[0:fw, u % 2, HI, :].bitcast(F32), ALU.subtract).then_inc(lo_done, 1)
                    if u == 1 and not (isinstance(e, int) and e == NX - 1):
                        split(e + 1, (j + 1) % 2)
                    beside.gpsimd(pool, u)
                for_units(pool, emit)
                beside.at_end(pool)

            @block.vector
            def _(dve):
                for k in range(AHEAD):
                    dve.memset(ahead[:, 2 + k:3 + k], 0.0).then_inc(mult_done, 1)
                for k in range(2 * TPB):
                    dve.memset(ahead[:, 4 + k:5 + k], 0.0).then_inc(added, 1)

                def mult(e, j, u):
                    n, f = divmod(u, NF)
                    fw = fch[f][1]
                    U = e * UPE + u
                    dve.wait_ge(silu_done, U + 1)
                    dve.wait_ge(lo_done, U + 1)
                    dve.tensor_tensor(hf[0:fw, u % 2, :], sl[0:fw, u % 2, :], pU[u % 2][0:fw, :], ALU.mult
                                      ).then_inc(mult_done, 1)

                def add(e, n):
                    dve.wait_ge(d_done, e * UPE + NF * (n + 1) + AHEAD)
                    dve.wait_ge(added, TPB * (e * B + n) + 2 * TPB)
                    beside.before_add(dve)
                    for t in range(TPB):
                        tile = n * TPB + t
                        dve.scalar_tensor_tensor(res[:, tile, :], pY[n % 2][:, t, :],
                                                 Wt[:, tile, bass.ds(e + column, 1)], res[:, tile, :], ALU.mult,
                                                 ALU.add).then_inc(added, 1)

                mult(0, 0, 0)

                def emit(e, j, u, last):
                    if not last:
                        mult(*next_pair(e, j, u))
                    if u % NF == NF - 1:
                        add(e, u // NF)
                    beside.vector(dve, u, added, TPB * (e * B + (u + 1) // NF) + 2 * TPB)
                for_units(dve, emit)


def layer0_ffn(nc, io, res, ident):
    with ExitStack() as ctx:
        sb, ps, sem = scope(nc, ctx)
        Wt = sb("m0_Wt", [P, NT, N0])
        XH = sb("m0_XH", [P, 2, DC, B * S], F32R)
        moe_routes(nc, io, res, ident, XH, Wt, "m0", E0, route0)
        moe_experts(nc, io, res, ident, XH, Wt, "e0", N0, I0)


def route1(nc, io, sb, sem, pl, Wt, logits_done, tag, picked, slots_dram):
    zeros = sb(f"{tag}_zeros", [P, D])
    zeros_ready, slots_cleared = sem(f"{tag}_zeros_ready"), sem(f"{tag}_slots_cleared")
    lg, sel, rank = (sb(f"{tag}_{n}", [P, NT * E1]) for n in ("lg", "sel", "rank"))
    beats = [sb(f"{tag}_beats{k}", [P, NT * E1]) for k in range(2)]
    tot = sb(f"{tag}_tot", [P, NT])
    shifted, exp_done, steps = (sem(f"{tag}_{n}") for n in ("shifted", "exp_done", "steps"))

    def sync(sp):
        sp.wait_ge(zeros_ready, 1)
        sp.dma_start(slots_dram.rearrange("(n p) d -> p n d", p=P),
                     zeros[:, :].rearrange("p (o d) -> p o d", o=1).to_broadcast([P, NBLK, D])
                     ).then_inc(slots_cleared, 16)
        sp.wait_ge(slots_cleared, 16)

    def gpsimd_first(pool):
        pool.memset(zeros[:, :], 0.0).then_inc(zeros_ready, 1)

    def scalar(act):
        act.wait_ge(shifted, 1)
        act.activation(lg[:, :], lg[:, :], ACT.Exp).then_inc(exp_done, 1)

    def vector(dve):
        c = Counted(steps)
        by_token = lg[:, :].rearrange("p (t e) -> p t e", e=E1)
        dve.wait_ge(logits_done, B + 2)
        n = c.done(dve.tensor_reduce(tot[:, :], pl[:, :, :], AX.X, ALU.max))
        dve.wait_ge(c.sem, n)
        dve.tensor_tensor(by_token, pl[:, :, :], over(tot[:, :], E1, "last"), ALU.subtract).then_inc(shifted, 1)
        dve.wait_ge(exp_done, 1)
        n = c.done(dve.tensor_reduce(tot[:, :], by_token, AX.X, ALU.add))
        dve.wait_ge(c.sem, n)
        n = c.done(dve.reciprocal(tot[:, :], tot[:, :]))
        dve.wait_ge(c.sem, n)
        n = c.done(dve.tensor_tensor(by_token, by_token, over(tot[:, :], E1, "last"), ALU.mult))
        dve.wait_ge(c.sem, n)
        chosen(dve, c, lg[:, :], E1, TOPK1, beats, rank[:, :], sel[:, :])
        c.done(dve.tensor_copy(picked[:, :], sel[:, :]))
        weigh(dve, c, lg[:, :], sel[:, :], E1, tot[:, :], Wt, NS1)

    return {"sync": sync, "gpsimd_first": gpsimd_first, "scalar": scalar, "vector": vector}


def prefix(dve, c, a, b, n, part):
    d = 1
    while d < n:
        c.done(dve.tensor_copy(part(b, 0, d), part(a, 0, d)))
        m = c.done(dve.tensor_tensor(part(b, d, n), part(a, d, n), part(a, 0, n - d), ALU.add))
        dve.wait_ge(c.sem, m)
        a, b, d = b, a, 2 * d
    return a


def layer1_plan(nc, picked, Wt, slot, wk, bexp):
    TE = NT * E1
    with ExitStack() as ctx:
        sb, ps, sem = scope(nc, ctx)
        upper = sb("s_upper", [P, P])
        ones = sb("s_ones", [P, P])
        order_i = sb("s_order_i", [P, NBLK], mybir.dt.int32)
        order_f = sb("s_order_f", [P, NBLK])
        thr = sb("s_thr", [P, NT])
        tot, run, run2, place, mk = (sb(f"s_{n}", [P, TE]) for n in ("tot", "run", "run2", "place", "mk"))
        more = mk[:, :].rearrange("p (e j) -> p e j", j=NT)
        cnt, cnt2, mw = run, run2, tot
        nblk, bs, bs2, start = (sb(f"s_{n}", [P, E1]) for n in ("nblk", "bs", "bs2", "start"))
        bf = sb("s_bf", [P, NBLK])
        slot_f = sb("s_slot_f", [P, TOPK1, NT])
        p_pre = ps("s_p_pre", [P, TE])
        p_tot = ps("s_p_tot", [P, TE])
        consts, counted, steps = (sem(f"s_{n}") for n in ("consts", "counted", "steps"))
        v3 = lambda a: a[:, :].rearrange("p (t e) -> p t e", e=E1)

        with nc.Block() as block:
            @block.gpsimd
            def _(pool):
                pool.iota(order_i[:, :], [[1, NBLK]], base=0, channel_multiplier=0).then_inc(consts, 1)
                pool.memset(ones[:, :], 1.0).then_inc(consts, 1)
                pool.memset(upper[:, :], 1.0).then_inc(consts, 1)
                pool.wait_ge(consts, 3)
                pool.affine_select(out=upper[:, :], in_=upper[:, :], compare_op=ALU.is_ge, fill=0.0, base=-1,
                                   pattern=[[1, P]], channel_multiplier=-1).then_inc(consts, 1)

            @block.tensor
            def _(pe):
                pe.wait_ge(consts, 4)
                pe.matmul(p_pre[:, :], upper[:, :], picked[:, :], start=True, stop=True).then_inc(counted, 1)
                pe.matmul(p_tot[:, :], ones[:, :], picked[:, :], start=True, stop=True).then_inc(counted, 1)

            @block.vector
            def _(dve):
                c = Counted(steps)
                step = lambda ins: dve.wait_ge(c.sem, c.done(ins))
                dve.wait_ge(consts, 4)
                step(dve.tensor_copy(order_f[:, :], order_i[:, :]))
                step(dve.tensor_scalar(thr[:, :], order_f[:, 0:NT], float(P), None, ALU.mult))
                dve.wait_ge(counted, 2)
                step(dve.tensor_copy(tot[:, :], p_tot[:, :]))
                c.done(dve.tensor_tensor(place[:, :], p_pre[:, :], tot[:, :], ALU.subtract))
                step(dve.tensor_copy(run[:, :], tot[:, :]))
                r = prefix(dve, c, run, run2, NT, lambda a, i, j: v3(a)[:, i:j, :])
                step(dve.tensor_tensor(place[:, :], place[:, :], r[:, :], ALU.add))
                total = v3(r)[:, NT - 1, :]
                step(dve.tensor_tensor(more, over(total, NT, "last"), over(thr[:, :], E1, "ahead"), ALU.is_gt))
                step(dve.tensor_reduce(nblk[:, :], more, AX.X, ALU.add))
                step(dve.tensor_copy(bs[:, :], nblk[:, :]))
                e_ = prefix(dve, c, bs, bs2, E1, lambda a, i, j: a[:, i:j])
                step(dve.tensor_tensor(start[:, :], e_[:, :], nblk[:, :], ALU.subtract))
                step(dve.tensor_scalar(start[:, :], start[:, :], float(P), None, ALU.mult))
                step(dve.tensor_tensor(v3(place), v3(place), over(start[:, :], NT, "ahead"), ALU.add))
                step(dve.tensor_scalar(bf[:, :], order_f[:, :], e_[:, 0:1], None, ALU.is_ge))
                for e in range(1, E1):
                    step(dve.scalar_tensor_tensor(bf[:, :], order_f[:, :], e_[:, e:e + 1], bf[:, :], ALU.is_ge,
                                                  ALU.add))
                step(dve.tensor_scalar(bf[:, :], bf[:, :], float(E1 - 1), None, ALU.min))
                step(dve.tensor_copy(bexp[:, :], bf[:, :]))
                step(dve.tensor_copy(cnt[:, :], picked[:, :]))
                n_ = prefix(dve, c, cnt, cnt2, E1, lambda a, i, j: v3(a)[:, :, i:j])
                for k in range(TOPK1):
                    step(dve.tensor_scalar(mk[:, :], n_[:, :], float(k + 1), None, ALU.is_equal))
                    step(dve.tensor_tensor(mk[:, :], mk[:, :], picked[:, :], ALU.mult))
                    c.done(dve.tensor_tensor(v3(mw), v3(mk), Wt[:, :, 0:E1], ALU.mult))
                    step(dve.tensor_tensor(mk[:, :], mk[:, :], place[:, :], ALU.mult))
                    c.done(dve.tensor_reduce(wk[:, k, :], v3(mw), AX.X, ALU.add))
                    step(dve.tensor_reduce(slot_f[:, k, :], v3(mk), AX.X, ALU.add))
                dve.tensor_copy(slot[:, :, :], slot_f[:, :, :])


class Dispatch(Nothing):

    def __init__(self, sem, rows, slot, xslots):
        self.rows, self.slot, self.xslots, self.sent = rows, slot, xslots, 0
        self.scattered = sem("s_scattered")

    def gpsimd(self, pool, u):
        for _ in range(min(3, NT * TOPK1 - self.sent)):
            t, k = divmod(self.sent, TOPK1)
            pool.indirect_dma_start(self.xslots, bass.IndirectOffsetOnAxis(self.slot[:, k, t:t + 1], 0),
                                    self.rows[:, t, :], None).then_inc(self.scattered, 16)
            self.sent += 1

    def at_end(self, pool):
        assert self.sent == NT * TOPK1
        pool.wait_ge(self.scattered, 16 * self.sent)


class Combine(Nothing):
    NBUF = 12

    def __init__(self, sb, sem, res, slot, wk, yslots, out):
        self.out, self.stored = out, sem("g_stored")
        self.res, self.slot, self.wk, self.yslots = res, slot, wk, yslots
        self.asked = self.summed = 0
        self.got = sb("g_got", [P, self.NBUF, D])
        self.fetched = [sem(f"g_fetched{k}") for k in range(self.NBUF)]
        self.weighed = sem("g_weighed")

    def sync(self, sp, added, n):
        for b in range(B):
            sp.wait_ge(added, n + TPB * (b + 1))
            sp.wait_ge(self.weighed, TPB * TOPK1 * (b + 1))
            sp.dma_start(self.out[b].rearrange("(t p) d -> p t d", p=P), self.res[:, b * TPB:(b + 1) * TPB, :]
                         ).then_inc(self.stored, 16)
        sp.wait_ge(self.stored, 16 * B)

    def gpsimd(self, pool, u):
        for _ in range(min(3, NT * TOPK1 - self.asked)):
            n = self.asked
            t, k = divmod(n, TOPK1)
            if n >= self.NBUF:
                pool.wait_ge(self.weighed, n - self.NBUF + 1)
            pool.indirect_dma_start(self.got[:, n % self.NBUF, :], None, self.yslots,
                                    bass.IndirectOffsetOnAxis(self.slot[:, k, t:t + 1], 0)
                                    ).then_inc(self.fetched[n % self.NBUF], 16)
            self.asked += 1

    def vector(self, dve, u, added, n_added):
        if u:
            dve.wait_ge(added, n_added)
            self.add(dve, min(3 * u, NT * TOPK1))
        if u == B * len(FCH1) - 1:
            self.add(dve, NT * TOPK1)

    def add(self, dve, upto):
        while self.summed < upto:
            n = self.summed
            t, k = divmod(n, TOPK1)
            dve.wait_ge(self.fetched[n % self.NBUF], 16 * (n // self.NBUF + 1))
            if k:
                dve.wait_ge(self.weighed, n)
            dve.scalar_tensor_tensor(self.res[:, t, :], self.got[:, n % self.NBUF, :], self.wk[:, k, t:t + 1],
                                     self.res[:, t, :], ALU.mult, ALU.add).then_inc(self.weighed, 1)
            self.summed += 1

    def before_add(self, dve):
        if self.summed:
            dve.wait_ge(self.weighed, self.summed)


def layer1_blocks(nc, io, ident, bexp, xslots, yslots):
    with ExitStack() as ctx:
        sb, ps, sem = scope(nc, ctx)
        wgu = sb("b_wgu", [P, E1, 2 * DC, F1])
        wd = sb("b_wd", [P, E1, len(FCH1), D])
        x = sb("b_x", [P, 2, D])
        xT = sb("b_xT", [P, 2, DC, P])
        sg = sb("b_sg", [P, 2, F1])
        h = sb("b_h", [P, 2, F1])
        hT = sb("b_hT", [P, 2, len(FCH1), P])
        y = sb("b_y", [P, 2, D])
        pG, pU, pH = ([ps(f"b_{n}{k}", [P, w]) for k in range(2)] for n, w in (("pG", F1), ("pU", F1), ("pH", 3 * P)))
        pX = ps("b_pX", [P, DC * P])
        pY = ps("b_pY", [P, D])
        x_turned, x_ready, gu_done, silu_done, h_ready, h_turned, hT_ready, y_done, y_ready = (
            sem(f"b_{n}") for n in ("x_turned", "x_ready", "gu_done", "silu_done", "h_ready", "h_turned", "hT_ready",
                                    "y_done", "y_ready"))
        x_in, y_out = ([sem(f"b_{n}{k}") for k in range(2)] for n in ("x_in", "y_out"))
        w_in = [sem(f"b_w_in{e}") for e in range(E1)]
        w_ready = sem("b_w_ready")
        told = sb("b_told", [P, E1])
        PEEL = 4

        def for_blocks(eng, emit):
            loops = (NBLK - 2 - PEEL) // 2
            for j in range(PEEL):
                emit(j, j // 2, j % 2)
            with eng.Fori(0, loops) as i:
                for k in range(2):
                    emit(2 * i + (PEEL + k), i + PEEL // 2, k)
            for j in range(PEEL + 2 * loops, NBLK + 2):
                emit(j, j // 2, j % 2)

        def within(j, lo, hi):
            return not isinstance(j, int) or lo <= j <= hi

        with nc.Block() as block:
            @block.sync
            def _(sp):
                def load(j, k):
                    sp.dma_start(x[:, k, :], xslots[bass.ds(j * P, P), :]).then_inc(x_in[k], 16)

                load(0, 0)
                load(1, 1)

                def emit(j, i, k):
                    if within(j, 0, NBLK - 3):
                        sp.wait_ge(x_turned, j + 1)
                        load(j + 2, k)
                    if within(j, 2, NBLK + 1):
                        sp.wait_ge(y_ready, j - 1)
                        sp.dma_start(yslots[bass.ds(j * P - 2 * P, P), :], y[:, k, :]).then_inc(y_out[k], 16)
                for_blocks(sp, emit)
                for k in range(2):
                    sp.wait_ge(y_out[k], 16 * ((NBLK + 1 - k) // 2))

            @block.gpsimd
            def _(pool):
                for e in range(E1):
                    pool.wait_ge(w_in[e], 48)
                    pool.memset(told[:, e:e + 1], 0.0).then_inc(w_ready, 1)

            @block.tensor
            def _(pe):
                def turn_x(j, i, k):
                    pe.wait_ge(x_in[k], 16 * i + 16)
                    if within(j, 1, NBLK):
                        pe.wait_ge(x_ready, j)
                    for c in range(DC):
                        last = pe.transpose(pX[:, c * P:(c + 1) * P], x[:, k, c * P:(c + 1) * P], ident[:, :])
                    last.then_inc(x_turned, 1)

                turn_x(0, 0, 0)

                def emit(j, i, k):
                    if within(j, 0, NBLK - 1):
                        e = pe.value_load(bexp[0:1, bass.ds(j, 1)], min_val=0, max_val=E1 - 1)
                        pe.wait_ge(w_ready, e + 1)
                        pe.wait_ge(x_ready, j + 1)
                        if within(j, 2, NBLK):
                            pe.wait_ge(h_ready, j - 1)
                        for g, out in enumerate((pG, pU)):
                            for c in range(DC):
                                last = pe.matmul(out[k][:, :], xT[:, k, c, :],
                                                 wgu[:, bass.ds(e, 1), g * DC + c, :].rearrange("p a f -> p (a f)"),
                                                 start=(c == 0), stop=(c == DC - 1))
                        last.then_inc(gu_done, 1)
                    if within(j, 1, NBLK):
                        pe.wait_ge(h_ready, j)
                        if within(j, 3, NBLK + 1):
                            pe.wait_ge(hT_ready, j - 2)
                        for f, (f0, fw) in enumerate(FCH1):
                            last = pe.transpose(pH[1 - k][0:fw, f * P:(f + 1) * P], h[:, 1 - k, f0:f0 + fw],
                                                ident[:, :])
                        last.then_inc(h_turned, 1)
                    if within(j, 0, NBLK - 2):
                        turn_x(j + 1, i + k, 1 - k)
                    if within(j, 2, NBLK + 1):
                        e = pe.value_load(bexp[0:1, bass.ds(j - 2, 1)], min_val=0, max_val=E1 - 1)
                        pe.wait_ge(hT_ready, j - 1)
                        if within(j, 3, NBLK + 1):
                            pe.wait_ge(y_ready, j - 2)
                        for f, (f0, fw) in enumerate(FCH1):
                            last = pe.matmul(pY[:, :], hT[0:fw, k, f, :],
                                             wd[0:fw, bass.ds(e, 1), f, :].rearrange("p a d -> p (a d)"),
                                             start=(f == 0), stop=(f == len(FCH1) - 1))
                        last.then_inc(y_done, 1)
                for_blocks(pe, emit)

            @block.scalar
            def _(act):
                for e in range(E1):
                    act.dma_start(wgu[:, e, :, :], io["r1_gu"][:, e]).then_inc(w_in[e], 16)
                    act.dma_start(wd[:, e, 0:2, :], io["r1_d"][e, 0:2 * P].rearrange("(f p) d -> p f d", p=P)
                                  ).then_inc(w_in[e], 16)
                    act.dma_start(wd[0:F1 - 2 * P, e, 2, :], io["r1_d"][e, 2 * P:F1]).then_inc(w_in[e], 16)

                def copy_x(j, k):
                    act.wait_ge(x_turned, j + 1)
                    act.copy(xT[:, k, :, :].rearrange("p c n -> p (c n)"), pX[:, :]).then_inc(x_ready, 1)

                copy_x(0, 0)

                def emit(j, i, k):
                    if within(j, 0, NBLK - 1):
                        act.wait_ge(gu_done, j + 1)
                        if within(j, 2, NBLK):
                            act.wait_ge(h_ready, j - 1)
                        act.activation(sg[:, k, :], pG[k][:, :], ACT.Silu).then_inc(silu_done, 1)
                    if within(j, 0, NBLK - 2):
                        copy_x(j + 1, 1 - k)
                    if within(j, 2, NBLK + 1):
                        act.wait_ge(y_done, j - 1)
                        if within(j, 4, NBLK + 1):
                            act.wait_ge(y_out[k], 16 * i - 16)
                        act.copy(y[:, k, :], pY[:, :]).then_inc(y_ready, 1)
                for_blocks(act, emit)

            @block.vector
            def _(dve):
                def emit(j, i, k):
                    if within(j, 0, NBLK - 1):
                        dve.wait_ge(silu_done, j + 1)
                        if within(j, 2, NBLK):
                            dve.wait_ge(h_turned, j - 1)
                        dve.tensor_tensor(h[:, k, :], sg[:, k, :], pU[k][:, :], ALU.mult).then_inc(h_ready, 1)
                    if within(j, 1, NBLK):
                        dve.wait_ge(h_turned, j)
                        if within(j, 3, NBLK + 1):
                            dve.wait_ge(y_done, j - 2)
                        w = FCH1[-1][1]
                        dve.tensor_copy(hT[:, 1 - k, 0:2, :].rearrange("p f n -> p (f n)"), pH[1 - k][:, 0:2 * P])
                        dve.tensor_copy(hT[0:w, 1 - k, 2, :], pH[1 - k][0:w, 2 * P:3 * P]).then_inc(hT_ready, 1)
                for_blocks(dve, emit)


def layer1_ffn(nc, io, res, ident):
    xslots = nc.dram_tensor("x_slots", (NBLK * P, D), F32, kind="Internal").ap()
    yslots = nc.dram_tensor("y_slots", (NBLK * P, D), F32, kind="Internal").ap()
    with ExitStack() as ctx:
        sb, ps, sem = scope(nc, ctx)
        Wt = sb("m1_Wt", [P, NT, E1 + NS1])
        XH = sb("m1_XH", [P, 2, DC, B * S], F32R)
        slot = sb("m1_slot", [P, TOPK1, NT], mybir.dt.uint32)
        wk = sb("m1_wk", [P, TOPK1, NT])
        bexp = sb("m1_bexp", [P, NBLK], mybir.dt.int32)
        with ExitStack() as inner:
            sb1, _, sem1 = scope(nc, inner)
            rows = sb1("m1_rows", [P, NT, D])
            picked = sb1("m1_picked", [P, NT * E1])
            moe_routes(nc, io, res, ident, XH, Wt, "m1", E1,
                       lambda *a: route1(*a, picked, xslots), rows)
            layer1_plan(nc, picked, Wt, slot, wk, bexp)
            moe_experts(nc, io, res, ident, XH, Wt, "ea", 1, F1, "e1", 0, E1, Dispatch(sem1, rows, slot, xslots))
        layer1_blocks(nc, io, ident, bexp, xslots, yslots)
        moe_experts(nc, io, res, ident, XH, Wt, "eb", 1, F1, "e1", 1, E1 + 1,
                    Combine(sb, sem, res, slot, wk, yslots, io["out"]))


def layer1_keys_in(nc, io, res, ident, kv, wsp, mb):
    with ExitStack() as ctx:
        sb, ps, sem = scope(nc, ctx)
        cin = sb("c_cin", [P, 2, TPB, D])
        xh = sb("c_xh", [P, 2, 2, TPB, D])
        st = sb("c_st", [P, 2, TPB, 6])
        mv = sb("c_mv", [P, 2, TPB, 2])
        ve = sb("c_ve", [P, 2, TPB])
        rs = sb("c_rs", [P, 2, TPB])
        gb = sb("c_gb", [P, 2, 2, DC])
        yf = sb("c_yf", [P, 2, 2, DC, S])
        ys = sb("c_ys", [P, 2, 2, 2, DC, S], F32R)
        wr = sb("c_wr", [P, 3, DC, INNER])
        wq = sb("c_wq", [P, 2, 3, DC, 256], F32R)
        m8 = sb("c_m8", [B, S], U8)
        mrow = sb("c_mrow", [B, KEYS], F32R)
        px = [[ps(f"c_px{k}{m}", [P, DC, S]) for m in range(2)] for k in range(2)]
        (gb_in, w_in, m_in, m_ready, stats, moments, var, sd, rstd, xhat, turned, y_done, y_hi, y_lo, wq_hi,
         wq_lo, wq_out, m_out) = (sem("c_" + n) for n in (
             "gb_in w_in m_in m_ready stats moments var sd rstd xhat turned y_done y_hi y_lo wq_hi wq_lo wq_out "
             "m_out").split())
        cin_s = [sem(f"c_cin_in{k}") for k in range(2)]
        kv_out = [sem(f"c_kv_out{k}") for k in range(2)]

        with nc.Block() as block:
            @block.sync
            def _(sp):
                def load(b, k):
                    hpt = P // KPH
                    src = io["ctx"][bass.ds(b, 1)].rearrange("b (j h) d -> (b h) j d", h=STRIDE)
                    for t in range(TPB):
                        sp.dma_start(cin[:, k, t, :], src[t * hpt:(t + 1) * hpt]).then_inc(cin_s[k], 16)

                load(0, 0)
                load(1, 1)
                sp.dma_start(gb[:, :, :, :], io["gb1"]).then_inc(gb_in, 16)

                def emit(b, i, k):
                    if not (isinstance(b, int) and b >= B - 2):
                        sp.wait_ge(xhat, 2 * TPB * (b + 1))
                        load(b + 2, k)
                    for m in range(2):
                        sp.wait_ge(y_lo, 2 * b + m + 1)
                        sp.dma_start(kv[bass.ds(b, 1), :, :, :, m * S:(m + 1) * S].rearrange(
                            "b p a c n -> p (b a) c n"), ys[:, k, m, :, :, :].bitcast(F32)).then_inc(kv_out[k], 16)

                for_batches(sp, emit)
                for k in range(2):
                    sp.wait_ge(kv_out[k], 32 * (B // 2))

            @block.gpsimd
            def _(pool):
                pool.dma_start(m8[:, :], io["mask"]).then_inc(m_in, 16)
                pool.wait_ge(m_in, 16)
                pool.memset(mrow[:, S:KEYS].bitcast(F32), 0.0).then_inc(m_ready, 1)
                pool.tensor_scalar(mrow[:, 0:S].rearrange("b (h j) -> b j h", j=KPH),
                                   m8[:, :].rearrange("b (j h) -> b j h", h=STRIDE), -1.0, MASKED, ALU.add, ALU.mult
                                   ).then_inc(m_ready, 1)
                pool.wait_ge(m_ready, 2)
                pool.dma_start(mb, mrow[:, :].bitcast(F32)).then_inc(m_out, 16)
                pool.wait_ge(w_in, 48)
                for q in range(NQUAD):
                    hi = wq[:, HI, :, :, :].rearrange("p w c n -> p (w c) n")
                    src = wr[:, :, :, q * 256:(q + 1) * 256].rearrange("p w c n -> p (w c) n")
                    if q:
                        pool.wait_ge(wq_out, 16 * q)
                    pool.tensor_copy(hi, src).then_inc(wq_hi, 1)
                    pool.wait_ge(wq_hi, q + 1)
                    pool.tensor_tensor(wq[:, LO, :, :, :].rearrange("p w c n -> p (w c) n"), src, hi.bitcast(F32),
                                       ALU.subtract).then_inc(wq_lo, 1)
                    pool.wait_ge(wq_lo, q + 1)
                    pool.dma_start(wsp[q].rearrange("p a w c n -> p (a w c n)"),
                                   wq[:, :, :, :, :].rearrange("p a w c n -> p (a w c n)").bitcast(F32)
                                   ).then_inc(wq_out, 16)
                pool.wait_ge(m_out, 16)
                pool.wait_ge(wq_out, 16 * NQUAD)

            @block.scalar
            def _(act):
                for m, n in enumerate("kvq"):
                    act.dma_start(wr[:, m, :, :], io[f"w{n}1"]).then_inc(w_in, 16)

                def root(b):
                    act.wait_ge(var, 2 * b + 2)
                    act.activation(ve[:, :, :], ve[:, :, :], ACT.Sqrt).then_inc(sd, 1)

                def emit(b, i, k):
                    if isinstance(b, int) and b == 0:
                        root(0)
                        act.wait_ge(gb_in, 16)
                    if not (isinstance(b, int) and b == B - 1):
                        root(b + 1)
                    if not (isinstance(i, int) and i == 0):
                        act.wait_ge(kv_out[k], 32 * i)
                    for m in range(2):
                        act.wait_ge(turned, 2 * b + m + 1)
                        for c in range(DC):
                            act.activation(yf[:, k, m, c, :], px[k][m][:, c, :], ACT.Identity,
                                           bias=gb[:, m, 1, c:c + 1], scale=gb[:, m, 0, c:c + 1]).then_inc(y_done, 1)
                        act.wait_ge(y_done, DC * (2 * b + m + 1))
                        act.copy(ys[:, k, m, HI, :, :], yf[:, k, m, :, :]).then_inc(y_hi, 1)

                for_batches(act, emit)

            @block.vector
            def _(dve):
                def normalise(b, i, k):
                    src = [lambda t: cin[:, k, t, :],
                           lambda t: res[:, bass.ds(b * TPB + t, 1), :].rearrange("p a d -> p (a d)")]
                    for m in (1, 0):
                        if m == 0:
                            dve.wait_ge(cin_s[k], 16 * TPB * (i + 1))
                        for t in range(TPB):
                            dve.bn_stats(st[:, m, t, :], src[m](t)).then_inc(stats, 1)
                    dve.wait_ge(stats, 2 * TPB * (b + 1))
                    dve.memset(rs[:, 0, 0:1], 0.0)
                    for m in range(2):
                        for t in range(TPB):
                            dve.bn_aggr(mv[:, m, t, :], st[:, m, t, :]).then_inc(moments, 1)
                    dve.wait_ge(moments, 2 * TPB * (b + 1))
                    dve.tensor_scalar(ve[:, 0, :], mv[:, 0, :, 1], EPS, None, ALU.add).then_inc(var, 1)
                    dve.tensor_scalar(ve[:, 1, :], mv[:, 1, :, 1], 1.0 + EPS, EPS * EPS, ALU.mult, ALU.add
                                      ).then_inc(var, 1)
                    dve.wait_ge(sd, b + 1)
                    dve.reciprocal(rs[:, :, :], ve[:, :, :]).then_inc(rstd, 1)
                    dve.wait_ge(rstd, b + 1)
                    if not (isinstance(b, int) and b < 2):
                        dve.wait_ge(turned, 2 * b - 2)
                    for m in range(2):
                        for t in range(TPB):
                            dve.tensor_scalar(xh[:, k, m, t, :], src[m](t), mv[:, m, t, 0:1], rs[:, m, t:t + 1],
                                              ALU.subtract, ALU.mult).then_inc(xhat, 1)

                def emit(b, i, k):
                    if isinstance(b, int) and b == 0:
                        normalise(0, 0, 0)
                    if not (isinstance(b, int) and b == B - 1):
                        normalise(b + 1, i + k, 1 - k)
                    for m in range(2):
                        dve.wait_ge(y_hi, 2 * b + m + 1)
                        dve.tensor_tensor(ys[:, k, m, LO, :, :], yf[:, k, m, :, :],
                                          ys[:, k, m, HI, :, :].bitcast(F32), ALU.subtract).then_inc(y_lo, 1)

                for_batches(dve, emit)

            @block.tensor
            def _(pe):
                def emit(b, i, k):
                    pe.wait_ge(xhat, 2 * TPB * (b + 1))
                    if not (isinstance(i, int) and i == 0):
                        pe.wait_ge(y_done, 2 * DC * (b - 1))
                    for m in range(2):
                        for t in range(TPB):
                            for c in range(DC):
                                last = pe.transpose(px[k][m][:, c, t * P:(t + 1) * P],
                                                    xh[:, k, m, t, c * P:(c + 1) * P], ident[:, :])
                        last.then_inc(turned, 1)

                for_batches(pe, emit)


WHOLE = (
    """M den ST0 Q r0 ST1 r1 ST2 r2 PV0 PV1 c2 r3 K0 c0 ST3 ST4 PV2 S0 S1 K1 S2 ST5 ST6 S3 Y0 S4 S5
       PV3 S6 c1 ST7 S7 S8 PV4 S9 S10 Y1 S11 PV5 S12 S13 PV6 S14 S15 N PV7 O""".split(),
    """den M Q r0 ST0 ST1 c2 PV0 r1 K0 r2 PV1 c0 ST2 ST3 S0 S1 K1 ST4 S2 S3 PV2 ST5 S4 V0 S5 c1 S6 PV3
       V1 r3 ST6 Y0 S7 S8 PV4 PV5 S9 PV6 S10 S11 V2 S12 ST7 S13 S14 V3 S15 N PV7 O Y1""".split())
SHARED = ("K0", "K1", "Q", "V0", "V1", "V2", "V3", "den", "Y0", "Y1")


class Step:

    def __init__(self, g, parity, by2, b=None, batch_half=None, off=None):
        self.g, self.parity, self.by2, self.b, self.batch_half, self.off = g, parity, by2, b, batch_half, off


NSTEP = B * NPAIR


def misc_uses(g0, parity):
    last = isinstance(g0, int) and g0 >= NSTEP - 1
    return [u for u in WHOLE[parity] if u in SHARED and not (g0 == 0 and u[0] in "dY")
            and not (last and u[0] in "KQV")]


PROLOGUE = ["Q", "K0", "K1", "V0", "V1", "V2", "V3"]


def use_before(st):
    if isinstance(st.g, int):
        if st.g == -1:
            return 0
        if st.g == 0:
            return len(PROLOGUE)
        if st.g == NSTEP:
            return 8 * (NSTEP - 1) + 2 + 3
    return 8 * st.g + (2 if st.parity else 4)


def uses_of(st):
    if isinstance(st.g, int):
        if st.g == -1:
            return PROLOGUE
        if st.g in (0, NSTEP - 1, NSTEP):
            return misc_uses(st.g, st.parity)
    return misc_uses(None, st.parity)


def use(st, name):
    return use_before(st) + uses_of(st).index(name) + 1


def order(st):
    if isinstance(st.g, int) and st.g == -1:
        return ([(u, 0) for u in PROLOGUE] + [("c", c) for c in (2, 0, 1)] +
                [("S", c) for c in range(4 * TPB)] + [("N", 0)])
    uses = uses_of(st)
    epilogue = isinstance(st.g, int) and st.g == NSTEP
    out = []
    for u in WHOLE[st.parity]:
        if u in SHARED:
            if u in uses:
                out.append((u, 0))
        elif u[:2] in ("ST", "PV"):
            if not epilogue:
                out.append((u[:2], int(u[2:])))
        elif u[0] == "r":
            if "den" in uses:
                out.append(("r", int(u[1:])))
        elif u[0] in "cSN":
            if "K0" in uses:
                out.append((u[0], int(u[1:] or 0)))
        elif not epilogue:
            out.append((u, 0))
    return out


def for_steps(eng, emit, unroll_halves=False):
    emit(Step(-1, 1, None))
    emit(Step(0, 0, 0, 0, 0, 0))

    def four(b, h):
        for off in range(1, 5):
            emit(Step(8 * b + 4 * h + off, off % 2, 4 * b + 2 * h + off // 2, b, h, off))

    with eng.Fori(0, B - 1) as b:
        if unroll_halves:
            four(b, 0)
            four(b, 1)
        else:
            with eng.Fori(0, 2) as h:
                four(b, h)
    four(B - 1, 0)
    for off in range(1, 4):
        emit(Step(NSTEP - 4 + off, off % 2, NSTEP // 2 - 2 + off // 2, B - 1, 1, off))
    emit(Step(NSTEP, 0, NSTEP // 2, B - 1, 1, 4))


def layer1_pairs(nc, io, res, ident, kv_d, wsp, mb):
    with ExitStack() as ctx:
        sb, ps, sem = scope(nc, ctx)
        kv = sb("d_kv", [P, 2, DC, KEYS], F32R)
        W = [sb(f"d_W{k}", [P, 2, 3, DC, 256], F32R) for k in range(2)]
        K1, K2 = ([[sb(f"d_{n}{j}{h}", [P, KEYS], F32R) for h in range(2)] for j in range(2)] for n in ("K1", "K2"))
        Q0, Q1, Q2 = ([[sb(f"d_{n}{j}{h}", [P, S], F32R) for h in range(2)] for j in range(2)]
                      for n in ("Q0", "Q1", "Q2"))
        V = [sb(f"d_V{k}", [P, NKT, 256]) for k in range(2)]
        pr = sb("d_pr", [P, 4, 2, S])
        acc = sb("d_acc", [P, 2, 2, S])
        osb = sb("d_osb", [P, 2, S])
        rb = sb("d_rb", [P, S])
        OT = sb("d_OT", [P, 2, S])
        Wo = sb("d_Wo", [P, NPAIR, D])
        nm2 = sb("d_nm2", [P, 2, 8, 2])
        nm = sb("d_nm", [P, 2, 8])
        ones = sb("d_ones", [P, HD1])
        onerow = sb("d_onerow", [1, KEYS], F32R)
        ahead = sb("d_ahead", [P, 8])
        pT = [ps(f"d_pT{k}", [P, 2, S]) for k in range(2)]
        pS = ps("d_pS", [P, 2, S])
        pO = ps("d_pO", [P, S])
        pm = ps("d_pm", [P, S])
        (set_up, set_rows, wo_in, kv_in, misc_done, misc_read, k_hi, q_hi, s_done, max_done, m_done, m_copied,
         st_done, exp_done, pv_done, acc_done, o_copied, ot_done, r_done) = (sem("d_" + n) for n in (
             "set_up set_rows wo_in kv_in misc_done misc_read k_hi q_hi s_done max_done m_done m_copied st_done "
             "exp_done pv_done acc_done o_copied ot_done r_done").split())
        w_in = [sem(f"d_w_in{k}") for k in range(2)]
        mask_in = [sem(f"d_mask_in{k}") for k in range(2)]
        copied = sem("d_copied")

        own = (slice(0, HD1), slice(HD1, P))
        other = (slice(HD1, P), slice(0, HD1))
        row0 = (HD1, 0)
        NCOPY = 8
        PT = 4

        def pair(st):
            if isinstance(st.g, int) and st.g == -1:
                return 0, 0, 0
            return (st.parity + 1) % 2, st.g + 1, st.by2 + (1 if st.parity else 0)

        with nc.Block() as block:
            @block.sync
            def _(sp):
                sp.dma_start(kv[:, :, :, :].bitcast(F32), kv_d[0]).then_inc(kv_in, 16)
                sp.dma_start(W[0][:, :, :, :, :].bitcast(F32), wsp[0]).then_inc(w_in[0], 16)
                sp.wait_ge(set_up, 14)
                for j in range(2):
                    for h in range(2):
                        sp.dma_start(K2[j][h][row0[h]:row0[h] + 1, :].bitcast(F32), onerow[:, :].bitcast(F32)
                                     ).then_inc(set_rows, 16)
                        for q in (Q0, Q2):
                            sp.dma_start(q[j][h][row0[h] + 1:row0[h] + 2, :].bitcast(F32),
                                         onerow[:, 0:S].bitcast(F32)).then_inc(set_rows, 16)
                sp.wait_ge(set_rows, 12 * 16)
                sp.dma_start(W[1][:, :, :, :, :].bitcast(F32), wsp[1]).then_inc(w_in[1], 16)
                sp.dma_start(Wo[:, :, :], io["wo1"]).then_inc(wo_in, 16)

                def emit(st):
                    j, gp, by2 = pair(st)
                    first = isinstance(st.g, int) and st.g == -1
                    for what, _ in order(st):
                        if what == "Q":
                            if first or st.off == 0:
                                bb = 0
                            elif st.batch_half == 1 and st.off >= 3:
                                bb = st.b + 1
                            else:
                                bb = st.b
                            sp.wait_ge(q_hi, 2 * gp + 1)
                            for h in range(2):
                                sp.dma_start(K2[j][h][row0[h] + 1:row0[h] + 2, :].bitcast(F32),
                                             mb[bass.ds(bb, 1), :]).then_inc(mask_in[j], 16)
                        if what == "K1":
                            if not first and not st.parity and st.off:
                                k = 1 if st.off == 2 else 0
                                nq = (2 * st.batch_half + (3 if st.off == 2 else 4)) % NQUAD
                                sp.wait_ge(misc_done, use(st, what))
                                if not (isinstance(st.g, int) and st.g >= NSTEP - 4):
                                    sp.dma_start(W[k][:, :, :, :, :].bitcast(F32), wsp[nq]).then_inc(w_in[k], 16)
                                if st.batch_half == 1 and st.off == 2 and not isinstance(st.b, int):
                                    sp.dma_start(kv[:, :, :, :].bitcast(F32), kv_d[bass.ds(st.b + 1, 1)].rearrange(
                                        "b p a c n -> (b p) a c n")).then_inc(kv_in, 16)
                            if not first and st.off == 0:
                                sp.wait_ge(misc_done, use(st, what))
                                sp.dma_start(W[0][:, :, :, :, :].bitcast(F32), wsp[2]).then_inc(w_in[0], 16)
                for_steps(sp, emit, unroll_halves=True)

            @block.tensor
            def _(pe):
                pe.wait_ge(set_up, 14)

                def emit(st):
                    first = isinstance(st.g, int) and st.g == -1
                    j, gp, by2 = pair(st)
                    T = None if first else NKT * st.g
                    q = st.parity

                    def bank(name):
                        n = use(st, name)
                        if not (isinstance(n, int) and n == 1):
                            pe.wait_ge(misc_read, n - 1)

                    if first or st.off == 0:
                        wk = 0
                    else:
                        wk = {1: 1, 2: 1, 3: 0, 4: 0}[st.off]

                    def project(w, i):
                        for c in range(DC):
                            for n, (wp, xp) in enumerate(PASSES):
                                last = pe.matmul(pm[:, :], W[wk][:, wp, w, c, j * P:(j + 1) * P],
                                                 kv[:, xp, c, i * S:(i + 1) * S], start=(c == 0 and n == 0),
                                                 stop=(c == DC - 1 and n == len(PASSES) - 1))
                        last.then_inc(misc_done, 1)

                    def outputs(par, s, tt, vb):
                        pe.wait_ge(exp_done, tt + 1 + 2)
                        for h in range(2):
                            last = pe.matmul(pO[own[h], :], V[vb][:, s, par * P + h * HD1:par * P + (h + 1) * HD1],
                                             pr[:, s % PT, h, :], start=(s == 0), stop=(s == NKT - 1),
                                             skip_group_check=True)
                        last.then_inc(pv_done, 1)

                    if not first:
                        vb_now = {0: 0, 1: 0, 2: 1, 3: 1, 4: 0}[st.off]
                    for what, n in order(st):
                        if what in ("K0", "K1"):
                            bank(what)
                            project(0, int(what[1]))
                        elif what == "Q":
                            bank(what)
                            if first:
                                pe.wait_ge(kv_in, 16)
                                pe.wait_ge(w_in[0], 16)
                            elif st.off in (1, 3):
                                pe.wait_ge(w_in[wk], 16 * (2 * st.b + st.batch_half) + (16 if st.off == 1 else 32))
                                if st.off == 3:
                                    pe.wait_ge(kv_in, 16 * (st.b + st.batch_half + 1))
                            project(2, 1)
                        elif what[0] == "V":
                            i = int(what[1])
                            bank(what)
                            for t in range(2):
                                kt = 2 * i + t
                                for c in range(DC):
                                    for m, (xp, wp) in enumerate(PASSES):
                                        last = pe.matmul(pm[:, t * 256:(t + 1) * 256],
                                                         kv[:, xp, c, kt * P:(kt + 1) * P], W[wk][:, wp, 1, c, :],
                                                         start=(c == 0 and m == 0),
                                                         stop=(c == DC - 1 and m == len(PASSES) - 1))
                            last.then_inc(misc_done, 1)
                        elif what == "S":
                            m, h, qt = n // 8, n // TPB % 2, n % TPB
                            if n == 0 and first:
                                pe.wait_ge(set_rows, 12 * 16)
                            if n == 0:
                                pe.wait_ge(copied, NCOPY * gp + 6)
                                pe.wait_ge(mask_in[j], 32 * by2 + 32)
                                if not first:
                                    pe.wait_ge(m_copied, 2 * gp)
                            if n == 8:
                                pe.wait_ge(copied, NCOPY * gp + NCOPY)
                            if n > 1:
                                pe.wait_ge(max_done, 17 * gp + n - 1)
                            pe.matmul(pS[:, n % 2, :], Q0[j][h][:, qt * P:(qt + 1) * P],
                                      K2[j][h][:, m * S:(m + 1) * S], start=True, stop=True).then_inc(s_done, 1)
                        elif what == "M":
                            if isinstance(st.g, int) and st.g == 0:
                                pe.wait_ge(wo_in, 16)
                            pe.wait_ge(max_done, 17 * st.g + 17)
                            for h in range(2):
                                for qt in range(TPB):
                                    last = pe.matmul(pS[row0[h]:row0[h] + 1, 0, qt * P:(qt + 1) * P],
                                                     nm[:, q, h * TPB + qt:h * TPB + qt + 1], ident[:, :],
                                                     start=True, stop=True)
                            last.then_inc(m_done, 1)
                        elif what == "ST":
                            s = n
                            if s == 0:
                                pe.wait_ge(m_copied, 2 * st.g + 2)
                                prev = Step(-1, 1, None) if isinstance(st.g, int) and st.g == 0 else (
                                    Step(0, 0, 0) if isinstance(st.g, int) and st.g == 1 else
                                    Step(st.g - 1, 1 - st.parity, None))
                                pe.wait_ge(misc_read, use(prev, "K1"))
                            pe.wait_ge(exp_done, T + s + 1)
                            for h in range(2):
                                pe.matmul(pT[s % 2][:, h, :], K1[q][h][:, s * P:(s + 1) * P], Q1[q][h][:, :],
                                          start=True, stop=False)
                                last = pe.matmul(pT[s % 2][:, h, :], K2[q][h][:, s * P:(s + 1) * P], Q2[q][h][:, :],
                                                 start=False, stop=True)
                            last.then_inc(st_done, 1)
                        elif what == "PV":
                            if n == 0:
                                pe.wait_ge(o_copied, st.g + 1)
                            outputs(q, n, T + n, vb_now)
                        elif what == "den":
                            bank(what)
                            pe.wait_ge(acc_done, 7 * st.g + 7)
                            for h in range(2):
                                last = pe.matmul(pm[own[h], :], ones[:, :], acc[:, 1 - q, h, :],
                                                 start=True, stop=True, skip_group_check=True)
                            last.then_inc(misc_done, 1)
                        elif what[0] == "Y":
                            i = int(what[1])
                            bank(what)
                            pe.wait_ge(ot_done, st.g + 2)
                            wo = Wo[:, bass.ds(4 * st.batch_half + st.off - 1, 1), :].rearrange("p a d -> p (a d)")
                            for t in range(2):
                                tt = 2 * i + t
                                last = pe.matmul(pm[:, t * D:(t + 1) * D], OT[:, 1 - q, tt * P:(tt + 1) * P], wo,
                                                 start=True, stop=True)
                            last.then_inc(misc_done, 1)
                for_steps(pe, emit)

            @block.scalar
            def _(act):
                for k in range(2):
                    act.copy(ahead[:, k:k + 1], ident[:, 0:1]).then_inc(exp_done, 1)
                act.copy(ahead[:, 2:3], ident[:, 0:1]).then_inc(o_copied, 1)

                def emit(st):
                    first = isinstance(st.g, int) and st.g == -1
                    j, gp, by2 = pair(st)
                    q = st.parity
                    for what, n in order(st):
                        if what in ("K0", "K1"):
                            i = int(what[1])
                            act.wait_ge(misc_done, use(st, what))
                            for h in range(2):
                                act.copy(K1[j][h][own[h], i * S:(i + 1) * S], pm[own[h], :]).then_inc(k_hi, 1)
                        elif what == "c" and n < 2:
                            half = slice(n * S, (n + 1) * S)
                            for h in range(2):
                                act.wait_ge(k_hi, 4 * gp + 2 * n + h + 1)
                                act.copy(K2[j][h][own[h], half], K1[j][h][own[h], half].bitcast(F32)
                                         ).then_inc(copied, 1)
                        elif what == "Q":
                            act.wait_ge(misc_done, use(st, what))
                            if not (isinstance(st.g, int) and st.g <= 0):
                                act.wait_ge(st_done, NKT * st.g)
                            for h in range(2):
                                act.mul(Q1[j][h][own[h], :], pm[own[h], :], SCALE1).then_inc(q_hi, 1)
                        elif what == "c":
                            for q_, rows in ((Q0, own), (Q1, other)):
                                for h in range(2):
                                    act.wait_ge(q_hi, 2 * gp + h + 1)
                                    act.copy(q_[j][h][rows[h], :], Q1[j][h][own[h], :].bitcast(F32)).then_inc(copied, 1)
                        elif what[0] == "V":
                            i = int(what[1])
                            vb = 0 if first else {1: 1, 3: 0}[st.off]
                            act.wait_ge(misc_done, use(st, what))
                            if not first:
                                act.wait_ge(pv_done, NKT * st.g + PT)
                            act.copy(V[vb][:, 2 * i:2 * i + 2, :].rearrange("p a n -> p (a n)"), pm[:, :]
                                     ).then_inc(misc_read, 1)
                        elif what == "M":
                            act.wait_ge(m_done, st.g + 1)
                            act.copy(Q2[q][0][row0[0]:row0[0] + 1, :], pS[row0[0]:row0[0] + 1, 0, :]
                                     ).then_inc(m_copied, 1)
                        elif what == "den":
                            act.wait_ge(misc_done, use(st, what))
                            act.wait_ge(ot_done, st.g + 1)
                            act.copy(rb[:, :], pm[:, :]).then_inc(misc_read, 1)
                        elif what == "ST":
                            T = NKT * st.g + n
                            act.wait_ge(st_done, T + 1)
                            act.wait_ge(pv_done, T + 1)
                            act.wait_ge(acc_done, 7 * st.g + 7 + (n - 3 if n < 4 else max(n - 4, 1)))
                            act.activation(pr[:, n % PT, :, :], pT[n % 2][:, :, :], ACT.Exp).then_inc(exp_done, 1)
                        elif what == "O":
                            act.wait_ge(pv_done, NKT * st.g + NKT + PT)
                            act.wait_ge(ot_done, st.g + 1)
                            act.copy(osb[:, q, :], pO[:, :]).then_inc(o_copied, 1)
                for_steps(act, emit)

            @block.vector
            def _(dve):
                for k in range(2):
                    dve.memset(ahead[:, 3 + k:4 + k], 0.0).then_inc(ot_done, 1)

                def emit(st):
                    j, gp, by2 = pair(st)
                    q = st.parity
                    for what, n in order(st):
                        if what in ("K0", "K1"):
                            i = int(what[1])
                            for h in range(2):
                                dve.wait_ge(k_hi, 4 * gp + 2 * i + h + 1)
                                ins = dve.tensor_tensor(K1[j][h][other[h], i * S:(i + 1) * S], pm[own[h], :],
                                                        K1[j][h][own[h], i * S:(i + 1) * S].bitcast(F32),
                                                        ALU.subtract)
                            ins.then_inc(misc_read, 1)
                        elif what == "Q":
                            for h in range(2):
                                dve.wait_ge(q_hi, 2 * gp + h + 1)
                                ins = dve.scalar_tensor_tensor(Q2[j][h][own[h], :], pm[own[h], :], SCALE1,
                                                               Q1[j][h][own[h], :].bitcast(F32), ALU.mult,
                                                               ALU.subtract)
                            ins.then_inc(misc_read, 1)
                        elif what == "S":
                            dve.wait_ge(s_done, 16 * gp + n + 1)
                            dve.tensor_reduce(nm2[:, j, n % 8, n // 8:n // 8 + 1], pS[:, n % 2, :], AX.X,
                                              ALU.max, negate=True).then_inc(max_done, 1)
                        elif what == "N":
                            dve.wait_ge(max_done, 17 * gp + 16)
                            dve.tensor_tensor(nm[:, j, :], nm2[:, j, :, 0], nm2[:, j, :, 1], ALU.min
                                              ).then_inc(max_done, 1)
                        elif what == "M":
                            dve.wait_ge(m_done, st.g + 1)
                            dve.tensor_copy(Q2[q][1][row0[1]:row0[1] + 1, :], pS[row0[1]:row0[1] + 1, 0, :]
                                            ).then_inc(m_copied, 1)
                        elif what == "r":
                            if n == 0:
                                dve.wait_ge(misc_read, use(st, "den"))
                            quarter = slice(n * P, (n + 1) * P)
                            dve.reciprocal(rb[:, quarter], rb[:, quarter]).then_inc(r_done, 1)
                            if n == TPB - 1:
                                dve.wait_ge(r_done, TPB * st.g)
                                dve.wait_ge(o_copied, st.g + 1)
                                dve.tensor_tensor(OT[:, 1 - q, :], osb[:, 1 - q, :], rb[:, :], ALU.mult
                                                  ).then_inc(ot_done, 1)
                        elif what[0] == "Y":
                            i = int(what[1])
                            dve.wait_ge(misc_done, use(st, what))
                            r = res[:, bass.ds(TPB * st.b + 2 * i, 2), :]
                            dve.tensor_tensor(r, r, pm[:, :].rearrange("p (t d) -> p t d", d=D), ALU.add
                                              ).then_inc(misc_read, 1)
                for_steps(dve, emit)

            @block.gpsimd
            def _(pool):
                for j in range(2):
                    for h in range(2):
                        for b_ in (K2, Q0, Q2):
                            pool.memset(b_[j][h][:, :].bitcast(F32), 0.0).then_inc(set_up, 1)
                pool.memset(onerow[:, :].bitcast(F32), 1.0).then_inc(set_up, 1)
                pool.memset(ones[:, :], 1.0).then_inc(set_up, 1)
                pool.memset(ahead[:, 6:7], 0.0).then_inc(pv_done, PT)
                pool.memset(ahead[:, 7:8], 0.0).then_inc(acc_done, 7)

                def emit(st):
                    if isinstance(st.g, int) and st.g in (-1, NSTEP):
                        return
                    q = st.parity
                    for s in range(1, NKT):
                        T = NKT * st.g + s
                        pool.wait_ge(exp_done, T + 1 + 2)
                        if s == 1:
                            if not (isinstance(st.g, int) and st.g < 2):
                                prev = Step(st.g - 1, 1 - q, None)
                                pool.wait_ge(misc_done, use(prev, "den"))
                            a = pr[:, 0, :, :]
                        else:
                            pool.wait_ge(acc_done, 7 * st.g + s - 1 + 7)
                            a = acc[:, q, :, :]
                        pool.tensor_tensor(acc[:, q, :, :], a, pr[:, s % PT, :, :], ALU.add).then_inc(acc_done, 1)
                for_steps(pool, emit)


def layer1_attention(nc, io, res, ident):
    kv = nc.dram_tensor("kv_split", (B, P, 2, DC, KEYS), F32, kind="Internal").ap()
    wsp = nc.dram_tensor("w_split", (NQUAD, P, 2, 3, DC, 256), F32, kind="Internal").ap()
    mb = nc.dram_tensor("mask_bias", (B, KEYS), F32, kind="Internal").ap()
    layer1_keys_in(nc, io, res, ident, kv, wsp, mb)
    layer1_pairs(nc, io, res, ident, kv, wsp, mb)


PHASES = [layer0_attention, layer0_ffn, layer1_attention, layer1_ffn]


def network(nc, io, out):
    with ExitStack() as ctx:
        sb, ps, sem = scope(nc, ctx)
        res = sb("res", [P, NT, D])
        ident = sb("ident", [P, P])
        id_ready = sem("id_ready")
        with nc.Block() as block:
            @block.gpsimd
            def _(pool):
                pool.memset(ident[:, :], 0.0).then_inc(id_ready, 1)
                pool.wait_ge(id_ready, 1)
                pool.affine_select(out=ident[:, :], in_=ident[:, :], compare_op=ALU.not_equal, fill=1.0, base=0,
                                   pattern=[[-1, P]], channel_multiplier=1).then_inc(id_ready, 1)
        io["out"] = out
        for phase in PHASES:
            phase(nc, io, res, ident)


def _rows(a):
    return a.reshape(-1, P, a.shape[-1]).transpose(1, 0, 2)


def _gate_up(np, parts):
    out = []
    for ws in parts:
        w = np.concatenate(ws).transpose(0, 2, 1)
        out.append(w.reshape(w.shape[0], DC, P, -1).transpose(0, 2, 1, 3).reshape(w.shape[0], P, -1))
    return np.concatenate(out, axis=2)


def _widths(w):
    return w.reshape(D, NS1, F1).transpose(1, 2, 0)


def laid_out(np, a):
    z = {"x": a["x"], "ctx": a["ctx_1024"]}
    for n in "qkvo":
        z[f"w{n}0"] = _rows(a[f"L0_xattn_W{n}"].T)
    for n in "qkv":
        z[f"b{n}0"] = a[f"L0_xattn_b{n}"].reshape(DC, P).T
    z["bo0"] = a["L0_xattn_bo"]
    z["ebias"] = a["L0_ffn_e_bias"]
    z["m0_gate"] = _rows(a["L0_ffn_gate_w"].T)
    z["e0_gu"] = _gate_up(np, [[a["L0_ffn_gate_proj"], a["L0_ffn_shared_gate_w"][None]],
                               [a["L0_ffn_up_proj"], a["L0_ffn_shared_up_w"][None]]])
    z["e0_d"] = np.concatenate([a["L0_ffn_down_proj"], a["L0_ffn_shared_down_w"][None]]).transpose(0, 2, 1)
    for n in "kvq":
        z[f"w{n}1"] = _rows(a[f"L1_xattn_W{n}"])
    z["wo1"] = _rows(a["L1_xattn_Wo"])
    z["gb1"] = np.stack([np.stack([a[f"L1_xattn_{p}{m}"].reshape(DC, P) for p in "gb"]) for m in "ml"]
                        ).transpose(3, 0, 1, 2)
    z["mask"] = a["mask_BxS2_bf1"].view(np.uint8)
    z["m1_gate"] = _rows(a["L1_ffn_gate_w"].T)
    z["r1_gu"] = np.stack([a["L1_ffn_w_gate"], a["L1_ffn_w_up"]], axis=1).reshape(E1, 2 * DC, P, F1
                                                                                  ).transpose(2, 0, 1, 3)
    z["r1_d"] = a["L1_ffn_w_down"]
    z["e1_gu"] = _gate_up(np, [[_widths(a["L1_ffn_sw_gate"])], [_widths(a["L1_ffn_sw_up"])]])
    z["e1_d"] = a["L1_ffn_sw_down"].reshape(NS1, F1, D)
    return {k: np.ascontiguousarray(v) for k, v in z.items()}


def kernel(**inputs):
    import numpy as _np
    import concourse.bacc as _bacc
    from concourse import mybir as _mybir
    from concourse.bass_utils import run_bass_kernel_spmd as _run

    nc = _bacc.Bacc("TRN2", target_bir_lowering=False, num_devices=1)
    arrays, io = {}, {}
    for name, a in laid_out(_np, {k: _np.asarray(v) for k, v in inputs.items()}).items():
        arrays[f"in_{name}_dram"] = a
        io[name] = nc.dram_tensor(f"in_{name}_dram", a.shape, _mybir.dt.from_np(a.dtype), kind="ExternalInput").ap()
    out = nc.dram_tensor("out_0_dram", (B, S, D), F32, kind="ExternalOutput").ap()
    network(nc, io, out)
    r = _run(nc, [arrays], core_ids=[0])
    return r.results[0]["out_0_dram"]
```
